# Optimizing a Trainium2 kernel written in Bass

```python
import numpy as np
import jax
import jax.numpy as jnp

def _softmax(x, axis=-1):
    return jax.nn.softmax(x, axis=axis)

def _gelu(x):
    return jax.nn.gelu(x, approximate=True)

def _silu(x):
    return jax.nn.silu(x)

def _sigmoid(x):
    return jax.nn.sigmoid(x)

def _layernorm(x, axis=-1, eps=1e-05):
    m = jnp.mean(x, axis=axis, keepdims=True)
    v = jnp.var(x, axis=axis, keepdims=True)
    return (x - m) / jnp.sqrt(v + eps)

def _scatter_add(tgt, idx, src, axis=0):
    return tgt.at[idx].add(src)

def _segment_sum(src, seg, n):
    return jax.ops.segment_sum(src, seg, n)
kernel_name = 'mk_gnn_resnorm_d4_gnn_r32_ee6f84'

def setup_inputs(seed: int=0):
    np.random.seed(seed)
    _w = jnp.asarray

    def _rec_inputs():
        import jax
        import jax.numpy as jnp
        _gk = jax.random.key(seed)
        x = -0.0002928 + 1 * jax.random.normal(jax.random.fold_in(_gk, 1), (2048, 64), jnp.float32)
        src = jax.random.randint(jax.random.fold_in(_gk, 2), (65536,), 0, 2048, jnp.int32)
        dst = jnp.minimum((2048 * jax.random.uniform(jax.random.fold_in(_gk, 3), (65536,)) ** 2.0).astype(jnp.int32), 65535)
        _o = jnp.argsort(dst, stable=True)
        src = src[_o]
        dst = dst[_o]
        edge_attr_16 = 0.000196303 + 1.00016 * jax.random.normal(jax.random.fold_in(_gk, 12), (65536, 16), jnp.float32)
        return (x, src, dst, edge_attr_16)
    x, src, dst, edge_attr_16 = _rec_inputs()

    def _L0_gnn_setup():
        import jax, jax.numpy as jnp
        import numpy as np
        N = 2048
        C = 64
        H = 4
        D = 16
        KVOL = 125
        P = 32768

        def _l2norm(t):
            n = jnp.linalg.norm(t, axis=-1, keepdims=True)
            return t / jnp.maximum(n, 1e-12)
        key = jax.random.key(seed)
        ks = jax.random.split(key, 10)
        s = 1.0 / np.sqrt(C)
        x = jax.random.normal(ks[0], (N, C), dtype=jnp.float32)
        Wq = jax.random.normal(ks[1], (C, C), dtype=jnp.float32) * s
        Wk = jax.random.normal(ks[2], (C, C), dtype=jnp.float32) * s
        Wv = jax.random.normal(ks[3], (C, C), dtype=jnp.float32) * s
        Wo = jax.random.normal(ks[4], (C, C), dtype=jnp.float32) * s
        bq = jnp.zeros((C,), jnp.float32)
        bk = jnp.zeros((C,), jnp.float32)
        bv = jnp.zeros((C,), jnp.float32)
        bo = jnp.zeros((C,), jnp.float32)
        pos_enc = jax.random.normal(ks[5], (KVOL, H, D), dtype=jnp.float32)
        in_idx = jax.random.randint(ks[6], (P,), 0, N)
        kern_idx = jax.random.randint(ks[7], (P,), 0, KVOL)
        out_idx = jax.random.randint(ks[8], (P,), 0, N)
        kq_map = jnp.stack([in_idx * KVOL + kern_idx, out_idx]).astype(jnp.int32)
        return dict(x=x, Wq=Wq, bq=bq, Wk=Wk, bk=bk, Wv=Wv, bv=bv, Wo=Wo, bo=bo, pos_enc=pos_enc, kq_map=kq_map)
    _L0_gnn_all = _L0_gnn_setup()
    _L0_gnn_in = {k: v for k, v in _L0_gnn_all.items() if k in ('Wq', 'bq', 'Wk', 'bk', 'Wv', 'bv', 'Wo', 'bo', 'pos_enc')}
    del _L0_gnn_all

    def _L1_gnn_setup():
        import jax, jax.numpy as jnp
        import numpy as np
        LEAKY_SLOPE = 0.2
        LN_EPS = 1e-05
        SOFTMAX_EPS = 1e-16
        key = jax.random.key(seed)
        ks = jax.random.split(key, 8)
        N, E, F, H, C, ED = (3125, 50000, 64, 8, 8, 16)
        s = 1.0 / np.sqrt(F)
        return {'x': jax.random.normal(ks[0], (N, F), jnp.float32), 'edge_index': jax.random.randint(ks[1], (2, E), 0, N, jnp.int32), 'edge_attr': jax.random.normal(ks[2], (E, ED), jnp.float32), 'W_l': jax.random.normal(ks[3], (H * C, F), jnp.float32) * s, 'b_l': jnp.zeros((H * C,), jnp.float32), 'W_r': jax.random.normal(ks[4], (H * C, F), jnp.float32) * s, 'b_r': jnp.zeros((H * C,), jnp.float32), 'W_e': jax.random.normal(ks[5], (H * C, ED), jnp.float32) * (1.0 / np.sqrt(ED)), 'att': jax.random.normal(ks[6], (1, H, C), jnp.float32) * (1.0 / np.sqrt(C)), 'bias': jnp.zeros((H * C,), jnp.float32), 'gamma': jnp.ones((F,), jnp.float32), 'beta': jnp.zeros((F,), jnp.float32)}
    _L1_gnn_all = _L1_gnn_setup()
    _L1_gnn_in = {k: v for k, v in _L1_gnn_all.items() if k in ('W_l', 'b_l', 'W_r', 'b_r', 'W_e', 'att', 'bias', 'gamma', 'beta')}
    del _L1_gnn_all

    def _L2_gnn_setup():
        import jax, jax.numpy as jnp
        import numpy as np
        N_NODES = 50000
        N_EDGES = 25000
        D_FEAT = 64
        D_HID = 128
        key = jax.random.key(seed)
        k_hid, k_w1, k_w2, k_src, k_dst = jax.random.split(key, 5)
        hid = jax.random.normal(k_hid, (N_NODES, D_FEAT), dtype=jnp.float32)
        W1 = jax.random.normal(k_w1, (2 * D_FEAT, D_HID), dtype=jnp.float32) * (1.0 / np.sqrt(2 * D_FEAT))
        b1 = jnp.zeros((D_HID,), dtype=jnp.float32)
        W2 = jax.random.normal(k_w2, (D_HID, D_FEAT), dtype=jnp.float32) * (1.0 / np.sqrt(D_HID))
        b2 = jnp.zeros((D_FEAT,), dtype=jnp.float32)
        src_idx = jax.random.randint(k_src, (N_EDGES,), 0, N_NODES, dtype=jnp.int64 if jax.config.jax_enable_x64 else jnp.int32)
        dst_idx = jax.random.randint(k_dst, (N_EDGES,), 0, N_NODES, dtype=jnp.int64 if jax.config.jax_enable_x64 else jnp.int32)
        return {'hid': hid, 'W1': W1, 'b1': b1, 'W2': W2, 'b2': b2, 'src_idx': src_idx, 'dst_idx': dst_idx}
    _L2_gnn_all = _L2_gnn_setup()
    _L2_gnn_in = {k: v for k, v in _L2_gnn_all.items() if k in ('W1', 'b1', 'W2', 'b2')}
    del _L2_gnn_all

    def _L3_gnn_setup():
        import jax, jax.numpy as jnp
        import numpy as np
        N_NODES = 3125
        N_EDGES = 1250000
        D_IN = 64
        D_OUT = 64
        key = jax.random.key(seed)
        k1, k2, k3, k4, k5 = jax.random.split(key, 5)
        x = jax.random.normal(k1, (N_NODES, D_IN), dtype=jnp.float32)
        edge_index = jax.random.randint(k2, (2, N_EDGES), 0, N_NODES, dtype=jnp.int64)
        w_neigh = jax.random.normal(k3, (D_OUT, D_IN), dtype=jnp.float32) / np.sqrt(D_IN)
        w_self = jax.random.normal(k4, (D_OUT, D_IN), dtype=jnp.float32) / np.sqrt(D_IN)
        b_self = jax.random.normal(k5, (D_OUT,), dtype=jnp.float32) * 0.01
        return {'x': x, 'edge_index': edge_index, 'w_neigh': w_neigh, 'w_self': w_self, 'b_self': b_self}
    _L3_gnn_all = _L3_gnn_setup()
    _L3_gnn_in = {k: v for k, v in _L3_gnn_all.items() if k in ('w_neigh', 'w_self', 'b_self')}
    del _L3_gnn_all
    return {'x': x, 'src': src, 'dst': dst, 'edge_attr_16': edge_attr_16, 'L0_gnn_Wq': _L0_gnn_in['Wq'], 'L0_gnn_bq': _L0_gnn_in['bq'], 'L0_gnn_Wk': _L0_gnn_in['Wk'], 'L0_gnn_bk': _L0_gnn_in['bk'], 'L0_gnn_Wv': _L0_gnn_in['Wv'], 'L0_gnn_bv': _L0_gnn_in['bv'], 'L0_gnn_Wo': _L0_gnn_in['Wo'], 'L0_gnn_bo': _L0_gnn_in['bo'], 'L0_gnn_pos_enc': _L0_gnn_in['pos_enc'], 'L1_gnn_W_l': _L1_gnn_in['W_l'], 'L1_gnn_b_l': _L1_gnn_in['b_l'], 'L1_gnn_W_r': _L1_gnn_in['W_r'], 'L1_gnn_b_r': _L1_gnn_in['b_r'], 'L1_gnn_W_e': _L1_gnn_in['W_e'], 'L1_gnn_att': _L1_gnn_in['att'], 'L1_gnn_bias': _L1_gnn_in['bias'], 'L1_gnn_gamma': _L1_gnn_in['gamma'], 'L1_gnn_beta': _L1_gnn_in['beta'], 'L2_gnn_W1': _L2_gnn_in['W1'], 'L2_gnn_b1': _L2_gnn_in['b1'], 'L2_gnn_W2': _L2_gnn_in['W2'], 'L2_gnn_b2': _L2_gnn_in['b2'], 'L3_gnn_w_neigh': _L3_gnn_in['w_neigh'], 'L3_gnn_w_self': _L3_gnn_in['w_self'], 'L3_gnn_b_self': _L3_gnn_in['b_self']}

def reference(x, src, dst, edge_attr_16, L0_gnn_Wq, L0_gnn_bq, L0_gnn_Wk, L0_gnn_bk, L0_gnn_Wv, L0_gnn_bv, L0_gnn_Wo, L0_gnn_bo, L0_gnn_pos_enc, L1_gnn_W_l, L1_gnn_b_l, L1_gnn_W_r, L1_gnn_b_r, L1_gnn_W_e, L1_gnn_att, L1_gnn_bias, L1_gnn_gamma, L1_gnn_beta, L2_gnn_W1, L2_gnn_b1, L2_gnn_W2, L2_gnn_b2, L3_gnn_w_neigh, L3_gnn_w_self, L3_gnn_b_self):
    import jax
    import jax.numpy as jnp

    def _L0_gnn_ref(x, Wq, bq, Wk, bk, Wv, bv, Wo, bo, pos_enc, kq_map):
        import jax, jax.numpy as jnp
        import numpy as np
        N = 2048
        C = 64
        H = 4
        D = 16
        KVOL = 125
        P = 32768

        def _l2norm(t):
            n = jnp.linalg.norm(t, axis=-1, keepdims=True)
            return t / jnp.maximum(n, 1e-12)
        q = (x @ Wq + bq).reshape(N, H, D)
        k = (x @ Wk + bk).reshape(N, H, D)
        v = (x @ Wv + bv).reshape(N, H, D)
        nq = _l2norm(q)
        nk = _l2norm(k)
        npos = _l2norm(pos_enc)
        in_idx = kq_map[0] // KVOL
        kidx = kq_map[0] % KVOL
        out_idx = kq_map[1]
        attn = jnp.einsum('phd,phd->ph', nq[out_idx], nk[in_idx] + npos[kidx])
        msg = attn[:, :, None] * v[in_idx]
        out = jax.ops.segment_sum(msg, out_idx, num_segments=N)
        out = out.reshape(N, C) @ Wo + bo
        return out + x

    def _L1_gnn_ref(x, edge_index, edge_attr, W_l, b_l, W_r, b_r, W_e, att, bias, gamma, beta):
        import jax, jax.numpy as jnp
        import numpy as np
        LEAKY_SLOPE = 0.2
        LN_EPS = 1e-05
        SOFTMAX_EPS = 1e-16
        N, F = x.shape
        H, C = (att.shape[1], att.shape[2])
        src, dst = (edge_index[0], edge_index[1])
        xl = (x @ W_l.T + b_l).reshape(N, H, C)
        xr = (x @ W_r.T + b_r).reshape(N, H, C)
        e = (edge_attr @ W_e.T).reshape(-1, H, C)
        m = jax.nn.leaky_relu(xl[src] + xr[dst] + e, LEAKY_SLOPE)
        logits = jnp.einsum('ehc,hc->eh', m, att[0])
        mx = jax.ops.segment_max(logits, dst, num_segments=N)
        mx = jnp.where(jnp.isfinite(mx), mx, 0.0)
        ex = jnp.exp(logits - mx[dst])
        denom = jax.ops.segment_sum(ex, dst, num_segments=N)
        alpha = ex / (denom[dst] + SOFTMAX_EPS)
        agg = jax.ops.segment_sum(alpha[:, :, None] * xl[src], dst, num_segments=N)
        out = agg.reshape(N, H * C) + bias
        h = out + x
        mu = jnp.mean(h, axis=-1, keepdims=True)
        var = jnp.mean((h - mu) ** 2, axis=-1, keepdims=True)
        hn = (h - mu) * jax.lax.rsqrt(var + LN_EPS) * gamma + beta
        return jax.nn.relu(hn)

    def _L2_gnn_ref(hid, W1, b1, W2, b2, src_idx, dst_idx):
        import jax, jax.numpy as jnp
        import numpy as np
        N_NODES = 50000
        N_EDGES = 25000
        D_FEAT = 64
        D_HID = 128
        n_nodes = hid.shape[0]
        e = jnp.concatenate([hid[src_idx], hid[dst_idx]], axis=1)
        m = jax.nn.relu(e @ W1 + b1) @ W2 + b2
        s = jax.ops.segment_sum(m, dst_idx, num_segments=n_nodes)
        cnt = jax.ops.segment_sum(jnp.ones((m.shape[0],), dtype=m.dtype), dst_idx, num_segments=n_nodes)
        return s / jnp.maximum(cnt, 1.0)[:, None]

    def _L3_gnn_ref(x, edge_index, w_neigh, w_self, b_self):
        import jax, jax.numpy as jnp
        import numpy as np
        N_NODES = 3125
        N_EDGES = 1250000
        D_IN = 64
        D_OUT = 64
        num_nodes = x.shape[0]
        src, dst = (edge_index[0], edge_index[1])
        agg = jax.ops.segment_sum(x[src], dst, num_segments=num_nodes)
        degree = jax.ops.segment_sum(jnp.ones_like(dst, dtype=x.dtype), dst, num_segments=num_nodes)
        degree = jnp.maximum(degree, 1.0)
        agg = agg / degree[:, None]
        return agg @ w_neigh.T + x @ w_self.T + b_self
    edge_index = jnp.stack([src, dst])
    x = _layernorm(x + _L0_gnn_ref(x, L0_gnn_Wq, L0_gnn_bq, L0_gnn_Wk, L0_gnn_bk, L0_gnn_Wv, L0_gnn_bv, L0_gnn_Wo, L0_gnn_bo, L0_gnn_pos_enc, edge_index), axis=-1)
    x = _layernorm(x + _L1_gnn_ref(x, edge_index, edge_attr_16, L1_gnn_W_l, L1_gnn_b_l, L1_gnn_W_r, L1_gnn_b_r, L1_gnn_W_e, L1_gnn_att, L1_gnn_bias, L1_gnn_gamma, L1_gnn_beta), axis=-1)
    x = _layernorm(x + _L2_gnn_ref(x, L2_gnn_W1, L2_gnn_b1, L2_gnn_W2, L2_gnn_b2, src, dst), axis=-1)
    x = _layernorm(x + _L3_gnn_ref(x, edge_index, L3_gnn_w_neigh, L3_gnn_w_self, L3_gnn_b_self), axis=-1)
    return x

_drawn_inputs = setup_inputs


def setup_inputs(seed=0):
    import zlib

    import numpy as np

    out = dict(_drawn_inputs(seed))
    spreads = {'L0_gnn_bq': (0.0, 0.1),
     'L0_gnn_bk': (0.0, 0.1),
     'L0_gnn_bv': (0.0, 0.1),
     'L0_gnn_bo': (0.0, 0.1),
     'L1_gnn_b_l': (0.0, 0.1),
     'L1_gnn_b_r': (0.0, 0.8),
     'L1_gnn_bias': (0.0, 0.1),
     'L1_gnn_gamma': (1.0, 0.2),
     'L1_gnn_beta': (0.0, 0.1),
     'L2_gnn_b1': (0.0, 0.1),
     'L2_gnn_b2': (0.0, 0.1)}
    factors = {'L3_gnn_b_self': 8.0}
    for name, (base, spread) in spreads.items():
        noise = np.random.default_rng([zlib.crc32(name.encode()), seed]).standard_normal(out[name].shape)
        drawn = base * np.exp(spread * noise) if base else spread * noise
        out[name] = jnp.asarray(drawn.astype(out[name].dtype))
    for name, factor in factors.items():
        out[name] = (out[name] * factor).astype(out[name].dtype)
    return out
```

```python
import concourse.bass as bass
from concourse import mybir
from contextlib import ExitStack

F32 = mybir.dt.float32
BF16 = mybir.dt.bfloat16
I32 = mybir.dt.int32
ALU = mybir.AluOpType
ACT = mybir.ActivationFunctionType
AX = mybir.AxisListType

N = 2048
E = 65536
C = 64
P = 128
NB = N // P
G = 4
EC = G * P
NCH = E // EC
NQ = NCH + NB
NT = NQ + 2
KVOL = 125
NI = -(-N // KVOL)
H0, D0 = 4, 16
H1, D1 = 8, 8
ED = 16
HID = 128
NG = P // H1
KG = NQ * G // NG
TL = KG * P
NW = 26
BIG = 1e30
SLOTS = 2


def build(nc, io, out):
    ctx = ExitStack()
    with ctx:
        def sb(name, shape, dt=F32):
            return ctx.enter_context(nc.sbuf_tensor(name, shape, dt))

        sems = {}

        def S(name):
            if name not in sems:
                sems[name] = ctx.enter_context(nc.semaphore(name))
            return sems[name]

        kpv_dram = nc.dram_tensor("kpv_table", (N, 2 * C), F32, kind="Internal").ap()
        xl_dram = nc.dram_tensor("xl_table", (N, C), F32, kind="Internal").ap()
        a_dram = nc.dram_tensor("a_table", (N, HID), F32, kind="Internal").ap()
        x3_dram = nc.dram_tensor("x3_table", (N, C), F32, kind="Internal").ap()
        spill_dram = nc.dram_tensor("xl_rows", (P, NQ, G * C), F32, kind="Internal").ap()

        ident = sb("ident", [P, P])
        ones = sb("ones", [P, P])
        zeros = sb("zeros", [1, 512])
        col_i = sb("col_i", [P, NT], I32)
        col_f = sb("col_f", [P, NT])
        part_i = sb("part_i", [P, 1], I32)
        part_f = sb("part_f", [P, 1])
        notfirst = sb("notfirst", [P, 1])
        gmask = sb("gmask", [G * ED, G])
        wq = sb("wq", [C + 1, C])
        wkv = sb("wkv", [C + 1, 2 * C])
        wo = sb("wo", [C, C])
        wraw = sb("wraw", [C, 4 * C])
        weraw = sb("weraw", [C, G * ED])
        wlr = sb("wlr", [C + 1, 2 * C])
        wns = sb("wns", [C + 1, 2 * C])
        w1a = sb("w1a", [C, HID])
        w1b = sb("w1b", [C + 1, HID])
        w2 = sb("w2", [HID, C])
        web = sb("web", [G * ED, G, C])
        pos = sb("pos", [KVOL, C])
        vecs = sb("vecs", [P, 6, C])
        VBO, VATT, VBIAS, VGAMMA, VBETA, VB2 = range(6)
        x = sb("x", [P, NB, C])
        h = sb("h", [P, NB, C])
        sq = sb("sq", [P, NB * HID])
        st1 = sb("st1", [P, NB])
        st2 = sb("st2", [P, NB])
        st3 = sb("st3", [P, NB])
        nrm = sb("nrm", [P, NB * H1])
        xT = sb("xT", [C + 1, N])
        aggT = sb("aggT", [P, N])
        tab = sb("tab", [P, NB * HID])
        rows = sb("rows", [P, NI * HID])
        cnt = sb("cnt", [P, NB])
        rdeg = sb("rdeg", [P, NB])
        kvn = sb("kvn", [NI, 2 * C])
        dst_i = sb("dst_i", [P, EC], I32)
        src_i = sb("src_i", [P, EC], I32)
        tmp_i = sb("tmp_i", [P, EC], I32)
        dst_f = sb("dst_f", [P, EC])
        src_f = sb("src_f", [P, EC])
        blk = sb("blk", [P, 1], I32)
        qc = sb("qc", [P, 2])
        cqb = sb("cqb", [P, NT])
        bqb = sb("bqb", [P, NT])
        selF = sb("selF", [P, NT])
        sel = sb("sel", [P, NT], BF16)
        dhi = sb("dhi", [P, EC], BF16)
        dlo = sb("dlo", [P, EC], BF16)
        btab = sb("btab", [P, NT], I32)
        ctab = sb("ctab", [P, NT], I32)
        nb = sb("nb", [P, NT])
        srcI = sb("srcI", [P, NT * G], I32)
        dstK = sb("dstK", [P, NT * G])
        dstL = sb("dstL", [P, NT * G])
        pen = sb("pen", [P, NT * G])
        idx = [sb(f"idx{s}", [P, G], I32) for s in range(SLOTS)]
        gat = [sb(f"gat{s}", [P, G, HID]) for s in range(SLOTS)]
        g64 = [sb(f"g64{s}", [P, G * C]) for s in range(SLOTS)]
        oh = [sb(f"oh{s}", [P, G, P]) for s in range(SLOTS)]
        ohT = [sb(f"ohT{s}", [P, EC]) for s in range(SLOTS)]
        pay = [sb(f"pay{s}", [P, G, HID]) for s in range(SLOTS)]
        prod = sb("prod", [P, G * HID])
        lky = sb("lky", [P, G * C])
        wgt = sb("wgt", [P, G * C])
        attn = sb("attn", [P, G * H0])
        atr = [sb(f"atr{s}", [P, G * ED]) for s in range(SLOTS)]
        atT = [sb(f"atT{s}", [G * ED, P]) for s in range(SLOTS)]
        lg = sb("lg", [P, NQ * G * H1])
        lgT = sb("lgT", [P, TL])
        keyT = sb("keyT", [P, TL])
        brk = sb("brk", [P, TL + 1])
        run = sb("run", [P, TL])
        ends = sb("ends", [P, 4])
        crow = sb("crow", [1, 12, P])
        carry = sb("carry", [P, 2])

        ps = ctx.enter_context(nc.psum_tensor("ps", [P, 8, 512], F32))
        acc = ps[:, 0:4, :].rearrange("p a b -> p (a b)")
        top = ps[:, 4:8, :].rearrange("p a b -> p (a b)")
        bc = [ps[:, 4 + s, :] for s in range(SLOTS)]
        ga = [ps[:, 6 + s, :] for s in range(SLOTS)]

        def split(ap, width):
            return ap.rearrange("p (b c) -> p b c", c=width)

        def done(eng, name, m):
            if isinstance(m, int) and m < 0:
                return
            eng.wait_ge(S(name), m + 1)

        def steps(eng, body):
            for s in range(SLOTS):
                body(s, s, 0)
            with eng.Fori(1, NQ // SLOTS) as i:
                for s in range(SLOTS):
                    body(i * SLOTS + s, s, i)

        def counted(eng):
            seen = {}

            def wait_next(name):
                seen[name] = seen.get(name, 0) + 1
                eng.wait_ge(S(name), seen[name])
            return wait_next

        block = ctx.enter_context(nc.Block())

        @block.sync
        def _(sp):
            wait_next = counted(sp)

            def load(dst, src, name):
                sp.dma_start(dst, src).then_inc(S(name), 16)

            load(dst_i[:, :], io["dst"].rearrange("(c e) -> c e", e=EC), "dst_in")
            load(src_i[:, :], io["src"].rearrange("(c e) -> c e", e=EC), "src_in")
            load(x[:, :, :], io["x"].rearrange("(b p) c -> p b c", p=P), "x_in")
            weights = [
                (wq[0:C, :], io["L0_gnn_Wq"]), (wq[C:C + 1, :], io["L0_gnn_bq"][None, :]),
                (wkv[0:C, 0:C], io["L0_gnn_Wk"]), (wkv[0:C, C:2 * C], io["L0_gnn_Wv"]),
                (wkv[C:C + 1, 0:C], io["L0_gnn_bk"][None, :]), (wkv[C:C + 1, C:2 * C], io["L0_gnn_bv"][None, :]),
                (wo[:, :], io["L0_gnn_Wo"]), (pos[:, :], io["L0_gnn_pos_enc"].rearrange("k h d -> k (h d)")),
                (wraw[:, 0:C], io["L1_gnn_W_l"]), (wraw[:, C:2 * C], io["L1_gnn_W_r"]),
                (wraw[:, 2 * C:3 * C], io["L3_gnn_w_neigh"]), (wraw[:, 3 * C:4 * C], io["L3_gnn_w_self"]),
                (split(weraw[:, :], ED), io["L1_gnn_W_e"][:, None, :].to_broadcast([C, G, ED])), (wlr[C:C + 1, 0:C], io["L1_gnn_b_l"][None, :]),
                (wlr[C:C + 1, C:2 * C], io["L1_gnn_b_r"][None, :]),
                (wns[C:C + 1, C:2 * C], io["L3_gnn_b_self"][None, :]),
                (w1a[:, :], io["L2_gnn_W1"][0:C, :]), (w1b[0:C, :], io["L2_gnn_W1"][C:2 * C, :]),
                (w1b[C:C + 1, :], io["L2_gnn_b1"][None, :]), (w2[:, :], io["L2_gnn_W2"])]
            spread = [io["L0_gnn_bo"], io["L1_gnn_att"].rearrange("a h c -> (a h c)"), io["L1_gnn_bias"],
                      io["L1_gnn_gamma"], io["L1_gnn_beta"], io["L2_gnn_b2"]]
            weights += [(vecs[:, i, :], v[None, :].to_broadcast([P, C])) for i, v in enumerate(spread)]
            assert len(weights) == NW
            for dst, src in weights:
                load(dst, src, "w_in")

            wait_next("kpv_made")
            whole = N // KVOL
            load(kpv_dram[0:whole * KVOL, :].rearrange("(i k) c -> k i c", k=KVOL),
                 split(rows[0:KVOL, 0:whole * HID], HID), "kpv_out")
            load(kpv_dram[whole * KVOL:N, :], rows[0:N - whole * KVOL, whole * HID:NI * HID], "kpv_out")

            wait_next("xl_made")
            load(xl_dram.rearrange("(b p) c -> p b c", p=P), split(rows[:, 0:NB * C], C), "xl_out")

            wait_next("steps_made")
            attrs = io["edge_attr_16"].rearrange("(c j p) k -> p c j k", j=G, p=P)

            def attr(q, s, i):
                c = sp.value_load(ctab[0:1, bass.ds(q, 1)], min_val=0, max_val=NCH - 1)
                done(sp, "l1_tr", q - SLOTS)
                load(atr[s].ap().rearrange("p (o j k) -> p o j k", o=1, j=G), attrs[:, bass.ds(c, 1), :, :],
                     f"l1_attr{s}")

            def attr_and_spill(q, s, i):
                attr(q, s, i)
                sp.wait_ge(S(f"l1_rows{s}"), i * 16 * G + 16 * G)
                load(spill_dram[:, bass.ds(q, 1), :].rearrange("p o c -> p (o c)"), g64[s][:, :], f"l1_spill{s}")

            steps(sp, attr_and_spill)
            attr(NQ, 0, NQ // SLOTS)
            for s in range(SLOTS):
                sp.wait_ge(S(f"l1_spill{s}"), 16 * NQ // SLOTS)
            wait_next("l1_logits")

            def respill(q, s, i):
                done(sp, "l1b_pay", q - SLOTS)
                load(g64[s][:, :], spill_dram[:, bass.ds(q, 1), :].rearrange("p o c -> p (o c)"), f"l1b_rows{s}")

            steps(sp, respill)

            wait_next("a_made")
            load(a_dram.rearrange("(b p) c -> p b c", p=P), split(rows[:, 0:NB * HID], HID), "a_out")
            for _ in range(3):
                wait_next("x_made")
            load(x3_dram.rearrange("(b p) c -> p b c", p=P), x[:, :, :], "x3_out")
            wait_next("x_made")
            load(out.rearrange("(b p) c -> p b c", p=P), x[:, :, :], "result_out")
            for name, n in (("result_out", 1), ("kpv_out", 2), ("xl_out", 1), ("a_out", 1), ("x3_out", 1)):
                sp.wait_ge(S(name), 16 * n)

        @block.gpsimd
        def _(pool):
            wait_next = counted(pool)
            pool.iota(col_i[:, :], pattern=[[1, NT]], base=0, channel_multiplier=0).then_inc(S("iota"), 1)
            pool.iota(part_i[:, :], pattern=[[0, 1]], base=0, channel_multiplier=1).then_inc(S("iota"), 1)
            pool.memset(ident[:, :], 0.0).then_inc(S("pool_set"), 1)
            pool.memset(gmask[:, :], 1.0).then_inc(S("pool_set"), 1)
            pool.wait_ge(S("pool_set"), 2)
            pool.affine_select(out=ident[:, :], in_=ident[:, :], compare_op=ALU.not_equal, fill=1.0, base=0,
                               pattern=[[-1, P]], channel_multiplier=1).then_inc(S("ident"), 1)
            pool.affine_select(out=gmask[:, :], in_=gmask[:, :], compare_op=ALU.is_ge, fill=0.0, base=0,
                               pattern=[[-ED, G]], channel_multiplier=1).then_inc(S("pool_set"), 1)
            pool.wait_ge(S("pool_set"), 3)
            pool.affine_select(out=gmask[:, :], in_=gmask[:, :], compare_op=ALU.is_ge, fill=0.0, base=ED - 1,
                               pattern=[[ED, G]], channel_multiplier=-1).then_inc(S("gmask"), 1)

            def gather(layer, table, dst, used):
                def step(q, s, i):
                    done(pool, used, q - SLOTS)
                    if layer == "l1" and not (isinstance(i, int) and i == 0):
                        pool.wait_ge(S(f"l1_spill{s}"), i * 16)
                    pool.tensor_copy(idx[s][:, :], srcI[:, bass.ds(q * G, G)]).then_inc(S(f"{layer}_idx"), 1)
                    pool.wait_ge(S(f"{layer}_idx"), q + 1)
                    pool.nop(nofuse=True)
                    for j in range(G):
                        pool.indirect_dma_start(dst(s, j), None, table[:, :],
                                                bass.IndirectOffsetOnAxis(idx[s][:, j:j + 1], 0)) \
                            .then_inc(S(f"{layer}_rows{s}"), 16)
                steps(pool, step)

            def wide(s, j):
                return gat[s][:, j, :]

            def slim(s, j):
                return g64[s][:, j * C:(j + 1) * C]

            wait_next("steps_made")
            pool.wait_ge(S("kpv_out"), 32)
            gather("l0", kpv_dram, wide, "l0_pay")
            pool.wait_ge(S("xl_out"), 16)
            gather("l1", xl_dram, slim, "l1_z")
            pool.wait_ge(S("a_out"), 16)
            gather("l2", a_dram, wide, "l2_z")
            pool.wait_ge(S("x3_out"), 16)
            gather("l3", x3_dram, slim, "l3_sum")

        @block.tensor
        def _(pe):
            wait_next = counted(pe)

            def transpose_nodes(src, width, made):
                for b in range(NB):
                    last = pe.transpose(top[0:width, b * P:(b + 1) * P], src(b), ident[:, :])
                last.then_inc(S(made), 1)

            def project(dst, lhs, weight, width, name=None, start=True, stop=True):
                for b in range(NB):
                    last = pe.matmul(dst(b), lhs[:, b * P:(b + 1) * P], weight, start=start, stop=stop,
                                     skip_group_check=True)
                if name:
                    last.then_inc(S(name), 1)

            def zero_sums():
                wait_next("sums_free")
                for k in range(4):
                    pe.matmul(ps[:, k, :], zeros[0:1, 0:P], zeros[0:1, :], start=True, stop=True,
                              skip_group_check=True)

            def spread_targets(layer, q, s):
                done(pe, f"{layer}_ohT", q - SLOTS)
                for part in (dhi, dlo):
                    last = pe.matmul(bc[s], sel[:, bass.ds(q, 1)].to_broadcast([P, P]), part[:, :],
                                     start=part is dhi, stop=part is dlo)
                last.then_inc(S(f"{layer}_bc"), 1)

            def block_of(q):
                return pe.value_load(btab[0:1, bass.ds(q, 1)], min_val=0, max_val=NB - 1)

            def take_targets(layer, q, s, width, used):
                b = block_of(q)
                done(pe, f"{layer}_ohT", q)
                done(pe, used, q - SLOTS)
                for j in range(G):
                    last = pe.matmul(ga[s][:, j * width:(j + 1) * width], ohT[s][:, j * P:(j + 1) * P],
                                     tab[:, bass.ds(b * width, width)], start=True, stop=True)
                last.then_inc(S(f"{layer}_ga"), 1)

            def sum_rows(layer, q, s, rhs, width, wait_rows):
                b = block_of(q)
                wait_rows()
                done(pe, f"{layer}_oh", q)
                for j in range(G):
                    last = pe.matmul(acc[:, bass.ds(b * P, width)], oh[s][:, j, :], rhs(s, j),
                                     start=False, stop=True, skip_group_check=True)
                last.then_inc(S(f"{layer}_sum"), 1)

            wait_next("begun_made")
            pe.matmul(ps[:, 0, 0:NT], ones[:, :], selF[:, :], start=True, stop=True).then_inc(S("begun_ps"), 1)
            wait_next("sel_made")
            for r, ids in enumerate((src_f, dst_f)):
                for j in range(G):
                    last = pe.matmul(ps[:, r * G + j, 0:NT], ids[:, j * P:(j + 1) * P], selF[:, :],
                                     start=True, stop=True)
            last.then_inc(S("ids_ps"), 1)
            wait_next("steps_made")
            wait_next("ident")
            pe.wait_ge(S("w_in"), 16 * NW)
            pe.wait_ge(S("x_in"), 16)
            for k in range(4):
                pe.transpose(ps[0:C, 0, k * C:(k + 1) * C], wraw[:, k * C:(k + 1) * C], ident[0:C, 0:C])
            pe.matmul(ps[0:G * ED, 1, 0:C], weraw[:, :], ident[0:C, 0:C],
                      start=True, stop=True).then_inc(S("wt_ps"), 1)
            transpose_nodes(lambda b: x[:, b, :], C, "xT_ps")

            wait_next("wt_made")
            wait_next("xT_made")
            project(lambda b: acc[:, b * C:(b + 1) * C], xT, wq[:, :], C)
            pe.matmul(ps[0:NI, 2, 0:2 * C], xT[:, 0:NI], wkv[:, :], start=True, stop=True).then_inc(S("qkv_ps"), 1)
            wait_next("kvn_made")
            for i in range(NI):
                o = top[0:KVOL, i * HID:(i + 1) * HID] if i < NB else ps[0:KVOL, 3, 0:HID]
                last = pe.matmul(o, ident[0:NI, i:i + 1].to_broadcast([NI, KVOL]), kvn[:, :], start=True, stop=True)
            last.then_inc(S("kpv_ps"), 1)
            zero_sums()
            spread_targets("l0", 0, 0)
            take_targets("l0", 0, 0, C, "l0_prod")

            def step0(q, s, i):
                spread_targets("l0", q + 1, 1 - s)
                take_targets("l0", q + 1, 1 - s, C, "l0_prod")
                sum_rows("l0", q, s, lambda s, j: pay[s][:, j, 0:C + 1], C + 1, lambda: done(pe, "l0_pay", q))
            steps(pe, step0)
            wait_next("agg_made")
            transpose_nodes(lambda b: h[:, b, :], C, "aggT_ps")
            wait_next("aggT_made")
            project(lambda b: acc[:, b * C:(b + 1) * C], aggT[0:C, :], wo[:, :], C, "proj_ps")

            wait_next("x_made")
            transpose_nodes(lambda b: x[:, b, :], C, "xT_ps")
            wait_next("xT_made")
            project(lambda b: acc[:, b * P:(b + 1) * P], xT, wlr[:, :], P, "proj_ps")

            def take1(q, s, i):
                pe.wait_ge(S(f"l1_attr{s}"), i * 16 + 16)
                done(pe, "l1_z", q - SLOTS)
                pe.nop(nofuse=True)
                pe.transpose(ga[s][0:G * ED, 2 * P:3 * P], atr[s][:, :], ident[:, :]).then_inc(S("l1_tr"), 1)
                b = block_of(q)
                done(pe, "l1_atT", q)
                pe.matmul(ga[s][:, 0:G * C], atT[s][:, :], web[:, :, :].rearrange("p j c -> p (j c)"),
                          start=True, stop=False, skip_group_check=True)
                done(pe, "l1_ohT", q)
                for j in range(G):
                    last = pe.matmul(ga[s][:, j * C:(j + 1) * C], ohT[s][:, j * P:(j + 1) * P],
                                     tab[:, bass.ds(b * C, C)], start=False, stop=j == G - 1,
                                     skip_group_check=True)
                last.then_inc(S("l1_ga"), 1)

            def step1(q, s, i):
                spread_targets("l1", q + 1, 1 - s)
                take1(q + 1, 1 - s, i + s)
            wait_next("xr_made")
            spread_targets("l1", 0, 0)
            take1(0, 0, 0)
            steps(pe, step1)

            wait_next("l1_logits")
            bank = 0
            for by_tile in (brk, run):
                for k in range(0, KG, 4):
                    done(pe, "bank_out", bank - 8)
                    for j in range(4):
                        last = pe.transpose(ps[:, bank % 8, j * P:(j + 1) * P], by_tile[:, (k + j) * P:(k + j + 1) * P],
                                            ident[:, :])
                    last.then_inc(S("bank_in"), 1)
                    bank += 1
            wait_next("ends_made")
            done(pe, "bank_out", bank - 1)
            for k in range(4):
                last = pe.matmul(ps[0:1, k, 0:P], ends[:, k:k + 1], ident[:, :], start=True, stop=True)
            last.then_inc(S("ends_ps"), 1)
            wait_next("carry_made")
            for k in range(2):
                last = pe.matmul(ps[:, 4 + k, 0:1], crow[0:1, 10 + k, :], ones[0:1, 0:1], start=True, stop=True)
            last.then_inc(S("carry_ps"), 1)
            wait_next("ex_made")
            for n, k in enumerate(range(0, KG, 4)):
                done(pe, "ex_out", n - 8)
                for j in range(4):
                    last = pe.transpose(ps[:, n % 8, j * P:(j + 1) * P], lgT[:, (k + j) * P:(k + j + 1) * P],
                                        ident[:, :])
                last.then_inc(S("ex_in"), 1)
            done(pe, "ex_out", KG // 4 - 1)
            zero_sums()

            def step1b(q, s, i):
                sum_rows("l1b", q, s, lambda s, j: pay[s][:, j, 0:C + H1], C + H1, lambda: done(pe, "l1b_pay", q))
            steps(pe, step1b)

            wait_next("x_made")
            transpose_nodes(lambda b: x[:, b, :], C, "xT_ps")
            wait_next("xT_made")
            project(lambda b: acc[:, b * P:(b + 1) * P], xT[0:C, :], w1a[:, :], P)
            project(lambda b: top[:, b * P:(b + 1) * P], xT, w1b[:, :], P, "proj_ps")
            zero_sums()
            spread_targets("l2", 0, 0)
            take_targets("l2", 0, 0, HID, "l2_z")

            def step2(q, s, i):
                spread_targets("l2", q + 1, 1 - s)
                take_targets("l2", q + 1, 1 - s, HID, "l2_z")
                sum_rows("l2", q, s, lambda s, j: pay[s][:, j, :], HID, lambda: done(pe, "l2_relu", q))
            steps(pe, step2)
            wait_next("agg_made")
            transpose_nodes(lambda b: rows[:, b * P:(b + 1) * P], HID, "aggT_ps")
            wait_next("aggT_made")
            project(lambda b: acc[:, b * C:(b + 1) * C], aggT, w2[:, :], C, "proj_ps")

            wait_next("x_made")
            transpose_nodes(lambda b: x[:, b, :], C, "xT_ps")
            zero_sums()

            def step3(q, s, i):
                sum_rows("l3", q, s, lambda s, j: g64[s][:, j * C:(j + 1) * C], C,
                         lambda: pe.wait_ge(S(f"l3_rows{s}"), i * 16 * G + 16 * G))
            steps(pe, step3)
            wait_next("xT_made")
            wait_next("agg_made")
            transpose_nodes(lambda b: h[:, b, :], C, "aggT_ps")
            wait_next("aggT_made")
            for b in range(NB):
                pe.matmul(acc[:, b * C:(b + 1) * C], aggT[0:C, b * P:(b + 1) * P], wns[0:C, 0:C],
                          start=True, stop=False, skip_group_check=True)
                last = pe.matmul(acc[:, b * C:(b + 1) * C], xT[:, b * P:(b + 1) * P], wns[:, C:2 * C],
                                 start=False, stop=True, skip_group_check=True)
            last.then_inc(S("proj_ps"), 1)

        @block.scalar
        def _(act):
            wait_next = counted(act)

            def copy_banks(dst, width, ready, made):
                wait_next(ready)
                for k in range(4):
                    last = act.activation(dst[0:width, k * 512:(k + 1) * 512], ps[0:width, 4 + k, :], ACT.Copy)
                last.then_inc(S(made), 1)

            def root(dst, src):
                wait_next("square_sum")
                act.activation(dst, src, ACT.Sqrt).then_inc(S("root"), 1)

            copy_banks(xT, C, "xT_ps", "xT_made")
            root(nrm[:, 0:NB * H0], nrm[:, 0:NB * H0])
            root(nrm[0:NI, 0:H0], nrm[0:NI, 0:H0])
            root(nrm[0:KVOL, 0:H0], nrm[0:KVOL, 0:H0])
            copy_banks(aggT, C, "aggT_ps", "aggT_made")
            root(st2[:, :], st2[:, :])
            copy_banks(xT, C, "xT_ps", "xT_made")

            def attrs(q, s, i):
                done(act, "l1_tr", q)
                done(act, "l1_ga", q - SLOTS)
                act.activation(atT[s][:, :], ga[s][0:G * ED, 2 * P:3 * P], ACT.Copy).then_inc(S("l1_atT"), 1)
            steps(act, attrs)
            attrs(NQ, 0, NQ // SLOTS)
            bank = 0
            for dst in (keyT, lgT):
                for k in range(0, KG, 4):
                    done(act, "bank_in", bank)
                    act.activation(dst[:, k * P:(k + 4) * P], ps[:, bank % 8, :], ACT.Copy) \
                        .then_inc(S("bank_out"), 1)
                    bank += 1
            wait_next("shift_made")
            act.activation(lgT[:, :], lgT[:, :], ACT.Exp).then_inc(S("ex_made"), 1)
            for n, k in enumerate(range(0, KG, 4)):
                done(act, "ex_in", n)
                act.activation(lg[:, :].rearrange("p (g k h) -> p k g h", g=NG, h=H1)[:, k:k + 4, :, :],
                               ps[:, n % 8, :].rearrange("p (k g h) -> p k g h", k=4, h=H1), ACT.Copy) \
                    .then_inc(S("ex_out"), 1)
            root(st2[:, :], st2[:, :])
            root(st2[:, :], st2[:, :])
            copy_banks(xT, C, "xT_ps", "xT_made")

            def relu(q, s, i):
                done(act, "l2_z", q)
                act.activation(pay[s][:, :, :], pay[s][:, :, :], ACT.Relu) \
                    .then_inc(S("l2_relu"), 1)
            steps(act, relu)
            copy_banks(aggT, HID, "aggT_ps", "aggT_made")
            root(st2[:, :], st2[:, :])
            copy_banks(xT, C, "xT_ps", "xT_made")
            copy_banks(aggT, C, "aggT_ps", "aggT_made")
            root(st2[:, :], st2[:, :])

        @block.vector
        def _(v):
            wait_next = counted(v)
            chain = [0]

            def link(ins):
                chain[0] += 1
                ins.then_inc(S("vector_chain"), 1)
                v.wait_ge(S("vector_chain"), chain[0])

            def over(vec, k):
                return vec[:, k:k + 1, :].to_broadcast([P, NB, C])

            def per_row(t, width=C):
                return t[:, :, None].to_broadcast([P, NB, width])

            v.memset(ones[:, :], 1.0)
            v.memset(zeros[:, :], 0.0)
            for w in (xT[C:C + 1, :],):
                v.memset(w, 1.0)
            v.memset(pay[0][:, :, C:C + 1], 1.0)
            v.memset(pay[1][:, :, C:C + 1], 1.0)
            v.wait_ge(S("iota"), 2)
            v.tensor_copy(col_f[:, :], col_i[:, :])
            link(v.tensor_copy(part_f[:, :], part_i[:, :]))
            link(v.tensor_single_scalar(notfirst[:, :], part_f[:, :], 0.0, op=ALU.is_gt))
            v.wait_ge(S("dst_in"), 16)
            link(v.tensor_single_scalar(blk[:, :], dst_i[:, 0:1], 7, op=ALU.arith_shift_right))
            link(v.tensor_copy(qc[:, 0:1], blk[:, :]))
            link(v.scalar_tensor_tensor(out=qc[:, 1:2], in0=qc[:, 0:1], scalar=notfirst[:, 0:1],
                                        in1=part_f[:, :], op0=ALU.mult, op1=ALU.add))
            v.tensor_scalar(selF[:, :], col_f[:, :], qc[:, 1:2], None, ALU.is_ge).then_inc(S("begun_made"), 1)
            v.tensor_copy(dst_f[:, :], dst_i[:, :])
            v.wait_ge(S("src_in"), 16)
            v.tensor_copy(src_f[:, :], src_i[:, :])
            wait_next("begun_ps")
            link(v.tensor_scalar(cqb[:, :], ps[:, 0, 0:NT], -1.0, None, ALU.add))
            v.tensor_scalar(sel[:, :], cqb[:, :], part_f[:, 0:1], None, ALU.is_equal)
            v.tensor_scalar(selF[:, :], cqb[:, :], part_f[:, 0:1], None, ALU.is_equal).then_inc(S("sel_made"), 1)
            v.tensor_copy(ctab[:, :], cqb[:, :])
            link(v.tensor_tensor(bqb[:, :], col_f[:, :], cqb[:, :], ALU.subtract))
            v.tensor_scalar(btab[:, :], bqb[:, :], float(NB - 1), None, ALU.min)
            link(v.tensor_scalar(bqb[:, :], bqb[:, :], float(P), None, ALU.mult))
            v.tensor_scalar(nb[:, :], bqb[:, :], part_f[:, 0:1], None, ALU.add)
            link(v.tensor_scalar(tmp_i[:, :], dst_i[:, :], 7, 7, ALU.arith_shift_right, ALU.arith_shift_left))
            link(v.tensor_copy(dhi[:, :], tmp_i[:, :]))
            link(v.tensor_single_scalar(tmp_i[:, :], dst_i[:, :], P - 1, op=ALU.bitwise_and))
            v.tensor_copy(dlo[:, :], tmp_i[:, :])
            wait_next("ids_ps")
            for j in range(G):
                v.tensor_copy(split(srcI[:, :], G)[:, :, j], ps[:, j, 0:NT])
                last = v.tensor_copy(split(dstK[:, :], G)[:, :, j], ps[:, G + j, 0:NT])
            link(last)
            link(v.tensor_tensor(split(dstL[:, :], G), split(dstK[:, :], G),
                                 bqb[:, :, None].to_broadcast([P, NT, G]), ALU.subtract))
            v.tensor_single_scalar(pen[:, :], dstL[:, :], 0.0, op=ALU.is_ge)
            link(v.tensor_single_scalar(prod[:, 0:0 + 512], dstL[:, 0:512], float(P), op=ALU.is_lt))
            link(v.tensor_tensor(pen[:, 0:512], pen[:, 0:512], prod[:, 0:512], ALU.mult))
            rest = NT * G - 512
            link(v.tensor_single_scalar(prod[:, 0:rest], dstL[:, 512:NT * G], float(P), op=ALU.is_lt))
            link(v.tensor_tensor(pen[:, 512:NT * G], pen[:, 512:NT * G], prod[:, 0:rest], ALU.mult))
            v.tensor_scalar(pen[:, :], pen[:, :], -1.0, BIG, ALU.add, ALU.mult).then_inc(S("steps_made"), 1)

            wait_next("wt_ps")
            v.tensor_copy(wlr[0:C, :], ps[0:C, 0, 0:2 * C])
            v.tensor_copy(wns[0:C, :], ps[0:C, 0, 2 * C:4 * C])
            v.wait_ge(S("gmask"), 1)
            for j in range(G):
                last = v.tensor_scalar(web[:, j, :], ps[0:G * ED, 1, 0:C], gmask[:, j:j + 1], None, ALU.mult)
            last.then_inc(S("wt_made"), 1)

            def normalise(dst, src, parts, heads):
                w = heads * D0
                link(v.tensor_tensor(sq[0:parts, 0:w], src, src, ALU.mult))
                link(v.reduce_sum(nrm[0:parts, 0:heads], split(sq[0:parts, 0:w], D0), AX.X))
                v.tensor_single_scalar(nrm[0:parts, 0:heads], nrm[0:parts, 0:heads], 1e-24, op=ALU.max) \
                    .then_inc(S("square_sum"), 1)
                wait_next("root")
                link(v.reciprocal(nrm[0:parts, 0:heads], nrm[0:parts, 0:heads]))
                link(v.tensor_tensor(split(dst, D0), split(src, D0),
                                     nrm[0:parts, 0:heads, None].to_broadcast([parts, heads, D0]), ALU.mult))

            wait_next("qkv_ps")
            hf = h[:, :, :].rearrange("p b c -> p (b c)")
            v.tensor_copy(kvn[:, :], ps[0:NI, 2, 0:2 * C])
            link(v.tensor_copy(hf, acc[:, 0:NB * C]))
            normalise(tab[:, 0:NB * C], hf, P, NB * H0)
            normalise(kvn[:, 0:C], kvn[:, 0:C], NI, H0)
            v.tensor_copy(kvn[:, C:C + 1], kvn[:, C:C + 1]).then_inc(S("kvn_made"), 1)
            normalise(pos[:, :], pos[:, :], KVOL, H0)
            wait_next("kpv_ps")
            posn = pos[:, None, :].to_broadcast([KVOL, NB, C])
            v.tensor_tensor(split(rows[0:KVOL, 0:NB * HID], HID)[:, :, 0:C], split(top[0:KVOL, :], HID)[:, :, 0:C],
                            posn, ALU.add)
            v.tensor_copy(split(rows[0:KVOL, 0:NB * HID], HID)[:, :, C:HID], split(top[0:KVOL, :], HID)[:, :, C:HID])
            v.tensor_tensor(rows[0:KVOL, NB * HID:NB * HID + C], ps[0:KVOL, 3, 0:C], pos[:, :], ALU.add)
            link(v.tensor_copy(rows[0:KVOL, NB * HID + C:NI * HID], ps[0:KVOL, 3, C:HID]))
            v.memset(sq[:, 0:1], 0.0).then_inc(S("kpv_made"), 1)
            v.memset(sq[:, 1:2], 0.0).then_inc(S("sums_free"), 1)

            def onehot_T(layer, q, s, used):
                done(v, f"{layer}_bc", q)
                done(v, used, q - SLOTS)
                v.tensor_scalar(ohT[s][:, :], bc[s], nb[:, bass.ds(q, 1)], None, ALU.is_equal) \
                    .then_inc(S(f"{layer}_ohT"), 1)

            def onehot(layer, q, s):
                done(v, f"{layer}_sum", q - SLOTS)
                v.tensor_tensor(oh[s][:, :, :], col_f[:, None, 0:P].to_broadcast([P, G, P]),
                                dstL[:, bass.ds(q * G, G)][:, :, None].to_broadcast([P, G, P]), ALU.is_equal) \
                    .then_inc(S(f"{layer}_oh"), 1)

            def step0(q, s, i):
                onehot_T("l0", q + 1, 1 - s, "l0_ga")
                onehot("l0", q, s)
                done(v, "l0_ga", q)
                v.wait_ge(S(f"l0_rows{s}"), i * 16 * G + 16 * G)
                v.tensor_tensor(split(prod[:, 0:G * C], C), split(ga[s][:, 0:G * C], C), gat[s][:, :, 0:C],
                                ALU.mult).then_inc(S("l0_prod"), 1)
                done(v, "l0_prod", q)
                v.reduce_sum(attn[:, :], split(prod[:, 0:G * C], D0), AX.X).then_inc(S("l0_attn"), 1)
                done(v, "l0_attn", q)
                for j in range(G):
                    last = v.tensor_tensor(split(pay[s][:, j, 0:C], D0), split(gat[s][:, j, C:2 * C], D0),
                                           attn[:, j * H0:(j + 1) * H0, None].to_broadcast([P, H0, D0]), ALU.mult)
                last.then_inc(S("l0_pay"), 1)
            onehot_T("l0", 0, 0, "l0_ga")
            steps(v, step0)

            def norm(dst, gamma=None):
                link(v.reduce_sum(st1[:, :], h[:, :, :], AX.X))
                link(v.tensor_single_scalar(st1[:, :], st1[:, :], 1.0 / C, op=ALU.mult))
                link(v.tensor_tensor(h[:, :, :], h[:, :, :], per_row(st1), ALU.subtract))
                link(v.tensor_tensor(split(sq[:, 0:NB * C], C), h[:, :, :], h[:, :, :], ALU.mult))
                link(v.reduce_sum(st2[:, :], split(sq[:, 0:NB * C], C), AX.X))
                v.tensor_scalar(st2[:, :], st2[:, :], 1.0 / C, 1e-5, ALU.mult, ALU.add).then_inc(S("square_sum"), 1)
                wait_next("root")
                link(v.reciprocal(st3[:, :], st2[:, :]))
                if gamma is None:
                    v.tensor_tensor(dst, h[:, :, :], per_row(st3), ALU.mult).then_inc(S("x_made"), 1)
                    return
                link(v.tensor_tensor(h[:, :, :], h[:, :, :], per_row(st3), ALU.mult))
                link(v.tensor_tensor(h[:, :, :], h[:, :, :], over(vecs, VGAMMA), ALU.mult))
                link(v.tensor_tensor(h[:, :, :], h[:, :, :], over(vecs, VBETA), ALU.add))
                link(v.tensor_single_scalar(h[:, :, :], h[:, :, :], 0.0, op=ALU.max))

            done(v, "l0_sum", NQ - 1)
            accb = split(acc, P)
            v.tensor_copy(cnt[:, :], accb[:, :, C])
            v.tensor_copy(h[:, :, :], accb[:, :, 0:C]).then_inc(S("agg_made"), 1)
            wait_next("agg_made")
            link(v.tensor_single_scalar(rdeg[:, :], cnt[:, :], 1.0, op=ALU.max))
            v.reciprocal(rdeg[:, :], rdeg[:, :])
            wait_next("proj_ps")
            link(v.tensor_tensor(h[:, :, :], split(acc[:, 0:NB * C], C), over(vecs, VBO), ALU.add))
            link(v.scalar_tensor_tensor(out=h[:, :, :], in0=x[:, :, :], scalar=2.0, in1=h[:, :, :],
                                        op0=ALU.mult, op1=ALU.add))
            norm(x[:, :, :])

            wait_next("proj_ps")
            v.tensor_copy(split(rows[:, 0:NB * C], C), accb[:, :, 0:C]).then_inc(S("xl_made"), 1)
            v.tensor_copy(split(tab[:, 0:NB * C], C), accb[:, :, C:P]).then_inc(S("xr_made"), 1)

            def step1(q, s, i):
                onehot_T("l1", q + 1, 1 - s, "l1_ga")
                done(v, "l1_ga", q)
                v.wait_ge(S(f"l1_rows{s}"), i * 16 * G + 16 * G)
                v.tensor_tensor(prod[:, 0:G * C], ga[s][:, 0:G * C], g64[s][:, :], ALU.add).then_inc(S("l1_z"), 1)
                done(v, "l1_z", q)
                v.scalar_tensor_tensor(out=lky[:, :], in0=prod[:, 0:G * C], scalar=0.2, in1=prod[:, 0:G * C],
                                       op0=ALU.mult, op1=ALU.max).then_inc(S("l1_lky"), 1)
                done(v, "l1_lky", q)
                v.tensor_tensor(split(wgt[:, :], C), split(lky[:, :], C),
                                vecs[:, VATT:VATT + 1, :].to_broadcast([P, G, C]), ALU.mult) \
                    .then_inc(S("l1_wgt"), 1)
                done(v, "l1_wgt", q)
                v.reduce_sum(lg[:, bass.ds(q * G * H1, G * H1)], split(wgt[:, :], D1), AX.X).then_inc(S("l1_lg"), 1)
            onehot_T("l1", 0, 0, "l1_ga")
            steps(v, step1)
            done(v, "l1_lg", NQ - 1)
            def by_group(t):
                return t.rearrange("p (g k) -> p g k", g=NG)[:, :, :, None].to_broadcast([P, NG, KG, H1])

            def by_tile(t):
                return t.rearrange("p (k g h) -> p g k h", g=NG, h=H1)
            v.tensor_copy(by_tile(brk[:, 0:TL]), by_group(dstK[:, 0:NQ * G]))
            v.tensor_tensor(by_tile(run[:, :]), lg[:, :].rearrange("p (g k h) -> p g k h", g=NG, h=H1),
                            by_group(pen[:, 0:NQ * G]), ALU.add).then_inc(S("l1_logits"), 1)

            done(v, "bank_out", KG // 4 - 1)
            v.memset(brk[:, 0:1], 0.0)
            v.memset(brk[:, TL:TL + 1], 0.0)
            link(v.tensor_tensor(brk[:, 1:TL], keyT[:, 1:TL], keyT[:, 0:TL - 1], ALU.is_equal))
            link(v.tensor_scalar(brk[:, 1:TL], brk[:, 1:TL], -1.0, BIG, ALU.add, ALU.mult))
            done(v, "bank_out", 2 * KG // 4 - 1)

            def scan_right(src, initial):
                link(v.tensor_tensor_scan(out=run[:, :], data0=brk[:, 0:TL], data1=src, initial=initial,
                                          op0=ALU.add, op1=ALU.max))

            def scan_left(src, initial):
                link(v.tensor_tensor_scan(out=run[:, ::-1], data0=brk[:, 1:TL + 1][:, ::-1], data1=src[:, ::-1],
                                          initial=initial, op0=ALU.add, op1=ALU.max))
            scan_right(lgT[:, :], -BIG)
            v.tensor_copy(ends[:, 0:1], run[:, TL - 1:TL])
            v.tensor_copy(ends[:, 2:3], keyT[:, 0:1])
            link(v.tensor_copy(ends[:, 3:4], keyT[:, TL - 1:TL]))
            scan_left(lgT[:, :], -BIG)
            v.tensor_copy(ends[:, 1:2], run[:, 0:1]).then_inc(S("ends_made"), 1)
            wait_next("ends_ps")
            LAST, FIRST, KF, KL, WHOLE, SAME, S0, S1, T0, T1, CR, CL = range(12)
            for k in range(4):
                last = v.tensor_copy(crow[0:1, k, :].rearrange("p (h g) -> p h g", g=NG),
                                     ps[0:1, k, 0:P].rearrange("p (g h) -> p h g", h=H1))
            link(last)

            def row(k, a=0, b=NG):
                return crow[0:1, k, :].rearrange("p (h g) -> p h g", g=NG)[:, :, a:b]
            v.memset(crow[0:1, SAME:T1 + 1, :].rearrange("p a b -> p (a b)"), -BIG)
            link(v.tensor_tensor(row(WHOLE), row(KF), row(KL), ALU.is_equal))
            link(v.tensor_scalar(row(WHOLE), row(WHOLE), -1.0, BIG, ALU.add, ALU.mult))
            link(v.tensor_tensor(row(SAME, 0, NG - 1), row(KL, 0, NG - 1), row(KF, 1, NG), ALU.is_equal))
            link(v.tensor_scalar(row(SAME, 0, NG - 1), row(SAME, 0, NG - 1), -1.0, BIG, ALU.add, ALU.mult))
            v.tensor_tensor(row(S0, 1, NG), row(SAME, 0, NG - 1), row(WHOLE, 0, NG - 1), ALU.add)
            v.tensor_tensor(row(S1, 1, NG), row(SAME, 0, NG - 1), row(LAST, 0, NG - 1), ALU.add)
            v.tensor_tensor(row(T0, 0, NG - 1), row(SAME, 0, NG - 1), row(WHOLE, 1, NG), ALU.add)
            link(v.tensor_tensor(row(T1, 0, NG - 1), row(SAME, 0, NG - 1), row(FIRST, 1, NG), ALU.add))
            link(v.tensor_tensor_scan(out=crow[0:1, WHOLE, :], data0=crow[0:1, S0, :], data1=crow[0:1, S1, :],
                                      initial=-BIG, op0=ALU.add, op1=ALU.max))
            link(v.tensor_tensor_scan(out=crow[0:1, SAME, ::-1], data0=crow[0:1, T0, ::-1],
                                      data1=crow[0:1, T1, ::-1], initial=-BIG, op0=ALU.add, op1=ALU.max))
            for o, k in ((CR, WHOLE), (CL, SAME)):
                last = v.tensor_copy(crow[0:1, o, :].rearrange("p (g h) -> p h g", h=H1), row(k))
            last.then_inc(S("carry_made"), 1)
            wait_next("carry_ps")
            for k in range(2):
                last = v.tensor_copy(carry[:, k:k + 1], ps[:, 4 + k, 0:1])
            link(last)
            scan_right(lgT[:, :], carry[:, 0:1])
            link(v.tensor_copy(keyT[:, :], run[:, :]))
            scan_left(keyT[:, :], carry[:, 1:2])
            v.tensor_tensor(lgT[:, :], lgT[:, :], run[:, :], ALU.subtract).then_inc(S("shift_made"), 1)

            v.memset(sq[:, 0:1], 0.0).then_inc(S("sums_free"), 1)
            done(v, "ex_out", KG // 4 - 1)

            def step1b(q, s, i):
                onehot("l1b", q, s)
                ex = lg[:, bass.ds(q * G * H1, G * H1)]
                v.tensor_copy(pay[s][:, :, C:C + H1], split(ex, H1))
                v.wait_ge(S(f"l1b_rows{s}"), i * 16 + 16)
                for j in range(G):
                    last = v.tensor_tensor(split(pay[s][:, j, 0:C], D1), split(g64[s][:, j * C:(j + 1) * C], D1),
                                           lg[:, bass.ds(q * G * H1 + j * H1, H1)][:, :, None]
                                           .to_broadcast([P, H1, D1]), ALU.mult)
                last.then_inc(S("l1b_pay"), 1)
            steps(v, step1b)
            done(v, "l1b_sum", NQ - 1)
            den = sq[:, NB * C:NB * C + NB * H1]
            link(v.tensor_single_scalar(split(den, H1), accb[:, :, C:C + H1], 1e-16, op=ALU.add))
            link(v.reciprocal(den, den))
            v.tensor_copy(h[:, :, :], accb[:, :, 0:C])
            link(v.memset(sq[:, 0:1], 0.0))
            hh = h[:, :, :].rearrange("p b c -> p (b c)")
            link(v.tensor_tensor(split(hh, D1), split(hh, D1), den[:, :, None].to_broadcast([P, NB * H1, D1]),
                                 ALU.mult))
            link(v.tensor_tensor(h[:, :, :], h[:, :, :], over(vecs, VBIAS), ALU.add))
            link(v.tensor_tensor(h[:, :, :], h[:, :, :], x[:, :, :], ALU.add))
            norm(None, gamma=True)
            link(v.tensor_tensor(h[:, :, :], h[:, :, :], x[:, :, :], ALU.add))
            norm(x[:, :, :])

            wait_next("proj_ps")
            v.tensor_copy(rows[:, 0:NB * HID], acc).then_inc(S("a_made"), 1)
            v.tensor_copy(tab[:, :], top).then_inc(S("sums_free"), 1)

            def step2(q, s, i):
                onehot_T("l2", q + 1, 1 - s, "l2_ga")
                onehot("l2", q, s)
                done(v, "l2_ga", q)
                v.wait_ge(S(f"l2_rows{s}"), i * 16 * G + 16 * G)
                v.tensor_tensor(pay[s][:, :, :], split(ga[s], HID), gat[s][:, :, :], ALU.add) \
                    .then_inc(S("l2_z"), 1)
            onehot_T("l2", 0, 0, "l2_ga")
            steps(v, step2)
            done(v, "l2_sum", NQ - 1)
            v.wait_ge(S("a_out"), 16)
            v.tensor_copy(rows[:, 0:NB * HID], acc).then_inc(S("agg_made"), 1)
            link(v.tensor_tensor(h[:, :, :], over(vecs, VB2), per_row(cnt), ALU.mult))
            wait_next("proj_ps")
            link(v.tensor_tensor(h[:, :, :], h[:, :, :], split(acc[:, 0:NB * C], C), ALU.add))
            link(v.tensor_tensor(h[:, :, :], h[:, :, :], per_row(rdeg), ALU.mult))
            link(v.tensor_tensor(h[:, :, :], h[:, :, :], x[:, :, :], ALU.add))
            norm(x[:, :, :])
            v.memset(sq[:, 0:1], 0.0).then_inc(S("sums_free"), 1)

            def step3(q, s, i):
                onehot("l3", q, s)
            steps(v, step3)
            done(v, "l3_sum", NQ - 1)
            v.tensor_tensor(h[:, :, :], accb[:, :, 0:C], per_row(rdeg), ALU.mult).then_inc(S("agg_made"), 1)
            wait_next("proj_ps")
            v.wait_ge(S("x3_out"), 16)
            link(v.tensor_tensor(h[:, :, :], split(acc[:, 0:NB * C], C), x[:, :, :], ALU.add))
            norm(x[:, :, :])


_INS = ["x", "src", "dst", "edge_attr_16", "L0_gnn_Wq", "L0_gnn_bq", "L0_gnn_Wk", "L0_gnn_bk", "L0_gnn_Wv",
        "L0_gnn_bv", "L0_gnn_Wo", "L0_gnn_bo", "L0_gnn_pos_enc", "L1_gnn_W_l", "L1_gnn_b_l", "L1_gnn_W_r",
        "L1_gnn_b_r", "L1_gnn_W_e", "L1_gnn_att", "L1_gnn_bias", "L1_gnn_gamma", "L1_gnn_beta", "L2_gnn_W1",
        "L2_gnn_b1", "L2_gnn_W2", "L2_gnn_b2", "L3_gnn_w_neigh", "L3_gnn_w_self", "L3_gnn_b_self"]


def kernel(**inputs):
    import numpy as _np
    import concourse.bacc as _bacc
    from concourse import mybir as _mybir
    from concourse.bass_utils import run_bass_kernel_spmd as _run

    nc = _bacc.Bacc("TRN2", target_bir_lowering=False, num_devices=1)
    arrays, io = {}, {}
    for name in _INS:
        a = _np.ascontiguousarray(inputs[name])
        arrays[f"in_{name}_dram"] = a
        io[name] = nc.dram_tensor(f"in_{name}_dram", a.shape, _mybir.dt.from_np(a.dtype), kind="ExternalInput").ap()
    out = nc.dram_tensor("out_0_dram", (N, C), F32, kind="ExternalOutput").ap()
    build(nc, io, out)
    r = _run(nc, [arrays], core_ids=[0])
    return r.results[0]["out_0_dram"]
```

```python
import concourse.bass as bass
from concourse import mybir
from contextlib import ExitStack

F32 = mybir.dt.float32
BF16 = mybir.dt.bfloat16
I32 = mybir.dt.int32
ALU = mybir.AluOpType
ACT = mybir.ActivationFunctionType
AX = mybir.AxisListType

N = 2048
E = 65536
C = 64
P = 128
NB = N // P
G = 4
EC = G * P
NCH = E // EC
NQ = NCH + NB
NT = NQ + 4
KVOL = 125
NI = -(-N // KVOL)
H0, D0 = 4, 16
H1, D1 = 8, 8
ED = 16
HID = 128
NG = P // H1
KG = NQ * G // NG
TL = KG * P
IXQ = 4
POOL_TILES = {"l0": 4, "l1b": 2}
NW = 26
WHOLE_NUMBERS = 1.5 * 2 ** 23
BIG = 1e30
SLOTS = 2
GS = 4
PACK = GS + 3


def build(nc, io, out):
    ctx = ExitStack()
    with ctx:
        def sb(name, shape, dt=F32):
            return ctx.enter_context(nc.sbuf_tensor(name, shape, dt))

        sems = {}

        def S(name):
            if name not in sems:
                sems[name] = ctx.enter_context(nc.semaphore(name))
            return sems[name]

        xl_dram = nc.dram_tensor("xl_table", (N, C), F32, kind="Internal").ap()
        a_dram = nc.dram_tensor("a_table", (N, HID), F32, kind="Internal").ap()
        x3_dram = nc.dram_tensor("x3_table", (N, C), F32, kind="Internal").ap()
        ids_dram = nc.dram_tensor("step_ids", (NT, 3 * EC), BF16, kind="Internal").ap()
        spill_dram = nc.dram_tensor("xl_rows", (P, NCH, G * C), F32, kind="Internal").ap()

        ident = sb("ident", [P, P])
        ones = sb("ones", [P, P])
        zeros = sb("zeros", [1, 512])
        col_i = sb("col_i", [P, NT], I32)
        col_f = sb("col_f", [P, NT])
        col_b = sb("col_b", [P, P], BF16)
        part_i = sb("part_i", [P, 1], I32)
        part_f = sb("part_f", [P, 1])
        notfirst = sb("notfirst", [P, 1])
        gmask = sb("gmask", [G * ED, G])
        wq = sb("wq", [C + 1, C])
        wkv = sb("wkv", [C + 1, 2 * C])
        wo = sb("wo", [C, C])
        wraw = sb("wraw", [C, 4 * C])
        weraw = sb("weraw", [C, G * ED])
        wlr = sb("wlr", [C + 1, 2 * C])
        wns = sb("wns", [C + 1, 2 * C])
        w1a = sb("w1a", [C, HID])
        w1b = sb("w1b", [C + 1, HID])
        w2 = sb("w2", [HID, C])
        web = sb("web", [G * ED, G, C])
        pos = sb("pos", [KVOL, C])
        vecs = sb("vecs", [P, 6, C])
        VBO, VATT, VBIAS, VGAMMA, VBETA, VB2 = range(6)
        x = sb("x", [P, NB, C])
        h = sb("h", [P, NB, C])
        st1 = sb("st1", [P, NB])
        st2 = sb("st2", [P, NB])
        st3 = sb("st3", [P, NB])
        nrm = sb("nrm", [P, NB * H1])
        xT = sb("xT", [C + 1, N])
        tab3 = sb("tab3", [P, 3, NB * HID], BF16)
        cnt = sb("cnt", [P, NB])
        rdeg = sb("rdeg", [P, NB])
        kvn = sb("kvn", [NI, 2 * C])
        kvn3 = sb("kvn3", [NI, 3, 2 * C], BF16)
        kvs = sb("kvs", [3 * NI, 2 * C], BF16)
        dst4 = sb("dst4", [P, GS * G])
        mod_ni = sb("mod_ni", [3 * NI, 2])
        pos3 = sb("pos3", [KVOL, 3, C], BF16)
        blk = sb("blk", [P, 1], I32)
        qc = sb("qc", [P, 2])
        cqb = sb("cqb", [P, NT])
        bqb = sb("bqb", [P, NT])
        selF = sb("selF", [P, NT])
        begun = sb("begun", [P, NT])
        qcol = sb("qcol", [P, 4])
        btab = sb("btab", [P, NT], I32)
        bmin = sb("bmin", [1, NT + 1], I32)
        bpack = sb("bpack", [1, NQ - GS + 1], I32)
        ctab = sb("ctab", [P, NT], I32)
        srcI = sb("srcI", [P, (NCH + IXQ) * G], I32)
        qtab = sb("qtab", [1, NCH], I32)
        dstK = sb("dstK", [P, NT * G])
        dstL = sb("dstL", [P, NT * G])
        pen = sb("pen", [P, NT * G])
        idx = [sb(f"idx{s}", [P, IXQ * G], I32) for s in range(2)]
        idb = [sb(f"idb{s}", [P, EC], BF16) for s in range(GS)]
        ring = sb("ring", [P, GS * G * HID])
        gat = [ring[:, s * G * HID:(s + 1) * G * HID].rearrange("p (j c) -> p j c", j=G) for s in range(GS)]
        g64 = [gat[s][:, 0:G // 2, :].rearrange("p j c -> p (j c)") for s in range(GS)]
        oh = [sb(f"oh{s}", [P, G, P]) for s in range(SLOTS)]
        ohT = [sb(f"ohT{s}", [P, 3 * EC], BF16) for s in range(SLOTS)]
        pay = [sb(f"pay{s}", [P, G, HID]) for s in range(SLOTS)]
        pay3 = [sb(f"pay3{s}", [P, 3, G, C + H1], BF16) for s in range(GS)]
        ohb = [oh[s % SLOTS][:, (s // SLOTS) * 2:(s // SLOTS) * 2 + G // 2, :].bitcast(BF16)
               .rearrange("p a (b n) -> p (a b) n", n=P) for s in range(GS)]
        rest = [sb(f"rest{s}", [P, G, C + H1]) for s in range(SLOTS)]
        prod = sb("prod", [P, G * HID])
        lky = sb("lky", [P, G * C])
        wgt = sb("wgt", [P, G * C])
        attn = sb("attn", [P, G * H0])
        atr = [sb(f"atr{s}", [P, G * ED]) for s in range(GS)]
        atT = [sb(f"atT{s}", [G * ED, P]) for s in range(SLOTS)]
        lg = sb("lg", [P, NQ * G * H1])
        lgT = sb("lgT", [P, TL])
        keyT = sb("keyT", [P, TL])
        brk = sb("brk", [P, TL + 1])
        run = sb("run", [P, TL])
        dst_i, src_i = (run[:, k * EC:(k + 1) * EC].bitcast(I32) for k in range(2))
        dst_f, src_f, k_f, i_f = (keyT[:, k * EC:(k + 1) * EC] for k in range(4))
        idrow = [lgT[:, k * 3 * EC // 2:(k + 1) * 3 * EC // 2].bitcast(BF16) for k in range(2)]
        idb0 = [lgT[:, (2 + k) * 3 * EC // 2:(3 + k) * 3 * EC // 2].bitcast(BF16) for k in range(GS)]
        tab = brk[:, 0:NB * HID]
        sq = lg[:, 0:NB * HID]
        aggT = run[:, 0:N]
        rows = keyT[:, 0:NB * HID]
        ends = sb("ends", [P, 4])
        crow = sb("crow", [1, 12, P])
        carry = sb("carry", [P, 2])

        ps = ctx.enter_context(nc.psum_tensor("ps", [P, 8, 512], F32))
        acc = ps[:, 0:4, :].rearrange("p a b -> p (a b)")
        top = ps[:, 4:8, :].rearrange("p a b -> p (a b)")
        kv = [ps[:, 4 + s, :] for s in range(SLOTS)]
        ga = [ps[:, 6 + s, :] for s in range(SLOTS)]

        halves = ((0, P), (P, NT - P))

        def split(ap, width):
            return ap.rearrange("p (b c) -> p b c", c=width)

        def done(eng, name, m):
            if isinstance(m, int) and m < 0:
                return
            eng.wait_ge(S(name), m + 1)

        def steps(eng, body):
            for s in range(GS):
                body(s, s, 0)
            with eng.Fori(1, NQ // GS) as i:
                for s in range(GS):
                    body(i * GS + s, s, i)

        def first(q):
            return isinstance(q, int) and q == 0

        def counted(eng):
            seen = {}

            def wait_next(name):
                seen[name] = seen.get(name, 0) + 1
                eng.wait_ge(S(name), seen[name])
            return wait_next

        block = ctx.enter_context(nc.Block())

        @block.sync
        def _(sp):
            wait_next = counted(sp)

            def load(dst, src, name):
                sp.dma_start(dst, src).then_inc(S(name), 16)

            load(dst_i[:, :], io["dst"].rearrange("(c e) -> c e", e=EC), "dst_in")
            load(src_i[:, :], io["src"].rearrange("(c e) -> c e", e=EC), "src_in")
            load(x[:, :, :], io["x"].rearrange("(b p) c -> p b c", p=P), "x_in")
            weights = [
                (wq[0:C, :], io["L0_gnn_Wq"]), (wq[C:C + 1, :], io["L0_gnn_bq"][None, :]),
                (wkv[0:C, 0:C], io["L0_gnn_Wk"]), (wkv[0:C, C:2 * C], io["L0_gnn_Wv"]),
                (wkv[C:C + 1, 0:C], io["L0_gnn_bk"][None, :]), (wkv[C:C + 1, C:2 * C], io["L0_gnn_bv"][None, :]),
                (wo[:, :], io["L0_gnn_Wo"]), (pos[:, :], io["L0_gnn_pos_enc"].rearrange("k h d -> k (h d)")),
                (wraw[:, 0:C], io["L1_gnn_W_l"]), (wraw[:, C:2 * C], io["L1_gnn_W_r"]),
                (wraw[:, 2 * C:3 * C], io["L3_gnn_w_neigh"]), (wraw[:, 3 * C:4 * C], io["L3_gnn_w_self"]),
                (split(weraw[:, :], ED), io["L1_gnn_W_e"][:, None, :].to_broadcast([C, G, ED])), (wlr[C:C + 1, 0:C], io["L1_gnn_b_l"][None, :]),
                (wlr[C:C + 1, C:2 * C], io["L1_gnn_b_r"][None, :]),
                (wns[C:C + 1, C:2 * C], io["L3_gnn_b_self"][None, :]),
                (w1a[:, :], io["L2_gnn_W1"][0:C, :]), (w1b[0:C, :], io["L2_gnn_W1"][C:2 * C, :]),
                (w1b[C:C + 1, :], io["L2_gnn_b1"][None, :]), (w2[:, :], io["L2_gnn_W2"])]
            spread = [io["L0_gnn_bo"], io["L1_gnn_att"].rearrange("a h c -> (a h c)"), io["L1_gnn_bias"],
                      io["L1_gnn_gamma"], io["L1_gnn_beta"], io["L2_gnn_b2"]]
            weights += [(vecs[:, i, :], v[None, :].to_broadcast([P, C])) for i, v in enumerate(spread)]
            assert len(weights) == NW
            for dst, src in weights:
                load(dst, src, "w_in")

            def bring_ids(layer, q, s, dst, width):
                done(sp, f"{layer}_ohT", q - GS)
                load(dst, ids_dram[bass.ds(q, 1), 0:width].to_broadcast([P, width]), f"{layer}_ids{s}")

            wait_next("idrow_made")
            load(ids_dram[0:P, :], idrow[0], "ids_out")
            load(ids_dram[P:NT, :], idrow[1][0:NT - P, :], "ids_out")
            sp.wait_ge(S("ids_out"), 32)
            wait_next("kvn_made")
            for k in range(3):
                load(kvs[k * NI:(k + 1) * NI, :], kvn3[:, k, :], "kvs_in")
            steps(sp, lambda q, s, i: bring_ids("l0", q, s, idb0[s], 3 * EC))
            for s in range(2):
                bring_ids("l0", NQ + s, s, idb0[s], 3 * EC)

            wait_next("xl_made")
            load(xl_dram.rearrange("(b p) c -> p b c", p=P), split(rows[:, 0:NB * C], C), "xl_out")

            wait_next("steps_made")

            def chunks(body):
                for s in range(GS):
                    body(s, s, 0)
                with sp.Fori(1, NCH // GS) as i:
                    for s in range(GS):
                        body(i * GS + s, s, i)

            def arrived(layer, s, i):
                sp.wait_ge(S(f"{layer}_rows{s}"), i * 16 * G + 16 * G)
                sp.sem_inc(S(f"{layer}_here"), 1)

            def keep(c, s, i):
                arrived("l1", s, i)
                load(spill_dram[:, bass.ds(c, 1), :].rearrange("p o c -> p (o c)"), g64[s], f"l1_spill{s}")

            chunks(keep)
            for s in range(GS):
                sp.wait_ge(S(f"l1_spill{s}"), 16 * NCH // GS)
            wait_next("l1_logits")

            def respill(q, s, i):
                c = sp.value_load(ctab[0:1, bass.ds(q, 1)], min_val=0, max_val=NCH - 1)
                done(sp, "l1b_pay", q - GS)
                load(g64[s], spill_dram[:, bass.ds(c, 1), :].rearrange("p o c -> p (o c)"), f"l1b_rows{s}")

            steps(sp, respill)

            wait_next("a_made")
            load(a_dram.rearrange("(b p) c -> p b c", p=P), split(rows[:, 0:NB * HID], HID), "a_out")
            chunks(lambda c, s, i: arrived("l2", s, i))
            for _ in range(3):
                wait_next("x_made")
            load(x3_dram.rearrange("(b p) c -> p b c", p=P), x[:, :, :], "x3_out")
            chunks(lambda c, s, i: arrived("l3", s, i))
            wait_next("x_made")
            load(out.rearrange("(b p) c -> p b c", p=P), x[:, :, :], "result_out")
            for name, n in (("result_out", 1), ("ids_out", 2), ("xl_out", 1), ("a_out", 1), ("x3_out", 1)):
                sp.wait_ge(S(name), 16 * n)

        @block.gpsimd
        def _(pool):
            wait_next = counted(pool)
            pool.iota(col_i[:, :], pattern=[[1, NT]], base=0, channel_multiplier=0).then_inc(S("iota"), 1)
            pool.iota(part_i[:, :], pattern=[[0, 1]], base=0, channel_multiplier=1).then_inc(S("iota"), 1)
            pool.memset(ident[:, :], 0.0).then_inc(S("pool_set"), 1)
            pool.memset(gmask[:, :], 1.0).then_inc(S("pool_set"), 1)
            pool.wait_ge(S("pool_set"), 2)
            pool.affine_select(out=ident[:, :], in_=ident[:, :], compare_op=ALU.not_equal, fill=1.0, base=0,
                               pattern=[[-1, P]], channel_multiplier=1).then_inc(S("ident"), 1)
            pool.affine_select(out=gmask[:, :], in_=gmask[:, :], compare_op=ALU.is_ge, fill=0.0, base=0,
                               pattern=[[-ED, G]], channel_multiplier=1).then_inc(S("pool_set"), 1)
            pool.wait_ge(S("pool_set"), 3)
            pool.affine_select(out=gmask[:, :], in_=gmask[:, :], compare_op=ALU.is_ge, fill=0.0, base=ED - 1,
                               pattern=[[ED, G]], channel_multiplier=-1).then_inc(S("gmask"), 1)

            def gather(layer, table, dst, used):
                def turn(t):
                    for u in range(2):
                        for r in range(IXQ):
                            c = (2 * t + u) * IXQ + r
                            early = isinstance(c, int) and c < GS
                            if r == 0:
                                pool.wait_ge(S(f"{layer}_idx"), 2 * t + u + 1)
                            if r == IXQ - 1:
                                if not early:
                                    for z in range(GS):
                                        pool.wait_ge(S(f"{layer}_rows{z}"), (2 * t + u) * (16 * G * IXQ // GS))
                                pool.tensor_copy(idx[1 - u][:, :],
                                                 srcI[:, bass.ds(((2 * t + u) + 1) * IXQ * G, IXQ * G)]) \
                                    .then_inc(S(f"{layer}_idx"), 1)
                            if not early:
                                first = pool.value_load(qtab[0:1, bass.ds(c - GS + 1, 1)], min_val=1, max_val=NQ)
                                pool.wait_ge(S(used), first)
                                if layer == "l1":
                                    pool.wait_ge(S(f"l1_spill{r}"), (2 * t + u) * 16)
                            pool.nop(nofuse=True)
                            for j in range(G):
                                pool.indirect_dma_start(dst(r, j), None, table[:, :],
                                                        bass.IndirectOffsetOnAxis(
                                                            idx[u][:, r * G + j:r * G + j + 1], 0)) \
                                    .then_inc(S(f"{layer}_rows{r}"), 16)
                if layer != "l1":
                    last = f"l{int(layer[1]) - 1}"
                    pool.wait_ge(S(f"{last}_idx"), NCH // IXQ + 1)
                pool.tensor_copy(idx[0][:, :], srcI[:, 0:IXQ * G]).then_inc(S(f"{layer}_idx"), 1)
                turn(0)
                with pool.Fori(1, NCH // (2 * IXQ)) as t:
                    turn(t)

            def onehots(layer):
                def step(q, s, i):
                    if s == 0:
                        done(pool, f"{layer}_oh", q - 1)
                        pool.tensor_copy(dst4[:, :], dstL[:, bass.ds(q * G, GS * G)]).then_inc(S(f"{layer}_dst4"), 1)
                        pool.wait_ge(S(f"{layer}_dst4"), i + 1)
                    done(pool, f"{layer}_sum", q - GS)
                    pool.nop(nofuse=True)
                    for j in range(POOL_TILES[layer]):
                        last = pool.tensor_scalar(ohb[s % GS][:, j, :], col_f[:, 0:P],
                                                  dst4[:, s * G + j:s * G + j + 1], None, ALU.is_equal)
                    last.then_inc(S(f"{layer}_oh"), 1)
                steps(pool, step)

            def wide(s, j):
                return gat[s][:, j, :]

            def slim(s, j):
                return g64[s][:, j * C:(j + 1) * C]

            wait_next("steps_made")
            onehots("l0")
            pool.wait_ge(S("xl_out"), 16)
            gather("l1", xl_dram, slim, "l1_z")
            onehots("l1b")
            pool.wait_ge(S("a_out"), 16)
            gather("l2", a_dram, wide, "l2_z")
            pool.wait_ge(S("x3_out"), 16)
            gather("l3", x3_dram, slim, "l3_sum")

        @block.tensor
        def _(pe):
            wait_next = counted(pe)

            def transpose_nodes(src, width, made):
                for b in range(NB):
                    last = pe.transpose(top[0:width, b * P:(b + 1) * P], src(b), ident[:, :])
                last.then_inc(S(made), 1)

            def project(dst, lhs, weight, width, name=None, start=True, stop=True):
                for b in range(NB):
                    last = pe.matmul(dst(b), lhs[:, b * P:(b + 1) * P], weight, start=start, stop=stop,
                                     skip_group_check=True)
                if name:
                    last.then_inc(S(name), 1)

            def zero_sums():
                wait_next("sums_free")
                for k in range(4):
                    pe.matmul(ps[:, k, :], zeros[0:1, 0:P], zeros[0:1, :], start=True, stop=True,
                              skip_group_check=True)

            def block_of(q):
                return pe.value_load(btab[0:1, bass.ds(q, 1)], min_val=0, max_val=NB - 1)

            def blocks_ahead(known, q, s, a, n):
                if s == 0:
                    packed = pe.value_load(bpack[0:1, bass.ds(q, 1)], min_val=0, max_val=NB ** PACK - 1)
                    for r in range(a, GS - 1 + n + 1):
                        known[r] = pe.snap(packed // NB ** (r + 1) % NB)

            def take_targets(layer, q, s, width, used, b=None):
                b = block_of(q) if b is None else b
                done(pe, f"{layer}_ohT", q)
                done(pe, used, q - SLOTS)
                for j in range(G):
                    for part in range(3):
                        last = pe.matmul(ga[s % SLOTS][:, j * width:(j + 1) * width],
                                         ohT[s % SLOTS][:, j * P:(j + 1) * P],
                                         tab3[:, part, bass.ds(b * width, width)], start=part == 0, stop=part == 2)
                last.then_inc(S(f"{layer}_ga"), 1)

            def sum_rows(layer, q, s, rhs, width, wait_rows):
                b = block_of(q)
                wait_rows()
                done(pe, f"{layer}_oh", q)
                for j in range(G):
                    last = pe.matmul(acc[:, bass.ds(b * P, width)], oh[s % SLOTS][:, j, :], rhs(s, j),
                                     start=False, stop=True, skip_group_check=True)
                last.then_inc(S(f"{layer}_sum"), 1)

            def sum_thirds(layer, q, s, width, b=None):
                b = block_of(q) if b is None else b
                done(pe, f"{layer}_lo", q)
                done(pe, f"{layer}_oh", q)
                if POOL_TILES[layer] < G:
                    done(pe, f"{layer}_ohv", q)
                for j in range(G):
                    for part in range(3):
                        last = pe.matmul(acc[:, bass.ds(b * P, width)], ohb[s % GS][:, j, :],
                                         pay3[s % GS][:, part, j, 0:width], start=False, stop=True,
                                         skip_group_check=True)
                last.then_inc(S(f"{layer}_sum"), 1)

            wait_next("begun_made")
            pe.matmul(ps[:, 0, 0:NT], ones[:, :], begun[:, :], start=True, stop=True)
            for k, (a, n) in enumerate(halves):
                last = pe.matmul(ps[0:n, 1, k:k + 1], begun[:, a:a + n], ones[:, 0:1], start=True, stop=True)
            last.then_inc(S("begun_ps"), 1)
            wait_next("sel_made")
            wait_next("ident")
            pe.matmul(ps[0:1, 2, 0:NCH], qc[:, 1:2], ident[:, :], start=True, stop=True)
            for j in range(G):
                pe.transpose(ps[:, j // 4, j * P:(j + 1) * P], src_f[:, j * P:(j + 1) * P], ident[:, :])
                last = pe.matmul(ps[:, G + j, 0:NT], dst_f[:, j * P:(j + 1) * P], selF[:, :], start=True, stop=True)
            last.then_inc(S("ids_ps"), 1)
            wait_next("steps_made")
            for k, (a, n) in enumerate(halves):
                for r, ids in enumerate((dst_f, k_f, i_f)):
                    last = pe.matmul(ps[0:n, 3 * k + r, :], selF[:, a:a + n], ids, start=True, stop=True)
            last.then_inc(S("idrow_ps"), 1)
            wait_next("idrow_made")
            pe.wait_ge(S("w_in"), 16 * NW)
            pe.wait_ge(S("x_in"), 16)
            for k in range(4):
                pe.transpose(ps[0:C, 0, k * C:(k + 1) * C], wraw[:, k * C:(k + 1) * C], ident[0:C, 0:C])
            pe.matmul(ps[0:G * ED, 1, 0:C], weraw[:, :], ident[0:C, 0:C],
                      start=True, stop=True).then_inc(S("wt_ps"), 1)
            transpose_nodes(lambda b: x[:, b, :], C, "xT_ps")

            wait_next("wt_made")
            wait_next("xT_made")
            project(lambda b: acc[:, b * C:(b + 1) * C], xT, wq[:, :], C)
            pe.matmul(ps[0:NI, 2, 0:2 * C], xT[:, 0:NI], wkv[:, :], start=True, stop=True).then_inc(S("qkv_ps"), 1)
            wait_next("tables_made")
            zero_sums()

            def take_sources(q, s):
                done(pe, "l0_ohT", q)
                done(pe, "l0_kv", q - SLOTS)
                for j in range(G):
                    o = kv[s % SLOTS][:, j * HID:(j + 1) * HID]
                    pe.matmul(o, ohT[s % SLOTS][0:3 * NI, 2 * EC + j * P:2 * EC + (j + 1) * P], kvs[:, :],
                              start=True, stop=False, skip_group_check=True)
                    for part in range(3):
                        last = pe.matmul(o[:, 0:C], ohT[s % SLOTS][0:KVOL, EC + j * P:EC + (j + 1) * P],
                                         pos3[:, part, :], start=False, stop=part == 2, skip_group_check=True)
                last.then_inc(S("l0_src"), 1)
            pe.wait_ge(S("kvs_in"), 48)
            for q in range(2):
                take_targets("l0", q, q, C, "l0_prod")
                take_sources(q, q)

            known = {}

            def step0(q, s, i):
                blocks_ahead(known, q, s, -1, 2)
                take_targets("l0", q + 2, (s + 2) % GS, C, "l0_prod", known[s + 2])
                take_sources(q + 2, (s + 2) % GS)
                if not first(q):
                    sum_thirds("l0", q - 1, s - 1, C + 1, known[s - 1])
            steps(pe, step0)
            sum_thirds("l0", NQ - 1, GS - 1, C + 1)
            done(pe, "l0_kv", NQ + 1)
            wait_next("agg_made")
            transpose_nodes(lambda b: h[:, b, :], C, "aggT_ps")
            wait_next("aggT_made")
            project(lambda b: acc[:, b * C:(b + 1) * C], aggT[0:C, :], wo[:, :], C, "proj_ps")

            wait_next("x_made")
            transpose_nodes(lambda b: x[:, b, :], C, "xT_ps")
            wait_next("xT_made")
            project(lambda b: acc[:, b * P:(b + 1) * P], xT, wlr[:, :], P, "proj_ps")

            def take1(q, s, i):
                pe.wait_ge(S(f"l1_attr{s}"), i * 16 + 16)
                done(pe, "l1_z", q - SLOTS)
                pe.nop(nofuse=True)
                pe.transpose(ga[s % SLOTS][0:G * ED, 2 * P:3 * P], atr[s][:, :], ident[:, :]).then_inc(S("l1_tr"), 1)
                b = block_of(q)
                done(pe, "l1_atT", q)
                pe.matmul(ga[s % SLOTS][:, 0:G * C], atT[s % SLOTS][:, :], web[:, :, :].rearrange("p j c -> p (j c)"),
                          start=True, stop=False, skip_group_check=True)
                done(pe, "l1_ohT", q)
                for j in range(G):
                    for part in range(3):
                        last = pe.matmul(ga[s % SLOTS][:, j * C:(j + 1) * C],
                                         ohT[s % SLOTS][:, j * P:(j + 1) * P], tab3[:, part, bass.ds(b * C, C)],
                                         start=False, stop=j == G - 1 and part == 2, skip_group_check=True)
                last.then_inc(S("l1_ga"), 1)

            def step1(q, s, i):
                take1(q + 1, (s + 1) % GS, i + (s + 1) // GS)
            wait_next("xr_made")
            take1(0, 0, 0)
            steps(pe, step1)

            wait_next("l1_logits")
            bank = 0
            for by_tile in (brk, run):
                for k in range(0, KG, 4):
                    done(pe, "bank_out", bank - 8)
                    for j in range(4):
                        last = pe.transpose(ps[:, bank % 8, j * P:(j + 1) * P], by_tile[:, (k + j) * P:(k + j + 1) * P],
                                            ident[:, :])
                    last.then_inc(S("bank_in"), 1)
                    bank += 1
            wait_next("ends_made")
            done(pe, "bank_out", bank - 1)
            for k in range(4):
                last = pe.matmul(ps[0:1, k, 0:P], ends[:, k:k + 1], ident[:, :], start=True, stop=True)
            last.then_inc(S("ends_ps"), 1)
            wait_next("carry_made")
            for k in range(2):
                last = pe.matmul(ps[:, 4 + k, 0:1], crow[0:1, 10 + k, :], ones[0:1, 0:1], start=True, stop=True)
            last.then_inc(S("carry_ps"), 1)
            wait_next("ex_made")
            for n, k in enumerate(range(0, KG, 4)):
                done(pe, "ex_out", n - 8)
                for j in range(4):
                    last = pe.transpose(ps[:, n % 8, j * P:(j + 1) * P], lgT[:, (k + j) * P:(k + j + 1) * P],
                                        ident[:, :])
                last.then_inc(S("ex_in"), 1)
            done(pe, "ex_out", KG // 4 - 1)
            zero_sums()

            def step1b(q, s, i):
                blocks_ahead(known, q, s, -1, 0)
                if not first(q):
                    sum_thirds("l1b", q - 1, s - 1, C + H1, known[s - 1])
            steps(pe, step1b)
            sum_thirds("l1b", NQ - 1, GS - 1, C + H1)

            wait_next("x_made")
            transpose_nodes(lambda b: x[:, b, :], C, "xT_ps")
            wait_next("xT_made")
            project(lambda b: acc[:, b * P:(b + 1) * P], xT[0:C, :], w1a[:, :], P)
            project(lambda b: top[:, b * P:(b + 1) * P], xT, w1b[:, :], P, "proj_ps")
            zero_sums()
            take_targets("l2", 0, 0, HID, "l2_z")

            def step2(q, s, i):
                take_targets("l2", q + 1, (s + 1) % GS, HID, "l2_z")
                sum_rows("l2", q, s, lambda s, j: pay[s % SLOTS][:, j, :], HID, lambda: done(pe, "l2_relu", q))
            steps(pe, step2)
            wait_next("agg_made")
            transpose_nodes(lambda b: rows[:, b * P:(b + 1) * P], HID, "aggT_ps")
            wait_next("aggT_made")
            project(lambda b: acc[:, b * C:(b + 1) * C], aggT, w2[:, :], C, "proj_ps")

            wait_next("x_made")
            transpose_nodes(lambda b: x[:, b, :], C, "xT_ps")
            zero_sums()

            def step3(q, s, i):
                c = pe.value_load(ctab[0:1, bass.ds(q, 1)], min_val=0, max_val=NCH - 1)
                sum_rows("l3", q, s, lambda s, j: ring[:, bass.ds(c % GS * (G * HID) + j * C, C)], C,
                         lambda: pe.wait_ge(S("l3_here"), c + 1))
            steps(pe, step3)
            wait_next("xT_made")
            wait_next("agg_made")
            transpose_nodes(lambda b: h[:, b, :], C, "aggT_ps")
            wait_next("aggT_made")
            for b in range(NB):
                pe.matmul(acc[:, b * C:(b + 1) * C], aggT[0:C, b * P:(b + 1) * P], wns[0:C, 0:C],
                          start=True, stop=False, skip_group_check=True)
                last = pe.matmul(acc[:, b * C:(b + 1) * C], xT[:, b * P:(b + 1) * P], wns[:, C:2 * C],
                                 start=False, stop=True, skip_group_check=True)
            last.then_inc(S("proj_ps"), 1)

        @block.scalar
        def _(act):
            wait_next = counted(act)

            def copy_banks(dst, width, ready, made):
                wait_next(ready)
                for k in range(4):
                    last = act.activation(dst[0:width, k * 512:(k + 1) * 512], ps[0:width, 4 + k, :], ACT.Copy)
                last.then_inc(S(made), 1)

            def split_rows(layer, q, s, width):
                done(act, f"{layer}_pay", q)
                done(act, f"{layer}_sum", q - GS)
                act.activation(pay3[s % GS][:, 0, :, 0:width], pay[s % SLOTS][:, :, 0:width], ACT.Copy) \
                    .then_inc(S(f"{layer}_hi"), 1)
                done(act, f"{layer}_rest", q)
                act.activation(pay3[s % GS][:, 1, :, 0:width], rest[s % SLOTS][:, :, 0:width], ACT.Copy) \
                    .then_inc(S(f"{layer}_mid"), 1)

            def bring_ids(layer, q, s):
                done(act, f"{layer}_ohT", q - GS)
                act.dma_start(idb[s % GS][:, :], ids_dram[bass.ds(q, 1), 0:EC].to_broadcast([P, EC])) \
                    .then_inc(S(f"{layer}_ids{s % GS}"), 16)

            attrs_dram = io["edge_attr_16"].rearrange("(c j p) k -> p c j k", j=G, p=P)

            def bring_attrs(q, s):
                c = act.value_load(ctab[0:1, bass.ds(q, 1)], min_val=0, max_val=NCH - 1)
                done(act, "l1_tr", q - GS)
                act.dma_start(atr[s % GS].ap().rearrange("p (o j k) -> p o j k", o=1, j=G),
                              attrs_dram[:, bass.ds(c, 1), :, :]).then_inc(S(f"l1_attr{s % GS}"), 16)

            AHEAD = GS - 1

            def root(dst, src):
                wait_next("square_sum")
                act.activation(dst, src, ACT.Sqrt).then_inc(S("root"), 1)

            copy_banks(xT, C, "xT_ps", "xT_made")
            root(nrm[:, 0:NB * H0], nrm[:, 0:NB * H0])
            root(nrm[0:NI, 0:H0], nrm[0:NI, 0:H0])
            root(nrm[0:KVOL, 0:H0], nrm[0:KVOL, 0:H0])

            def keys_values(q, s, i):
                s = q % GS if s is None else s
                done(act, "l0_src", q)
                done(act, "l0_pay", q - GS)
                act.activation(gat[s % GS], kv[s % SLOTS].rearrange("p (j c) -> p j c", j=G), ACT.Copy) \
                    .then_inc(S("l0_kv"), 1)
                if not first(q) and i is not None:
                    split_rows("l0", q - 1, s - 1, C)
            steps(act, keys_values)
            keys_values(NQ, GS, NQ // GS)
            keys_values(NQ + 1, None, None)
            copy_banks(aggT, C, "aggT_ps", "aggT_made")
            root(st2[:, :], st2[:, :])
            copy_banks(xT, C, "xT_ps", "xT_made")

            wait_next("steps_made")
            for q in range(AHEAD):
                bring_ids("l1", q, q)
                bring_attrs(q, q)

            def attrs(q, s, i):
                if s < GS:
                    bring_ids("l1", q + AHEAD, s + AHEAD)
                    bring_attrs(q + AHEAD, s + AHEAD)
                done(act, "l1_tr", q)
                done(act, "l1_ga", q - SLOTS)
                act.activation(atT[s % SLOTS][:, :], ga[s % SLOTS][0:G * ED, 2 * P:3 * P], ACT.Copy).then_inc(S("l1_atT"), 1)
            steps(act, attrs)
            attrs(NQ, GS, NQ // GS)
            for s in range(1, AHEAD):
                act.wait_ge(S(f"l1_ids{s}"), 16 * NQ // GS + 16)
                act.wait_ge(S(f"l1_attr{s}"), 16 * NQ // GS + 16)
            bank = 0
            for dst in (keyT, lgT):
                for k in range(0, KG, 4):
                    done(act, "bank_in", bank)
                    act.activation(dst[:, k * P:(k + 4) * P], ps[:, bank % 8, :], ACT.Copy) \
                        .then_inc(S("bank_out"), 1)
                    bank += 1
            wait_next("shift_made")
            act.activation(lgT[:, :], lgT[:, :], ACT.Exp).then_inc(S("ex_made"), 1)
            for n, k in enumerate(range(0, KG, 4)):
                done(act, "ex_in", n)
                act.activation(lg[:, :].rearrange("p (g k h) -> p k g h", g=NG, h=H1)[:, k:k + 4, :, :],
                               ps[:, n % 8, :].rearrange("p (k g h) -> p k g h", k=4, h=H1), ACT.Copy) \
                    .then_inc(S("ex_out"), 1)
            def thirds1(q, s, i):
                if not first(q):
                    split_rows("l1b", q - 1, s - 1, C + H1)
            steps(act, thirds1)
            thirds1(NQ, GS, NQ // GS)
            root(st2[:, :], st2[:, :])
            root(st2[:, :], st2[:, :])
            copy_banks(xT, C, "xT_ps", "xT_made")

            for q in range(AHEAD):
                bring_ids("l2", q, q)

            def relu(q, s, i):
                bring_ids("l2", q + AHEAD, s + AHEAD)
                done(act, "l2_z", q)
                act.activation(pay[s % SLOTS][:, :, :], pay[s % SLOTS][:, :, :], ACT.Relu) \
                    .then_inc(S("l2_relu"), 1)
            steps(act, relu)
            for s in range(1, AHEAD):
                act.wait_ge(S(f"l2_ids{s}"), 16 * NQ // GS + 16)
            copy_banks(aggT, HID, "aggT_ps", "aggT_made")
            root(st2[:, :], st2[:, :])
            copy_banks(xT, C, "xT_ps", "xT_made")
            copy_banks(aggT, C, "aggT_ps", "aggT_made")
            root(st2[:, :], st2[:, :])

        @block.vector
        def _(v):
            wait_next = counted(v)
            chain = [0]

            def link(ins):
                chain[0] += 1
                ins.then_inc(S("vector_chain"), 1)
                v.wait_ge(S("vector_chain"), chain[0])

            def over(vec, k):
                return vec[:, k:k + 1, :].to_broadcast([P, NB, C])

            def per_row(t, width=C):
                return t[:, :, None].to_broadcast([P, NB, width])

            v.memset(ones[:, :], 1.0)
            v.memset(zeros[:, :], 0.0)
            for w in (xT[C:C + 1, :],):
                v.memset(w, 1.0)
            for s in range(GS):
                v.memset(pay3[s][:, 0, :, C:C + 1], 1.0)
                v.memset(pay3[s][:, 1:3, :, C:C + 1], 0.0)
            v.wait_ge(S("iota"), 2)
            v.tensor_copy(col_f[:, :], col_i[:, :])
            v.tensor_copy(col_b[:, :], col_i[:, 0:P])
            link(v.tensor_copy(part_f[:, :], part_i[:, :]))
            link(v.tensor_single_scalar(notfirst[:, :], part_f[:, :], 0.0, op=ALU.is_gt))
            v.wait_ge(S("dst_in"), 16)
            link(v.tensor_single_scalar(blk[:, :], dst_i[:, 0:1], 7, op=ALU.arith_shift_right))
            link(v.tensor_copy(qc[:, 0:1], blk[:, :]))
            link(v.scalar_tensor_tensor(out=qc[:, 1:2], in0=qc[:, 0:1], scalar=notfirst[:, 0:1],
                                        in1=part_f[:, :], op0=ALU.mult, op1=ALU.add))
            v.tensor_scalar(begun[:, :], col_f[:, :], qc[:, 1:2], None, ALU.is_ge).then_inc(S("begun_made"), 1)
            v.tensor_copy(dst_f, dst_i)
            v.wait_ge(S("src_in"), 16)
            link(v.tensor_copy(src_f, src_i))
            link(v.tensor_scalar(i_f, src_f, 1.0 / KVOL, -(KVOL // 2) / KVOL, ALU.mult, ALU.add))
            link(v.tensor_single_scalar(i_f, i_f, WHOLE_NUMBERS, op=ALU.add))
            link(v.tensor_single_scalar(i_f, i_f, WHOLE_NUMBERS, op=ALU.subtract))
            v.scalar_tensor_tensor(out=k_f, in0=i_f, scalar=-float(KVOL), in1=src_f, op0=ALU.mult, op1=ALU.add)
            wait_next("begun_ps")
            link(v.tensor_scalar(cqb[:, :], ps[:, 0, 0:NT], -1.0, None, ALU.add))
            v.tensor_copy(ctab[:, :], cqb[:, :])
            link(v.tensor_tensor(bqb[:, :], col_f[:, :], cqb[:, :], ALU.subtract))
            v.tensor_scalar(btab[:, :], bqb[:, :], float(NB - 1), None, ALU.min)
            v.memset(bmin[:, 0:1], 0)
            link(v.tensor_scalar(bmin[:, 1:NT + 1], bqb[0:1, :], float(NB - 1), None, ALU.min))
            link(v.tensor_copy(bpack[:, :], bmin[:, PACK - 1:PACK + NQ - GS]))
            for r in reversed(range(PACK - 1)):
                link(v.tensor_single_scalar(bpack[:, :], bpack[:, :], NB.bit_length() - 1, op=ALU.arith_shift_left))
                link(v.tensor_tensor(bpack[:, :], bpack[:, :], bmin[:, r:r + NQ - GS + 1], ALU.bitwise_or))
            link(v.tensor_scalar(bqb[:, :], bqb[:, :], float(P), None, ALU.mult))
            for k, (a, n) in enumerate(halves):
                last = v.tensor_scalar(qcol[0:n, k:k + 1], part_f[0:n, :], float(a + 1), None, ALU.add)
            link(last)
            for k, (a, n) in enumerate(halves):
                last = v.tensor_tensor(qcol[0:n, 2 + k:3 + k], qcol[0:n, k:k + 1], ps[0:n, 1, k:k + 1], ALU.subtract)
            link(last)
            v.tensor_scalar(selF[:, :], cqb[:, :], part_f[:, 0:1], None, ALU.is_equal).then_inc(S("sel_made"), 1)
            link(v.tensor_scalar(qcol[:, 0:1], qcol[:, 2:3], float(P), None, ALU.mult))
            link(v.tensor_scalar(qcol[0:NT - P, 1:2], qcol[0:NT - P, 3:4], float(P), None, ALU.mult))
            wait_next("ids_ps")
            for j in range(G):
                v.tensor_copy(split(srcI[:, 0:NCH * G], G)[:, :, j], ps[:, 0, j * P:(j + 1) * P])
                last = v.tensor_copy(split(dstK[:, :], G)[:, :, j], ps[:, G + j, 0:NT])
            link(last)
            link(v.tensor_tensor(split(dstL[:, :], G), split(dstK[:, :], G),
                                 bqb[:, :, None].to_broadcast([P, NT, G]), ALU.subtract))
            v.memset(srcI[:, NCH * G:(NCH + IXQ) * G], 0)
            v.tensor_copy(qtab[:, :], ps[0:1, 2, 0:NCH])
            link(v.tensor_scalar(mod_ni[:, 0:1], part_f[0:3 * NI, :], float(NI), -float(NI), ALU.is_ge, ALU.mult))
            link(v.tensor_scalar(mod_ni[:, 1:2], part_f[0:3 * NI, :], 2.0 * NI, -float(NI), ALU.is_ge, ALU.mult))
            link(v.tensor_tensor(mod_ni[:, 0:1], mod_ni[:, 0:1], mod_ni[:, 1:2], ALU.add))
            link(v.tensor_tensor(mod_ni[:, 0:1], mod_ni[:, 0:1], part_f[0:3 * NI, :], ALU.add))
            v.tensor_single_scalar(pen[:, :], dstL[:, :], 0.0, op=ALU.is_ge)
            link(v.tensor_single_scalar(prod[:, 0:0 + 512], dstL[:, 0:512], float(P), op=ALU.is_lt))
            link(v.tensor_tensor(pen[:, 0:512], pen[:, 0:512], prod[:, 0:512], ALU.mult))
            more = NT * G - 512
            link(v.tensor_single_scalar(prod[:, 0:more], dstL[:, 512:NT * G], float(P), op=ALU.is_lt))
            link(v.tensor_tensor(pen[:, 512:NT * G], pen[:, 512:NT * G], prod[:, 0:more], ALU.mult))
            v.tensor_scalar(pen[:, :], pen[:, :], -1.0, BIG, ALU.add, ALU.mult).then_inc(S("steps_made"), 1)

            wait_next("idrow_ps")
            for k, (a, n) in enumerate(halves):
                link(v.tensor_scalar(dst_f[0:n, :], ps[0:n, 3 * k, :], qcol[0:n, k:k + 1], -1.0,
                                     ALU.subtract, ALU.max))
                v.tensor_single_scalar(idrow[k][0:n, 0:EC], dst_f[0:n, :], float(P), op=ALU.min)
                v.tensor_copy(idrow[k][0:n, EC:2 * EC], ps[0:n, 3 * k + 1, :])
                link(v.tensor_copy(idrow[k][0:n, 2 * EC:3 * EC], ps[0:n, 3 * k + 2, :]))
            v.sem_inc(S("idrow_made"), 1)

            wait_next("wt_ps")
            v.tensor_copy(wlr[0:C, :], ps[0:C, 0, 0:2 * C])
            v.tensor_copy(wns[0:C, :], ps[0:C, 0, 2 * C:4 * C])
            v.wait_ge(S("gmask"), 1)
            for j in range(G):
                last = v.tensor_scalar(web[:, j, :], ps[0:G * ED, 1, 0:C], gmask[:, j:j + 1], None, ALU.mult)
            last.then_inc(S("wt_made"), 1)

            def normalise(dst, src, parts, heads):
                w = heads * D0
                link(v.tensor_tensor(sq[0:parts, 0:w], src, src, ALU.mult))
                link(v.reduce_sum(nrm[0:parts, 0:heads], split(sq[0:parts, 0:w], D0), AX.X))
                v.tensor_single_scalar(nrm[0:parts, 0:heads], nrm[0:parts, 0:heads], 1e-24, op=ALU.max) \
                    .then_inc(S("square_sum"), 1)
                wait_next("root")
                link(v.reciprocal(nrm[0:parts, 0:heads], nrm[0:parts, 0:heads]))
                link(v.tensor_tensor(split(dst, D0), split(src, D0),
                                     nrm[0:parts, 0:heads, None].to_broadcast([parts, heads, D0]), ALU.mult))

            wait_next("qkv_ps")
            hf = h[:, :, :].rearrange("p b c -> p (b c)")
            v.tensor_copy(kvn[:, :], ps[0:NI, 2, 0:2 * C])
            link(v.tensor_copy(hf, acc[:, 0:NB * C]))
            def thirds(dst3, src, tmp):
                link(v.tensor_copy(dst3(0), src))
                link(v.tensor_tensor(tmp, src, dst3(0), ALU.subtract))
                link(v.tensor_copy(dst3(1), tmp))
                link(v.tensor_tensor(tmp, tmp, dst3(1), ALU.subtract))
                link(v.tensor_copy(dst3(2), tmp))

            normalise(tab[:, 0:NB * C], hf, P, NB * H0)
            thirds(lambda k: tab3[:, k, 0:NB * C], tab[:, 0:NB * C], sq[:, 0:NB * C])
            normalise(kvn[:, 0:C], kvn[:, 0:C], NI, H0)
            thirds(lambda k: kvn3[:, k, :], kvn[:, :], sq[0:NI, 0:2 * C])
            v.sem_inc(S("kvn_made"), 1)
            normalise(pos[:, :], pos[:, :], KVOL, H0)
            thirds(lambda k: pos3[:, k, :], pos[:, :], sq[0:KVOL, 0:C])
            v.sem_inc(S("tables_made"), 1)
            v.sem_inc(S("sums_free"), 1)

            def onehot_T(layer, q, s, i, used, ids):
                for name in used:
                    done(v, name, q - SLOTS)
                v.wait_ge(S(f"{layer}_ids{s}"), i * 16 + 16)
                o = ohT[s % SLOTS]
                if layer != "l0":
                    v.tensor_scalar(o[:, 0:EC], ids, part_f[:, 0:1], None, ALU.is_equal) \
                        .then_inc(S(f"{layer}_ohT"), 1)
                    return
                v.tensor_scalar(o[:, 0:2 * EC], ids[:, 0:2 * EC], part_f[:, 0:1], None, ALU.is_equal)
                v.tensor_scalar(o[0:3 * NI, 2 * EC:3 * EC], ids[0:3 * NI, 2 * EC:3 * EC], mod_ni[:, 0:1], None,
                                ALU.is_equal).then_inc(S(f"{layer}_ohT"), 1)

            def lowest(layer, q, s, width):
                def one():
                    done(v, f"{layer}_hi", q)
                    done(v, f"{layer}_lo", q - SLOTS)
                    v.tensor_tensor(rest[s % SLOTS][:, :, 0:width], pay[s % SLOTS][:, :, 0:width],
                                    pay3[s % GS][:, 0, :, 0:width], ALU.subtract).then_inc(S(f"{layer}_rest"), 1)

                def two():
                    done(v, f"{layer}_mid", q)
                    v.tensor_tensor(pay3[s % GS][:, 2, :, 0:width], rest[s % SLOTS][:, :, 0:width],
                                    pay3[s % GS][:, 1, :, 0:width], ALU.subtract).then_inc(S(f"{layer}_lo"), 1)
                return one, two

            def onehot_rest(layer, q, s):
                if POOL_TILES[layer] == G:
                    return
                done(v, f"{layer}_sum", q - GS)
                for j in range(POOL_TILES[layer], G):
                    last = v.tensor_scalar(ohb[s % GS][:, j, :], col_b[:, :], dstL[:, bass.ds(q * G + j, 1)], None,
                                           ALU.is_equal)
                last.then_inc(S(f"{layer}_ohv"), 1)

            def onehot(layer, q, s):
                done(v, f"{layer}_sum", q - SLOTS)
                v.tensor_tensor(oh[s % SLOTS][:, :, :], col_f[:, None, 0:P].to_broadcast([P, G, P]),
                                dstL[:, bass.ds(q * G, G)][:, :, None].to_broadcast([P, G, P]), ALU.is_equal) \
                    .then_inc(S(f"{layer}_oh"), 1)

            def step0(q, s, i):
                onehot_rest("l0", q, s)
                one, two = lowest("l0", q - 1, s - 1, C)
                done(v, "l0_ga", q)
                done(v, "l0_kv", q)
                v.tensor_tensor(split(prod[:, 0:G * C], C), split(ga[s % SLOTS][:, 0:G * C], C), gat[s][:, :, 0:C],
                                ALU.mult).then_inc(S("l0_prod"), 1)
                if not first(q):
                    one()
                done(v, "l0_prod", q)
                v.reduce_sum(attn[:, :], split(prod[:, 0:G * C], D0), AX.X).then_inc(S("l0_attn"), 1)
                onehot_T("l0", q + 2, (s + 2) % GS, i + (s + 2) // GS, ("l0_ga", "l0_src"), idb0[(s + 2) % GS])
                done(v, "l0_attn", q)
                v.tensor_tensor(pay[s % SLOTS][:, :, 0:C].rearrange("p j (h d) -> p j h d", d=D0),
                                gat[s][:, :, C:2 * C].rearrange("p j (h d) -> p j h d", d=D0),
                                split(attn[:, :], H0)[:, :, :, None].to_broadcast([P, G, H0, D0]), ALU.mult) \
                    .then_inc(S("l0_pay"), 1)
                if not first(q):
                    two()
            for q in range(2):
                onehot_T("l0", q, q, 0, ("l0_ga", "l0_src"), idb0[q])
            steps(v, step0)
            for part in lowest("l0", NQ - 1, GS - 1, C):
                part()

            def norm(dst, gamma=None):
                link(v.reduce_sum(st1[:, :], h[:, :, :], AX.X))
                link(v.tensor_single_scalar(st1[:, :], st1[:, :], 1.0 / C, op=ALU.mult))
                link(v.tensor_tensor(h[:, :, :], h[:, :, :], per_row(st1), ALU.subtract))
                link(v.tensor_tensor(split(sq[:, 0:NB * C], C), h[:, :, :], h[:, :, :], ALU.mult))
                link(v.reduce_sum(st2[:, :], split(sq[:, 0:NB * C], C), AX.X))
                v.tensor_scalar(st2[:, :], st2[:, :], 1.0 / C, 1e-5, ALU.mult, ALU.add).then_inc(S("square_sum"), 1)
                wait_next("root")
                link(v.reciprocal(st3[:, :], st2[:, :]))
                if gamma is None:
                    v.tensor_tensor(dst, h[:, :, :], per_row(st3), ALU.mult).then_inc(S("x_made"), 1)
                    return
                link(v.tensor_tensor(h[:, :, :], h[:, :, :], per_row(st3), ALU.mult))
                link(v.tensor_tensor(h[:, :, :], h[:, :, :], over(vecs, VGAMMA), ALU.mult))
                link(v.tensor_tensor(h[:, :, :], h[:, :, :], over(vecs, VBETA), ALU.add))
                link(v.tensor_single_scalar(h[:, :, :], h[:, :, :], 0.0, op=ALU.max))

            done(v, "l0_sum", NQ - 1)
            accb = split(acc, P)
            v.tensor_copy(cnt[:, :], accb[:, :, C])
            v.tensor_copy(h[:, :, :], accb[:, :, 0:C]).then_inc(S("agg_made"), 1)
            wait_next("agg_made")
            link(v.tensor_single_scalar(rdeg[:, :], cnt[:, :], 1.0, op=ALU.max))
            v.reciprocal(rdeg[:, :], rdeg[:, :])
            wait_next("proj_ps")
            link(v.tensor_tensor(h[:, :, :], split(acc[:, 0:NB * C], C), over(vecs, VBO), ALU.add))
            link(v.scalar_tensor_tensor(out=h[:, :, :], in0=x[:, :, :], scalar=2.0, in1=h[:, :, :],
                                        op0=ALU.mult, op1=ALU.add))
            norm(x[:, :, :])

            wait_next("proj_ps")
            v.tensor_copy(split(rows[:, 0:NB * C], C), accb[:, :, 0:C]).then_inc(S("xl_made"), 1)
            link(v.tensor_copy(split(tab[:, 0:NB * C], C), accb[:, :, C:P]))
            thirds(lambda k: tab3[:, k, 0:NB * C], tab[:, 0:NB * C], sq[:, 0:NB * C])
            v.sem_inc(S("xr_made"), 1)

            def step1(q, s, i):
                c = v.value_load(ctab[0:1, bass.ds(q, 1)], min_val=0, max_val=NCH - 1)
                onehot_T("l1", q + 1, (s + 1) % GS, i + (s + 1) // GS, ("l1_ga",), idb[(s + 1) % GS][:, :])
                done(v, "l1_ga", q)
                v.wait_ge(S("l1_here"), c + 1)
                v.tensor_tensor(prod[:, 0:G * C], ga[s % SLOTS][:, 0:G * C],
                                ring[:, bass.ds(c % GS * (G * HID), G * C)], ALU.add).then_inc(S("l1_z"), 1)
                done(v, "l1_z", q)
                v.scalar_tensor_tensor(out=lky[:, :], in0=prod[:, 0:G * C], scalar=0.2, in1=prod[:, 0:G * C],
                                       op0=ALU.mult, op1=ALU.max).then_inc(S("l1_lky"), 1)
                done(v, "l1_lky", q)
                v.tensor_tensor(split(wgt[:, :], C), split(lky[:, :], C),
                                vecs[:, VATT:VATT + 1, :].to_broadcast([P, G, C]), ALU.mult) \
                    .then_inc(S("l1_wgt"), 1)
                done(v, "l1_wgt", q)
                v.reduce_sum(lg[:, bass.ds(q * G * H1, G * H1)], split(wgt[:, :], D1), AX.X).then_inc(S("l1_lg"), 1)
            onehot_T("l1", 0, 0, 0, ("l1_ga",), idb[0][:, :])
            steps(v, step1)
            done(v, "l1_lg", NQ - 1)
            def by_group(t):
                return t.rearrange("p (g k) -> p g k", g=NG)[:, :, :, None].to_broadcast([P, NG, KG, H1])

            def by_tile(t):
                return t.rearrange("p (k g h) -> p g k h", g=NG, h=H1)
            v.tensor_copy(by_tile(brk[:, 0:TL]), by_group(dstK[:, 0:NQ * G]))
            v.tensor_tensor(by_tile(run[:, :]), lg[:, :].rearrange("p (g k h) -> p g k h", g=NG, h=H1),
                            by_group(pen[:, 0:NQ * G]), ALU.add).then_inc(S("l1_logits"), 1)

            done(v, "bank_out", KG // 4 - 1)
            v.memset(brk[:, 0:1], 0.0)
            v.memset(brk[:, TL:TL + 1], 0.0)
            link(v.tensor_tensor(brk[:, 1:TL], keyT[:, 1:TL], keyT[:, 0:TL - 1], ALU.is_equal))
            link(v.tensor_scalar(brk[:, 1:TL], brk[:, 1:TL], -1.0, BIG, ALU.add, ALU.mult))
            done(v, "bank_out", 2 * KG // 4 - 1)

            def scan_right(src, initial):
                link(v.tensor_tensor_scan(out=run[:, :], data0=brk[:, 0:TL], data1=src, initial=initial,
                                          op0=ALU.add, op1=ALU.max))

            def scan_left(src, initial):
                link(v.tensor_tensor_scan(out=run[:, ::-1], data0=brk[:, 1:TL + 1][:, ::-1], data1=src[:, ::-1],
                                          initial=initial, op0=ALU.add, op1=ALU.max))
            scan_right(lgT[:, :], -BIG)
            v.tensor_copy(ends[:, 0:1], run[:, TL - 1:TL])
            v.tensor_copy(ends[:, 2:3], keyT[:, 0:1])
            link(v.tensor_copy(ends[:, 3:4], keyT[:, TL - 1:TL]))
            scan_left(lgT[:, :], -BIG)
            v.tensor_copy(ends[:, 1:2], run[:, 0:1]).then_inc(S("ends_made"), 1)
            wait_next("ends_ps")
            LAST, FIRST, KF, KL, WHOLE, SAME, S0, S1, T0, T1, CR, CL = range(12)
            for k in range(4):
                last = v.tensor_copy(crow[0:1, k, :].rearrange("p (h g) -> p h g", g=NG),
                                     ps[0:1, k, 0:P].rearrange("p (g h) -> p h g", h=H1))
            link(last)

            def row(k, a=0, b=NG):
                return crow[0:1, k, :].rearrange("p (h g) -> p h g", g=NG)[:, :, a:b]
            v.memset(crow[0:1, SAME:T1 + 1, :].rearrange("p a b -> p (a b)"), -BIG)
            link(v.tensor_tensor(row(WHOLE), row(KF), row(KL), ALU.is_equal))
            link(v.tensor_scalar(row(WHOLE), row(WHOLE), -1.0, BIG, ALU.add, ALU.mult))
            link(v.tensor_tensor(row(SAME, 0, NG - 1), row(KL, 0, NG - 1), row(KF, 1, NG), ALU.is_equal))
            link(v.tensor_scalar(row(SAME, 0, NG - 1), row(SAME, 0, NG - 1), -1.0, BIG, ALU.add, ALU.mult))
            v.tensor_tensor(row(S0, 1, NG), row(SAME, 0, NG - 1), row(WHOLE, 0, NG - 1), ALU.add)
            v.tensor_tensor(row(S1, 1, NG), row(SAME, 0, NG - 1), row(LAST, 0, NG - 1), ALU.add)
            v.tensor_tensor(row(T0, 0, NG - 1), row(SAME, 0, NG - 1), row(WHOLE, 1, NG), ALU.add)
            link(v.tensor_tensor(row(T1, 0, NG - 1), row(SAME, 0, NG - 1), row(FIRST, 1, NG), ALU.add))
            link(v.tensor_tensor_scan(out=crow[0:1, WHOLE, :], data0=crow[0:1, S0, :], data1=crow[0:1, S1, :],
                                      initial=-BIG, op0=ALU.add, op1=ALU.max))
            link(v.tensor_tensor_scan(out=crow[0:1, SAME, ::-1], data0=crow[0:1, T0, ::-1],
                                      data1=crow[0:1, T1, ::-1], initial=-BIG, op0=ALU.add, op1=ALU.max))
            for o, k in ((CR, WHOLE), (CL, SAME)):
                last = v.tensor_copy(crow[0:1, o, :].rearrange("p (g h) -> p h g", h=H1), row(k))
            last.then_inc(S("carry_made"), 1)
            wait_next("carry_ps")
            for k in range(2):
                last = v.tensor_copy(carry[:, k:k + 1], ps[:, 4 + k, 0:1])
            link(last)
            scan_right(lgT[:, :], carry[:, 0:1])
            link(v.tensor_copy(keyT[:, :], run[:, :]))
            scan_left(keyT[:, :], carry[:, 1:2])
            v.tensor_tensor(lgT[:, :], lgT[:, :], run[:, :], ALU.subtract).then_inc(S("shift_made"), 1)

            v.sem_inc(S("sums_free"), 1)
            done(v, "ex_out", KG // 4 - 1)

            def step1b(q, s, i):
                one, two = lowest("l1b", q - 1, s - 1, C + H1)
                if not first(q):
                    one()
                ex = lg[:, bass.ds(q * G * H1, G * H1)]
                v.tensor_copy(pay[s % SLOTS][:, :, C:C + H1], split(ex, H1))
                v.wait_ge(S(f"l1b_rows{s}"), i * 16 + 16)
                v.tensor_tensor(pay[s % SLOTS][:, :, 0:C].rearrange("p j (h d) -> p j h d", d=D1),
                                g64[s].rearrange("p (j h d) -> p j h d", j=G, d=D1),
                                split(ex, H1)[:, :, :, None].to_broadcast([P, G, H1, D1]), ALU.mult) \
                    .then_inc(S("l1b_pay"), 1)
                onehot_rest("l1b", q, s)
                if not first(q):
                    two()
            steps(v, step1b)
            for part in lowest("l1b", NQ - 1, GS - 1, C + H1):
                part()
            done(v, "l1b_sum", NQ - 1)
            den = sq[:, NB * C:NB * C + NB * H1]
            link(v.tensor_single_scalar(split(den, H1), accb[:, :, C:C + H1], 1e-16, op=ALU.add))
            link(v.reciprocal(den, den))
            link(v.tensor_copy(h[:, :, :], accb[:, :, 0:C]))
            hh = h[:, :, :].rearrange("p b c -> p (b c)")
            link(v.tensor_tensor(split(hh, D1), split(hh, D1), den[:, :, None].to_broadcast([P, NB * H1, D1]),
                                 ALU.mult))
            link(v.tensor_tensor(h[:, :, :], h[:, :, :], over(vecs, VBIAS), ALU.add))
            link(v.tensor_tensor(h[:, :, :], h[:, :, :], x[:, :, :], ALU.add))
            norm(None, gamma=True)
            link(v.tensor_tensor(h[:, :, :], h[:, :, :], x[:, :, :], ALU.add))
            norm(x[:, :, :])

            wait_next("proj_ps")
            v.tensor_copy(rows[:, 0:NB * HID], acc).then_inc(S("a_made"), 1)
            link(v.tensor_copy(tab, top))
            thirds(lambda k: tab3[:, k, :], tab, sq)
            v.sem_inc(S("sums_free"), 1)

            def step2(q, s, i):
                c = v.value_load(ctab[0:1, bass.ds(q, 1)], min_val=0, max_val=NCH - 1)
                onehot_T("l2", q + 1, (s + 1) % GS, i + (s + 1) // GS, ("l2_ga",), idb[(s + 1) % GS][:, :])
                onehot("l2", q, s)
                done(v, "l2_ga", q)
                v.wait_ge(S("l2_here"), c + 1)
                v.tensor_tensor(pay[s % SLOTS][:, :, :], split(ga[s % SLOTS], HID),
                                split(ring[:, bass.ds(c % GS * (G * HID), G * HID)], HID), ALU.add) \
                    .then_inc(S("l2_z"), 1)
            onehot_T("l2", 0, 0, 0, ("l2_ga",), idb[0][:, :])
            steps(v, step2)
            done(v, "l2_sum", NQ - 1)
            v.wait_ge(S("a_out"), 16)
            v.tensor_copy(rows[:, 0:NB * HID], acc).then_inc(S("agg_made"), 1)
            link(v.tensor_tensor(h[:, :, :], over(vecs, VB2), per_row(cnt), ALU.mult))
            wait_next("proj_ps")
            link(v.tensor_tensor(h[:, :, :], h[:, :, :], split(acc[:, 0:NB * C], C), ALU.add))
            link(v.tensor_tensor(h[:, :, :], h[:, :, :], per_row(rdeg), ALU.mult))
            link(v.tensor_tensor(h[:, :, :], h[:, :, :], x[:, :, :], ALU.add))
            norm(x[:, :, :])
            v.sem_inc(S("sums_free"), 1)

            def step3(q, s, i):
                onehot("l3", q, s)
            steps(v, step3)
            done(v, "l3_sum", NQ - 1)
            v.tensor_tensor(h[:, :, :], accb[:, :, 0:C], per_row(rdeg), ALU.mult).then_inc(S("agg_made"), 1)
            wait_next("proj_ps")
            v.wait_ge(S("x3_out"), 16)
            link(v.tensor_tensor(h[:, :, :], split(acc[:, 0:NB * C], C), x[:, :, :], ALU.add))
            norm(x[:, :, :])


_INS = ["x", "src", "dst", "edge_attr_16", "L0_gnn_Wq", "L0_gnn_bq", "L0_gnn_Wk", "L0_gnn_bk", "L0_gnn_Wv",
        "L0_gnn_bv", "L0_gnn_Wo", "L0_gnn_bo", "L0_gnn_pos_enc", "L1_gnn_W_l", "L1_gnn_b_l", "L1_gnn_W_r",
        "L1_gnn_b_r", "L1_gnn_W_e", "L1_gnn_att", "L1_gnn_bias", "L1_gnn_gamma", "L1_gnn_beta", "L2_gnn_W1",
        "L2_gnn_b1", "L2_gnn_W2", "L2_gnn_b2", "L3_gnn_w_neigh", "L3_gnn_w_self", "L3_gnn_b_self"]


def kernel(**inputs):
    import numpy as _np
    import concourse.bacc as _bacc
    from concourse import mybir as _mybir
    from concourse.bass_utils import run_bass_kernel_spmd as _run

    nc = _bacc.Bacc("TRN2", target_bir_lowering=False, num_devices=1)
    arrays, io = {}, {}
    for name in _INS:
        a = _np.ascontiguousarray(inputs[name])
        arrays[f"in_{name}_dram"] = a
        io[name] = nc.dram_tensor(f"in_{name}_dram", a.shape, _mybir.dt.from_np(a.dtype), kind="ExternalInput").ap()
    out = nc.dram_tensor("out_0_dram", (N, C), F32, kind="ExternalOutput").ap()
    build(nc, io, out)
    r = _run(nc, [arrays], core_ids=[0])
    return r.results[0]["out_0_dram"]
```

```python
import concourse.bass as bass
from concourse import mybir
from contextlib import ExitStack

F32 = mybir.dt.float32
BF16 = mybir.dt.bfloat16
F16 = mybir.dt.float16
I32 = mybir.dt.int32
ALU = mybir.AluOpType
ACT = mybir.ActivationFunctionType
AX = mybir.AxisListType

N = 2048
E = 65536
C = 64
P = 128
NB = N // P
G = 4
EC = G * P
NCH = E // EC
NQ = NCH + NB
NT = NQ + 4
KVOL = 125
NI = -(-N // KVOL)
H0, D0 = 4, 16
H1, D1 = 8, 8
ED = 16
HID = 128
NG = P // H1
KG = NQ * G // NG
TL = KG * P
EXT = KG // 3
IXQ = 4
POOL_TILES = {"l0": 4, "l1b": 2}
NW = 26
WHOLE_NUMBERS = 1.5 * 2 ** 23
BIG = 1e30
SLOTS = 2
GS = 4
FAR = G - 1
IDW = P + 3 * EC
PACK = GS + 3


def build(nc, io, out):
    ctx = ExitStack()
    with ctx:
        def sb(name, shape, dt=F32):
            return ctx.enter_context(nc.sbuf_tensor(name, shape, dt))

        sems = {}

        def S(name):
            if name not in sems:
                sems[name] = ctx.enter_context(nc.semaphore(name))
            return sems[name]

        xl_dram = nc.dram_tensor("xl_table", (N, C), F32, kind="Internal").ap()
        a_dram = nc.dram_tensor("a_table", (N, HID), F32, kind="Internal").ap()
        x3_dram = nc.dram_tensor("x3_table", (N, C), F32, kind="Internal").ap()
        ids_dram = nc.dram_tensor("step_ids", (NT, IDW), BF16, kind="Internal").ap()
        spill_dram = nc.dram_tensor("xl_rows", (P, NCH, FAR * C), F32, kind="Internal").ap()
        near_dram = nc.dram_tensor("xl_rows_last", (P, NQ + GS - 1, C), F32, kind="Internal").ap()

        ident = sb("ident", [P, P])
        ones = sb("ones", [P, P])
        zeros = sb("zeros", [1, 512])
        col_i = sb("col_i", [P, NT], I32)
        col_f = sb("col_f", [P, NT])
        col_b = sb("col_b", [P, P], BF16)
        part_i = sb("part_i", [P, 1], I32)
        part_f = sb("part_f", [P, 1])
        notfirst = sb("notfirst", [P, 1])
        gmask = sb("gmask", [G * ED, G])
        wq = sb("wq", [C + 1, C])
        wkv = sb("wkv", [C + 1, 2 * C])
        wo = sb("wo", [C, C])
        wraw = sb("wraw", [C, 4 * C])
        weraw = sb("weraw", [C, G * ED])
        wlr = sb("wlr", [C + 1, 2 * C])
        wns = sb("wns", [C + 1, 2 * C])
        w1a = sb("w1a", [C, HID])
        w1b = sb("w1b", [C + 1, HID])
        w2 = sb("w2", [HID, C])
        web = sb("web", [G * ED, G, C])
        pos = sb("pos", [KVOL, C])
        vecs = sb("vecs", [P, 6, C])
        VBO, VATT, VBIAS, VGAMMA, VBETA, VB2 = range(6)
        x = sb("x", [P, NB, C])
        h = sb("h", [P, NB, C])
        st1 = sb("st1", [P, NB])
        st2 = sb("st2", [P, NB])
        st3 = sb("st3", [P, NB])
        nrm = sb("nrm", [P, NB * H1])
        xT = sb("xT", [C + 1, N])
        tab3 = sb("tab3", [P, 3, NB * HID], BF16)
        xs3 = sb("xs3", [P, 3, NB * C], BF16)
        cnt = sb("cnt", [P, NB])
        rdeg = sb("rdeg", [P, NB])
        kvn = sb("kvn", [NI, 2 * C])
        kvn3 = sb("kvn3", [NI, 3, 2 * C], BF16)
        kvs = sb("kvs", [3 * NI, 2 * C], BF16)
        dst4 = sb("dst4", [P, GS * G])
        mod_ni = sb("mod_ni", [3 * NI, 2])
        pos3 = sb("pos3", [KVOL, 3, C], BF16)
        blk = sb("blk", [P, 1], I32)
        qc = sb("qc", [P, 2])
        qcol = sb("qcol", [P, 4])
        btab = sb("btab", [P, NT], I32)
        bmin = sb("bmin", [1, 2, NT + 1], I32)
        bpack = sb("bpack", [1, 2, NQ - GS + 1], I32)
        ctab = sb("ctab", [P, NT], I32)
        srcI = sb("srcI", [P, (NCH + IXQ) * G], I32)
        qtab = sb("qtab", [1, NCH], I32)
        dstK = sb("dstK", [P, NT * G])
        dstL = sb("dstL", [P, NT * G])
        pen = sb("pen", [P, NT * G])
        idx = [sb(f"idx{s}", [P, IXQ * G], I32) for s in range(2)]
        idb = [sb(f"idb{s}", [P, P + EC], BF16) for s in range(GS)]
        node16 = sb("node16", [P, NB, P], F16)
        ohS = [sb(f"ohS{s}", [P, NB, P], BF16) for s in range(SLOTS)]
        near = [sb(f"near{s}", [P, C]) for s in range(GS)]
        ring = sb("ring", [P, GS * G * HID])
        gat = [ring[:, s * G * HID:(s + 1) * G * HID].rearrange("p (j c) -> p j c", j=G) for s in range(GS)]
        g64 = [gat[s][:, 0:G // 2, :].rearrange("p j c -> p (j c)") for s in range(GS)]
        oh = [sb(f"oh{s}", [P, G, P]) for s in range(SLOTS)]
        ohT = [sb(f"ohT{s}", [P, 3 * EC], BF16) for s in range(SLOTS)]
        pay = [sb(f"pay{s}", [P, G, HID]) for s in range(SLOTS)]
        pay3 = [sb(f"pay3{s}", [P, 3, G, C + H1], BF16) for s in range(GS)]
        ohb = [oh[s % SLOTS][:, (s // SLOTS) * 2:(s // SLOTS) * 2 + G // 2, :].bitcast(BF16)
               .rearrange("p a (b n) -> p (a b) n", n=P) for s in range(GS)]
        rest = [sb(f"rest{s}", [P, G, C + H1]) for s in range(SLOTS)]
        prod = sb("prod", [P, G * HID])
        lky = sb("lky", [P, G * C])
        wgt = sb("wgt", [P, G * C])
        attn = sb("attn", [P, G * H0])
        atr = [sb(f"atr{s}", [P, G * ED]) for s in range(GS)]
        atT = [sb(f"atT{s}", [G * ED, P]) for s in range(SLOTS)]
        lg = sb("lg", [P, NQ * G * H1])
        lgT = sb("lgT", [P, TL])
        keyT = sb("keyT", [P, TL])
        brk = sb("brk", [P, TL + 1])
        run = sb("run", [P, TL])
        dst_i, src_i = (run[:, k * EC:(k + 1) * EC].bitcast(I32) for k in range(2))
        dst_f, src_f, k_f, i_f = (keyT[:, k * EC:(k + 1) * EC] for k in range(4))
        idrow = [lgT[:, k * IDW // 2:(k + 1) * IDW // 2].bitcast(BF16) for k in range(2)]
        idb0 = [lgT[:, k * 3 * EC // 2:(k + 1) * 3 * EC // 2].bitcast(BF16) for k in range(GS)]
        tab = brk[:, 0:NB * HID]
        sq = lg[:, 0:NB * HID]
        aggT = run[:, 0:N]
        cqb, bqb, selF, begun = (lg[:, NB * HID + k * NT:NB * HID + (k + 1) * NT] for k in range(4))
        rows = keyT[:, 0:NB * HID]
        ends = sb("ends", [P, 4])
        crow = xT[0:1, 0:12 * P].rearrange("p (k c) -> p k c", k=12)
        carry = sb("carry", [P, 2])

        ps = ctx.enter_context(nc.psum_tensor("ps", [P, 8, 512], F32))
        acc = ps[:, 0:4, :].rearrange("p a b -> p (a b)")
        top = ps[:, 4:8, :].rearrange("p a b -> p (a b)")
        kv = [ps[:, 4 + s, :] for s in range(SLOTS)]
        ga = [ps[:, 6 + s, :] for s in range(SLOTS)]

        halves = ((0, P), (P, NT - P))

        def split(ap, width):
            return ap.rearrange("p (b c) -> p b c", c=width)

        def done(eng, name, m):
            if isinstance(m, int) and m < 0:
                return
            eng.wait_ge(S(name), m + 1)

        def steps(eng, body):
            for s in range(GS):
                body(s, s, 0)
            with eng.Fori(1, NQ // GS) as i:
                for s in range(GS):
                    body(i * GS + s, s, i)

        def unpack(eng, known, q, s, a, n, row=0):
            if s == 0:
                packed = eng.value_load(bpack[0:1, row, bass.ds(q, 1)], min_val=0, max_val=NB ** PACK - 1)
                for r in range(a, GS + n):
                    known[r] = eng.snap(packed // NB ** (r + 1) % NB)

        def first(q):
            return isinstance(q, int) and q == 0

        def counted(eng):
            seen = {}

            def wait_next(name):
                seen[name] = seen.get(name, 0) + 1
                eng.wait_ge(S(name), seen[name])
            return wait_next

        block = ctx.enter_context(nc.Block())

        @block.sync
        def _(sp):
            wait_next = counted(sp)

            def load(dst, src, name):
                sp.dma_start(dst, src).then_inc(S(name), 16)

            load(dst_i[:, :], io["dst"].rearrange("(c e) -> c e", e=EC), "dst_in")
            load(src_i[:, :], io["src"].rearrange("(c e) -> c e", e=EC), "src_in")
            load(x[:, :, :], io["x"].rearrange("(b p) c -> p b c", p=P), "w_in")
            weights = [
                (wq[0:C, :], io["L0_gnn_Wq"]), (wq[C:C + 1, :], io["L0_gnn_bq"][None, :]),
                (wkv[0:C, 0:C], io["L0_gnn_Wk"]), (wkv[0:C, C:2 * C], io["L0_gnn_Wv"]),
                (wkv[C:C + 1, 0:C], io["L0_gnn_bk"][None, :]), (wkv[C:C + 1, C:2 * C], io["L0_gnn_bv"][None, :]),
                (wo[:, :], io["L0_gnn_Wo"]), (pos[:, :], io["L0_gnn_pos_enc"].rearrange("k h d -> k (h d)")),
                (wraw[:, 0:C], io["L1_gnn_W_l"]), (wraw[:, C:2 * C], io["L1_gnn_W_r"]),
                (wraw[:, 2 * C:3 * C], io["L3_gnn_w_neigh"]), (wraw[:, 3 * C:4 * C], io["L3_gnn_w_self"]),
                (split(weraw[:, :], ED), io["L1_gnn_W_e"][:, None, :].to_broadcast([C, G, ED])),
                (wlr[C:C + 1, 0:C], io["L1_gnn_b_l"][None, :]),
                (wlr[C:C + 1, C:2 * C], io["L1_gnn_b_r"][None, :]),
                (wns[C:C + 1, C:2 * C], io["L3_gnn_b_self"][None, :]),
                (w1a[:, :], io["L2_gnn_W1"][0:C, :]), (w1b[0:C, :], io["L2_gnn_W1"][C:2 * C, :]),
                (w1b[C:C + 1, :], io["L2_gnn_b1"][None, :]), (w2[:, :], io["L2_gnn_W2"])]
            spread = [io["L0_gnn_bo"], io["L1_gnn_att"].rearrange("a h c -> (a h c)"), io["L1_gnn_bias"],
                      io["L1_gnn_gamma"], io["L1_gnn_beta"], io["L2_gnn_b2"]]
            weights += [(vecs[:, i, :], v[None, :].to_broadcast([P, C])) for i, v in enumerate(spread)]
            assert len(weights) == NW
            for dst, src in weights:
                load(dst, src, "w_in")

            def bring_ids(layer, q, s, dst, width):
                done(sp, f"{layer}_ohT", q - GS)
                load(dst, ids_dram[bass.ds(q, 1), P:P + width].to_broadcast([P, width]), f"{layer}_ids{s}")

            wait_next("idrow_made")
            load(ids_dram[0:P, :], idrow[0], "ids_out")
            load(ids_dram[P:NT, :], idrow[1][0:NT - P, :], "ids_out")
            sp.wait_ge(S("w_in"), 16 * (NW + 1))
            load(near_dram[:, NQ:NQ + GS - 1, :], x[:, 0:GS - 1, :], "ids_out")
            sp.wait_ge(S("ids_out"), 48)
            wait_next("kvn_made")
            for k in range(3):
                load(kvs[k * NI:(k + 1) * NI, :], kvn3[:, k, :], "kvs_in")
            steps(sp, lambda q, s, i: bring_ids("l0", q, s, idb0[s], 3 * EC))
            for s in range(2):
                bring_ids("l0", NQ + s, s, idb0[s], 3 * EC)

            wait_next("xl_made")
            load(xl_dram.rearrange("(b p) c -> p b c", p=P), split(rows[:, 0:NB * C], C), "xl_out")

            wait_next("steps_made")

            def chunks(layer, body):
                sp.sem_inc(S(f"{layer}_here"), NB)
                for s in range(GS):
                    body(s, s, 0)
                with sp.Fori(1, NCH // GS) as i:
                    for s in range(GS):
                        body(i * GS + s, s, i)
                sp.sem_inc(S(f"{layer}_here"), 1)

            def arrived(layer, s, i):
                n = 16 * (FAR)
                sp.wait_ge(S(f"{layer}_rows{s}"), i * n + n)
                sp.sem_inc(S(f"{layer}_here"), 1)

            def keep(c, s, i):
                arrived("l1", s, i)
                load(spill_dram[:, bass.ds(c, 1), :].rearrange("p o c -> p (o c)"), g64[s][:, 0:FAR * C],
                     f"l1_spill{s}")

            chunks("l1", keep)
            for s in range(GS):
                sp.wait_ge(S(f"l1_spill{s}"), 16 * NCH // GS)
                sp.wait_ge(S(f"l1_near_out{s}"), 16 * NQ // GS + (16 if s == GS - 1 else 0))
            wait_next("l1_logits")

            def respill(q, s, i):
                c = sp.value_load(ctab[0:1, bass.ds(q, 1)], min_val=0, max_val=NCH - 1)
                done(sp, "l1b_pay", q - GS)
                load(g64[s][:, 0:FAR * C], spill_dram[:, bass.ds(c, 1), :].rearrange("p o c -> p (o c)"),
                     f"l1b_rows{s}")

            steps(sp, respill)

            wait_next("a_made")
            load(a_dram.rearrange("(b p) c -> p b c", p=P), split(rows[:, 0:NB * HID], HID), "a_out")
            chunks("l2", lambda c, s, i: arrived("l2", s, i))
            for _ in range(3):
                wait_next("x_made")
            load(x3_dram.rearrange("(b p) c -> p b c", p=P), x[:, :, :], "x3_out")
            chunks("l3", lambda c, s, i: arrived("l3", s, i))
            wait_next("x_made")
            load(out.rearrange("(b p) c -> p b c", p=P), x[:, :, :], "result_out")
            for name, n in (("result_out", 1), ("ids_out", 3), ("xl_out", 1), ("a_out", 1), ("x3_out", 1)):
                sp.wait_ge(S(name), 16 * n)

        @block.gpsimd
        def _(pool):
            wait_next = counted(pool)
            pool.iota(col_i[:, :], pattern=[[1, NT]], base=0, channel_multiplier=0).then_inc(S("iota"), 1)
            pool.iota(part_i[:, :], pattern=[[0, 1]], base=0, channel_multiplier=1).then_inc(S("iota"), 1)
            pool.memset(ident[:, :], 0.0).then_inc(S("pool_set"), 1)
            pool.memset(gmask[:, :], 1.0).then_inc(S("pool_set"), 1)
            pool.wait_ge(S("pool_set"), 2)
            pool.affine_select(out=ident[:, :], in_=ident[:, :], compare_op=ALU.not_equal, fill=1.0, base=0,
                               pattern=[[-1, P]], channel_multiplier=1).then_inc(S("ident"), 1)
            pool.affine_select(out=gmask[:, :], in_=gmask[:, :], compare_op=ALU.is_ge, fill=0.0, base=0,
                               pattern=[[-ED, G]], channel_multiplier=1).then_inc(S("pool_set"), 1)
            pool.wait_ge(S("pool_set"), 3)
            pool.affine_select(out=gmask[:, :], in_=gmask[:, :], compare_op=ALU.is_ge, fill=0.0, base=ED - 1,
                               pattern=[[ED, G]], channel_multiplier=-1).then_inc(S("gmask"), 1)

            def gather(layer, table, dst, used):
                tiles = FAR

                def turn(t):
                    for u in range(2):
                        for r in range(IXQ):
                            c = (2 * t + u) * IXQ + r
                            early = isinstance(c, int) and c < GS
                            if r == 0:
                                pool.wait_ge(S(f"{layer}_idx"), 2 * t + u + 1)
                            if r == IXQ - 1:
                                if not early:
                                    for z in range(GS):
                                        pool.wait_ge(S(f"{layer}_rows{z}"), (2 * t + u) * (16 * tiles * IXQ // GS))
                                pool.tensor_copy(idx[1 - u][:, :],
                                                 srcI[:, bass.ds(((2 * t + u) + 1) * IXQ * G, IXQ * G)]) \
                                    .then_inc(S(f"{layer}_idx"), 1)
                            if not early:
                                begins = pool.value_load(qtab[0:1, bass.ds(c - GS + 1, 1)], min_val=1, max_val=NQ)
                                pool.wait_ge(S(used), begins)
                                if layer == "l1":
                                    pool.wait_ge(S(f"l1_spill{r}"), (2 * t + u) * 16)
                            pool.nop(nofuse=True)
                            for j in range(tiles):
                                pool.indirect_dma_start(dst(r, j), None, table[:, :],
                                                        bass.IndirectOffsetOnAxis(
                                                            idx[u][:, r * G + j:r * G + j + 1], 0)) \
                                    .then_inc(S(f"{layer}_rows{r}"), 16)
                if layer != "l1":
                    last = f"l{int(layer[1]) - 1}"
                    pool.wait_ge(S(f"{last}_idx"), NCH // IXQ + 1)
                pool.tensor_copy(idx[0][:, :], srcI[:, 0:IXQ * G]).then_inc(S(f"{layer}_idx"), 1)
                turn(0)
                with pool.Fori(1, NCH // (2 * IXQ)) as t:
                    turn(t)

            def onehots(layer):
                def step(q, s, i):
                    if s == 0:
                        done(pool, f"{layer}_oh", q - 1)
                        pool.tensor_copy(dst4[:, :], dstL[:, bass.ds(q * G, GS * G)]).then_inc(S(f"{layer}_dst4"), 1)
                        pool.wait_ge(S(f"{layer}_dst4"), i + 1)
                    done(pool, f"{layer}_sum", q - GS)
                    pool.nop(nofuse=True)
                    for j in range(POOL_TILES[layer]):
                        last = pool.tensor_scalar(ohb[s % GS][:, j, :], col_f[:, 0:P],
                                                  dst4[:, s * G + j:s * G + j + 1], None, ALU.is_equal)
                    last.then_inc(S(f"{layer}_oh"), 1)
                steps(pool, step)

            def wide(s, j):
                return gat[s][:, j, :]

            def slim(s, j):
                return g64[s][:, j * C:(j + 1) * C]

            wait_next("steps_made")
            onehots("l0")
            pool.wait_ge(S("xl_out"), 16)
            gather("l1", xl_dram, slim, "l1_z")
            onehots("l1b")
            pool.wait_ge(S("a_out"), 16)
            gather("l2", a_dram, wide, "l2_z")
            pool.wait_ge(S("x3_out"), 16)
            gather("l3", x3_dram, slim, "l3_sum")

        @block.tensor
        def _(pe):
            wait_next = counted(pe)

            def transpose_nodes(src, width, made):
                for b in range(NB):
                    last = pe.transpose(top[0:width, b * P:(b + 1) * P], src(b), ident[:, :])
                    if b % 4 == 3:
                        last.then_inc(S(made), 1)

            def project(dst, lhs, weight, width, name=None, ready=None, start=True, stop=True):
                for b in range(NB):
                    if ready and b % 4 == 0:
                        wait_next(ready)
                    last = pe.matmul(dst(b), lhs[:, b * P:(b + 1) * P], weight, start=start, stop=stop,
                                     skip_group_check=True)
                if name:
                    last.then_inc(S(name), 1)

            def zero_sums():
                wait_next("sums_free")
                for k in range(4):
                    pe.matmul(ps[:, k, :], zeros[0:1, 0:P], zeros[0:1, :], start=True, stop=True,
                              skip_group_check=True)

            def block_of(q):
                return pe.value_load(btab[0:1, bass.ds(q, 1)], min_val=0, max_val=NB - 1)

            def take_targets(layer, q, s, width, used, b=None):
                b = block_of(q) if b is None else b
                done(pe, f"{layer}_ohT", q)
                done(pe, used, q - SLOTS)
                for j in range(G):
                    for part in range(3):
                        last = pe.matmul(ga[s % SLOTS][:, j * width:(j + 1) * width],
                                         ohT[s % SLOTS][:, j * P:(j + 1) * P],
                                         tab3[:, part, bass.ds(b * width, width)], start=part == 0, stop=part == 2)
                if layer != "l2":
                    last.then_inc(S(f"{layer}_ga"), 1)

            def take_near(layer, q, s, table):
                done(pe, f"{layer}_ohS", q)
                done(pe, f"{layer}_near", q - SLOTS)
                for b in range(NB):
                    for part in range(3):
                        last = pe.matmul(kv[s % SLOTS][:, 0:C], ohS[s % SLOTS][:, b, :],
                                         table[:, part, b * C:(b + 1) * C], start=b == 0 and part == 0,
                                         stop=b == NB - 1 and part == 2, skip_group_check=True)
                last.then_inc(S(f"{layer}_near_ps"), 1)

            def sum_rows(layer, q, s, rhs, width, wait_rows, b):
                wait_rows()
                done(pe, f"{layer}_oh", q)
                for j in range(G):
                    last = pe.matmul(acc[:, bass.ds(b * P, width)], oh[s % SLOTS][:, j, :], rhs(s, j),
                                     start=False, stop=True, skip_group_check=True)
                last.then_inc(S(f"{layer}_sum"), 1)

            def sum_thirds(layer, q, s, width, b=None):
                b = block_of(q) if b is None else b
                done(pe, f"{layer}_lo", q)
                done(pe, f"{layer}_oh", q)
                if POOL_TILES[layer] < G:
                    done(pe, f"{layer}_ohv", q)
                for j in range(G):
                    for part in range(3):
                        last = pe.matmul(acc[:, bass.ds(b * P, width)], ohb[s % GS][:, j, :],
                                         pay3[s % GS][:, part, j, 0:width], start=False, stop=True,
                                         skip_group_check=True)
                last.then_inc(S(f"{layer}_sum"), 1)

            wait_next("begun_made")
            pe.matmul(ps[:, 0, 0:NT], ones[:, :], begun[:, :], start=True, stop=True)
            for k, (a, n) in enumerate(halves):
                last = pe.matmul(ps[0:n, 1, k:k + 1], begun[:, a:a + n], ones[:, 0:1], start=True, stop=True)
            last.then_inc(S("begun_ps"), 1)
            wait_next("sel_made")
            wait_next("ident")
            pe.matmul(ps[0:1, 2, 0:NCH], qc[:, 1:2], ident[:, :], start=True, stop=True)
            for j in range(G):
                pe.transpose(ps[:, j // 4, j * P:(j + 1) * P], src_f[:, j * P:(j + 1) * P], ident[:, :])
                last = pe.matmul(ps[:, G + j, 0:NT], dst_f[:, j * P:(j + 1) * P], selF[:, :], start=True, stop=True)
            last.then_inc(S("ids_ps"), 1)
            wait_next("steps_made")
            for k, (a, n) in enumerate(halves):
                pe.matmul(ps[0:n, 6 + k, 0:P], selF[:, a:a + n], src_f[:, FAR * P:G * P], start=True, stop=True)
                for r, ids in enumerate((dst_f, k_f, i_f)):
                    last = pe.matmul(ps[0:n, 3 * k + r, :], selF[:, a:a + n], ids, start=True, stop=True)
            last.then_inc(S("idrow_ps"), 1)
            wait_next("idrow_made")
            pe.wait_ge(S("w_in"), 16 * (NW + 1))
            for k in range(4):
                pe.transpose(ps[0:C, 0, k * C:(k + 1) * C], wraw[:, k * C:(k + 1) * C], ident[0:C, 0:C])
            pe.matmul(ps[0:G * ED, 1, 0:C], weraw[:, :], ident[0:C, 0:C],
                      start=True, stop=True).then_inc(S("wt_ps"), 1)
            transpose_nodes(lambda b: x[:, b, :], C, "xT_ps")

            wait_next("wt_made")
            project(lambda b: acc[:, b * C:(b + 1) * C], xT, wq[:, :], C, ready="xT_made")
            pe.matmul(ps[0:NI, 2, 0:2 * C], xT[:, 0:NI], wkv[:, :], start=True, stop=True).then_inc(S("proj_ps"), 1)
            wait_next("tables_made")
            zero_sums()

            def take_sources(q, s):
                done(pe, "l0_ohT", q)
                done(pe, "l0_kv", q - SLOTS)
                for j in range(G):
                    o = kv[s % SLOTS][:, j * HID:(j + 1) * HID]
                    pe.matmul(o, ohT[s % SLOTS][0:3 * NI, 2 * EC + j * P:2 * EC + (j + 1) * P], kvs[:, :],
                              start=True, stop=False, skip_group_check=True)
                    for part in range(3):
                        last = pe.matmul(o[:, 0:C], ohT[s % SLOTS][0:KVOL, EC + j * P:EC + (j + 1) * P],
                                         pos3[:, part, :], start=False, stop=part == 2, skip_group_check=True)
                last.then_inc(S("l0_src"), 1)
            pe.wait_ge(S("kvs_in"), 48)
            for q in range(2):
                take_targets("l0", q, q, C, "l0_prod")
                take_sources(q, q)

            known = {}

            def step0(q, s, i):
                unpack(pe, known, q, s, -1, 2)
                take_targets("l0", q + 2, (s + 2) % GS, C, "l0_prod", known[s + 2])
                take_sources(q + 2, (s + 2) % GS)
                if not first(q):
                    sum_thirds("l0", q - 1, s - 1, C + 1, known[s - 1])
            steps(pe, step0)
            sum_thirds("l0", NQ - 1, GS - 1, C + 1)
            done(pe, "l0_kv", NQ + 1)
            wait_next("agg_made")
            transpose_nodes(lambda b: h[:, b, :], C, "aggT_ps")
            project(lambda b: acc[:, b * C:(b + 1) * C], aggT[0:C, :], wo[:, :], C, "proj_ps", "aggT_made")

            wait_next("x_made")
            transpose_nodes(lambda b: x[:, b, :], C, "xT_ps")
            project(lambda b: acc[:, b * P:(b + 1) * P], xT, wlr[:, :], P, "proj_ps", "xT_made")

            def take1(q, s, i, find_block):
                pe.wait_ge(S(f"l1_attr{s}"), i * 16 + 16)
                done(pe, "l1_z", q - SLOTS)
                pe.nop(nofuse=True)
                pe.transpose(ga[s % SLOTS][0:G * ED, 2 * P:3 * P], atr[s][:, :], ident[:, :]).then_inc(S("l1_tr"), 1)
                take_near("l1", q, s, tab3[:, :, NB * C:2 * NB * C])
                b = find_block()
                done(pe, "l1_atT", q)
                pe.matmul(ga[s % SLOTS][:, 0:G * C], atT[s % SLOTS][:, :], web[:, :, :].rearrange("p j c -> p (j c)"),
                          start=True, stop=False, skip_group_check=True)
                done(pe, "l1_ohT", q)
                for j in range(G):
                    for part in range(3):
                        last = pe.matmul(ga[s % SLOTS][:, j * C:(j + 1) * C],
                                         ohT[s % SLOTS][:, j * P:(j + 1) * P], tab3[:, part, bass.ds(b * C, C)],
                                         start=False, stop=j == G - 1 and part == 2, skip_group_check=True)
                last.then_inc(S("l1_ga"), 1)

            def step1(q, s, i):
                def find_block():
                    unpack(pe, known, q, s, 1, 1)
                    return known[s + 1]
                take1(q + 1, (s + 1) % GS, i + (s + 1) // GS, find_block)
            wait_next("tables_made")
            take1(0, 0, 0, lambda: block_of(0))
            steps(pe, step1)

            done(pe, "l1_near", NQ)
            bank = 0
            for by_tile, made in ((brk, "l1_keys"), (run, "l1_logits")):
                wait_next(made)
                for k in range(0, KG, 4):
                    done(pe, "bank_out", bank - 8)
                    for j in range(4):
                        last = pe.transpose(ps[:, bank % 8, j * P:(j + 1) * P], by_tile[:, (k + j) * P:(k + j + 1) * P],
                                            ident[:, :])
                    last.then_inc(S("bank_in"), 1)
                    bank += 1
            wait_next("ends_made")
            done(pe, "bank_out", bank - 1)
            for k in range(4):
                last = pe.matmul(ps[0:1, k, 0:P], ends[:, k:k + 1], ident[:, :], start=True, stop=True)
            last.then_inc(S("ends_ps"), 1)
            wait_next("carry_made")
            for k in range(2):
                last = pe.matmul(ps[:, 4 + k, 0:1], crow[0:1, 10 + k, :], ones[0:1, 0:1], start=True, stop=True)
            last.then_inc(S("carry_ps"), 1)
            for n, k in enumerate(range(0, KG, 4)):
                if k % EXT == 0:
                    wait_next("ex_made")
                done(pe, "ex_out", n - 8)
                for j in range(4):
                    last = pe.transpose(ps[:, n % 8, j * P:(j + 1) * P], lgT[:, (k + j) * P:(k + j + 1) * P],
                                        ident[:, :])
                last.then_inc(S("ex_in"), 1)
            done(pe, "ex_out", KG // 4 - 1)
            zero_sums()

            def step1b(q, s, i):
                unpack(pe, known, q, s, -1, 0)
                if not first(q):
                    sum_thirds("l1b", q - 1, s - 1, C + H1, known[s - 1])
            steps(pe, step1b)
            sum_thirds("l1b", NQ - 1, GS - 1, C + H1)

            wait_next("x_made")
            transpose_nodes(lambda b: x[:, b, :], C, "xT_ps")
            project(lambda b: acc[:, b * P:(b + 1) * P], xT[0:C, :], w1a[:, :], P, "proj_ps", "xT_made")
            project(lambda b: top[:, b * P:(b + 1) * P], xT, w1b[:, :], P, "proj_ps")
            zero_sums()

            def near2(q, s):
                if not (isinstance(q, int) and q < SLOTS):
                    done(pe, "l2_nearT", q - SLOTS)
                take_near("l2", q, s, xs3)

            def turn_near2(q, s):
                done(pe, "l2_near", q)
                pe.nop(nofuse=True)
                pe.transpose(kv[s % SLOTS][0:C, P:2 * P], near[s][:, :], ident[:, :]).then_inc(S("l2_near_tr"), 1)

            def project_near2(q, s):
                done(pe, "l2_nearT", q)
                pe.matmul(ga[s % SLOTS][:, FAR * HID:G * HID], atT[s % SLOTS][:, :], w1a[:, :], start=False, stop=True,
                          skip_group_check=True).then_inc(S("l2_ga"), 1)
            wait_next("tables_made")
            near2(0, 0)
            take_targets("l2", 0, 0, HID, "l2_relu")
            turn_near2(0, 0)
            project_near2(0, 0)

            def step2(q, s, i):
                near2(q + 1, (s + 1) % GS)
                unpack(pe, known, q, s, 0, 1)
                take_targets("l2", q + 1, (s + 1) % GS, HID, "l2_relu", known[s + 1])
                turn_near2(q + 1, (s + 1) % GS)
                sum_rows("l2", q, s, lambda s, j: pay[s % SLOTS][:, j, :], HID, lambda: done(pe, "l2_relu", q), known[s])
                project_near2(q + 1, (s + 1) % GS)
            steps(pe, step2)
            wait_next("agg_made")
            transpose_nodes(lambda b: rows[:, b * P:(b + 1) * P], HID, "aggT_ps")
            project(lambda b: acc[:, b * C:(b + 1) * C], aggT, w2[:, :], C, "proj_ps", "aggT_made")

            wait_next("x_made")
            transpose_nodes(lambda b: x[:, b, :], C, "xT_ps")
            zero_sums()
            wait_next("tables_made")
            for _ in range(4):
                wait_next("xT_made")
            take_near("l3", 0, 0, xs3)

            back = {}

            def sum3(q, s, back):
                b = pe.snap(NB - 1 - back, min_val=0, max_val=NB - 1) if not isinstance(back, int) else NB - 1
                c = q + back + 1

                def rows_here():
                    pe.wait_ge(S("l3_here"), c + 1)
                    done(pe, "l3_near", q)
                sum_rows("l3", q, s, lambda s, j: near[s % GS][:, :] if j == FAR else
                         ring[:, bass.ds(c % GS * (G * HID) + j * C, C)], C, rows_here, b)

            def step3(q, s, i):
                take_near("l3", q + 1, (s + 1) % GS, xs3)
                unpack(pe, back, q, s, -1, 0, row=1)
                if not first(q):
                    sum3(q - 1, s - 1, back[s - 1])
            steps(pe, step3)
            sum3(NQ - 1, GS - 1, 0)
            done(pe, "l3_near", NQ)
            wait_next("agg_made")
            transpose_nodes(lambda b: h[:, b, :], C, "aggT_ps")
            for b in range(NB):
                if b % 4 == 0:
                    wait_next("aggT_made")
                pe.matmul(acc[:, b * C:(b + 1) * C], aggT[0:C, b * P:(b + 1) * P], wns[0:C, 0:C],
                          start=True, stop=False, skip_group_check=True)
                last = pe.matmul(acc[:, b * C:(b + 1) * C], xT[:, b * P:(b + 1) * P], wns[:, C:2 * C],
                                 start=False, stop=True, skip_group_check=True)
            last.then_inc(S("proj_ps"), 1)

        @block.scalar
        def _(act):
            wait_next = counted(act)

            def copy_banks(dst, width, ready, made):
                for k in range(4):
                    wait_next(ready)
                    act.activation(dst[0:width, k * 512:(k + 1) * 512], ps[0:width, 4 + k, :], ACT.Copy) \
                        .then_inc(S(made), 1)

            def split_rows(layer, q, s, width, between=None):
                done(act, f"{layer}_pay", q)
                done(act, f"{layer}_sum", q - GS)
                act.activation(pay3[s % GS][:, 0, :, 0:width], pay[s % SLOTS][:, :, 0:width], ACT.Copy) \
                    .then_inc(S(f"{layer}_hi"), 1)
                if between:
                    between()
                done(act, f"{layer}_rest", q)
                act.activation(pay3[s % GS][:, 1, :, 0:width], rest[s % SLOTS][:, :, 0:width], ACT.Copy) \
                    .then_inc(S(f"{layer}_mid"), 1)

            def bring_ids(layer, q, s):
                for name in {"l1": ("ohT", "ohS"), "l2": ("ohT", "ohS"), "l3": ("ohS",)}[layer]:
                    done(act, f"{layer}_{name}", q - GS)
                act.dma_start(idb[s % GS][:, :], ids_dram[bass.ds(q, 1), 0:P + EC].to_broadcast([P, P + EC])) \
                    .then_inc(S(f"{layer}_ids{s % GS}"), 16)

            attrs_dram = io["edge_attr_16"].rearrange("(c j p) k -> p c j k", j=G, p=P)

            def bring_attrs(q, s):
                c = act.value_load(ctab[0:1, bass.ds(q, 1)], min_val=0, max_val=NCH - 1)
                done(act, "l1_tr", q - GS)
                act.dma_start(atr[s % GS].ap().rearrange("p (o j k) -> p o j k", o=1, j=G),
                              attrs_dram[:, bass.ds(c, 1), :, :]).then_inc(S(f"l1_attr{s % GS}"), 16)

            def keep_near(layer, q, s, used):
                done(act, f"{layer}_near_ps", q)
                done(act, used, q - GS)
                act.activation(near[s % GS][:, :], kv[s % SLOTS][:, 0:C], ACT.Copy) \
                    .then_inc(S(f"{layer}_near"), 1)

            AHEAD = GS - 1

            def root(dst, src):
                wait_next("square_sum")
                act.activation(dst, src, ACT.Sqrt).then_inc(S("root"), 1)

            copy_banks(xT, C, "xT_ps", "xT_made")
            root(nrm[:, 0:NB * H0], nrm[:, 0:NB * H0])
            root(nrm[0:NI, 0:H0], nrm[0:NI, 0:H0])
            root(nrm[0:KVOL, 0:H0], nrm[0:KVOL, 0:H0])

            def keys_values(q, s, i):
                s = q % GS if s is None else s
                done(act, "l0_src", q)
                done(act, "l0_pay", q - GS)
                act.activation(gat[s % GS], kv[s % SLOTS].rearrange("p (j c) -> p j c", j=G), ACT.Copy) \
                    .then_inc(S("l0_kv"), 1)
                if not first(q) and i is not None:
                    split_rows("l0", q - 1, s - 1, C)
            steps(act, keys_values)
            keys_values(NQ, GS, NQ // GS)
            keys_values(NQ + 1, None, None)
            copy_banks(aggT, C, "aggT_ps", "aggT_made")
            root(st2[:, :], st2[:, :])
            copy_banks(xT, C, "xT_ps", "xT_made")

            wait_next("steps_made")
            for q in range(AHEAD):
                bring_ids("l1", q, q)
                bring_attrs(q, q)

            def attrs(q, s, i):
                if s < GS:
                    bring_ids("l1", q + AHEAD, s + AHEAD)
                    bring_attrs(q + AHEAD, s + AHEAD)
                done(act, "l1_tr", q)
                done(act, "l1_ga", q - SLOTS)
                act.activation(atT[s % SLOTS][:, :], ga[s % SLOTS][0:G * ED, 2 * P:3 * P], ACT.Copy) \
                    .then_inc(S("l1_atT"), 1)
                if not first(q):
                    near1(q - 1, s - 1, i)

            def near1(q, s, i):
                if not (isinstance(q, int) and q < GS):
                    act.wait_ge(S(f"l1_near_out{s % GS}"), i * 16)
                keep_near("l1", q, s, "l1_z")
                act.wait_ge(S("l1_near"), q + 1)
                act.dma_start(near_dram[:, bass.ds(q, 1), :].rearrange("p o c -> p (o c)"), near[s % GS][:, :]) \
                    .then_inc(S(f"l1_near_out{s % GS}"), 16)
            act.sem_inc(S(f"l1_near_out{GS - 1}"), 16)
            steps(act, attrs)
            attrs(NQ, GS, NQ // GS)
            act.wait_ge(S("l1_near_out0"), 16 * NQ // GS)
            keep_near("l1", NQ, 0, "l1_z")
            for s in range(1, AHEAD):
                act.wait_ge(S(f"l1_ids{s}"), 16 * NQ // GS + 16)
                act.wait_ge(S(f"l1_attr{s}"), 16 * NQ // GS + 16)
            bank = 0
            for dst in (keyT, lgT):
                for k in range(0, KG, 4):
                    done(act, "bank_in", bank)
                    act.activation(dst[:, k * P:(k + 4) * P], ps[:, bank % 8, :], ACT.Copy) \
                        .then_inc(S("bank_out"), 1)
                    bank += 1
            for k in range(0, KG, EXT):
                wait_next("shift_made")
                act.activation(lgT[:, k * P:(k + EXT) * P], lgT[:, k * P:(k + EXT) * P], ACT.Exp) \
                    .then_inc(S("ex_made"), 1)
            for n, k in enumerate(range(0, KG, 4)):
                done(act, "ex_in", n)
                act.activation(lg[:, :].rearrange("p (g k h) -> p k g h", g=NG, h=H1)[:, k:k + 4, :, :],
                               ps[:, n % 8, :].rearrange("p (k g h) -> p k g h", k=4, h=H1), ACT.Copy) \
                    .then_inc(S("ex_out"), 1)

            def near_back(q, s):
                act.dma_start(g64[s % GS][:, FAR * C:G * C],
                              near_dram[:, bass.ds(q, 1), :].rearrange("p o c -> p (o c)")) \
                    .then_inc(S(f"l1b_near{s % GS}"), 16)
            act.wait_ge(S("ids_out"), 48)
            for s in range(GS):
                act.wait_ge(S(f"l1_near_out{s}"), 16 * NQ // GS + (16 if s == GS - 1 else 0))
            for q in range(AHEAD):
                near_back(q, q)

            def thirds1(q, s, i):
                def ahead():
                    near_back(q + AHEAD, s + AHEAD)
                if first(q):
                    ahead()
                else:
                    split_rows("l1b", q - 1, s - 1, C + H1, ahead)
            steps(act, thirds1)
            split_rows("l1b", NQ - 1, GS - 1, C + H1)
            for s in range(AHEAD):
                act.wait_ge(S(f"l1b_near{s}"), 16 * NQ // GS + 16)
            root(st2[:, :], st2[:, :])
            root(st2[:, :], st2[:, :])
            copy_banks(xT, C, "xT_ps", "xT_made")

            for q in range(AHEAD):
                bring_ids("l2", q, q)

            def relu(q, s, i):
                bring_ids("l2", q + AHEAD, s + AHEAD)
                done(act, "l2_z", q)
                act.activation(pay[s % SLOTS][:, 0:FAR, :], pay[s % SLOTS][:, 0:FAR, :], ACT.Relu)
                act.activation(pay[s % SLOTS][:, FAR, :], ga[s % SLOTS][:, FAR * HID:G * HID], ACT.Relu) \
                    .then_inc(S("l2_relu"), 1)
                near2(q + 1, (s + 1) % GS)

            def near2(q, s):
                keep_near("l2", q, s, "l2_near_tr")
                done(act, "l2_near_tr", q)
                done(act, "l2_ga", q - SLOTS)
                act.activation(atT[s % SLOTS][:, :], kv[s % SLOTS][0:C, P:2 * P], ACT.Copy) \
                    .then_inc(S("l2_nearT"), 1)
            near2(0, 0)
            steps(act, relu)
            for s in range(1, AHEAD):
                act.wait_ge(S(f"l2_ids{s}"), 16 * NQ // GS + 16)
            copy_banks(aggT, HID, "aggT_ps", "aggT_made")
            root(st2[:, :], st2[:, :])
            copy_banks(xT, C, "xT_ps", "xT_made")

            for q in range(AHEAD):
                bring_ids("l3", q, q)

            def near3(q, s, i):
                bring_ids("l3", q + AHEAD, s + AHEAD)
                keep_near("l3", q, s, "l3_sum")
            steps(act, near3)
            keep_near("l3", NQ, 0, "l3_sum")
            for s in range(1, AHEAD):
                act.wait_ge(S(f"l3_ids{s}"), 16 * NQ // GS + 16)
            copy_banks(aggT, C, "aggT_ps", "aggT_made")
            root(st2[:, :], st2[:, :])

        @block.vector
        def _(v):
            wait_next = counted(v)
            chain = [0]

            def link(ins):
                chain[0] += 1
                ins.then_inc(S("vector_chain"), 1)
                v.wait_ge(S("vector_chain"), chain[0])

            def over(vec, k):
                return vec[:, k:k + 1, :].to_broadcast([P, NB, C])

            def per_row(t, width=C):
                return t[:, :, None].to_broadcast([P, NB, width])

            v.memset(ones[:, :], 1.0)
            v.memset(zeros[:, :], 0.0)
            v.memset(xT[C:C + 1, :], 1.0)
            for s in range(GS):
                v.memset(pay3[s][:, 0, :, C:C + 1], 1.0)
                v.memset(pay3[s][:, 1:3, :, C:C + 1], 0.0)
            v.wait_ge(S("iota"), 2)
            v.tensor_copy(col_f[:, :], col_i[:, :])
            v.tensor_copy(col_b[:, :], col_i[:, 0:P])
            link(v.tensor_copy(part_f[:, :], part_i[:, :]))
            link(v.tensor_single_scalar(notfirst[:, :], part_f[:, :], 0.0, op=ALU.is_gt))
            v.wait_ge(S("dst_in"), 16)
            link(v.tensor_single_scalar(blk[:, :], dst_i[:, 0:1], 7, op=ALU.arith_shift_right))
            link(v.tensor_copy(qc[:, 0:1], blk[:, :]))
            link(v.scalar_tensor_tensor(out=qc[:, 1:2], in0=qc[:, 0:1], scalar=notfirst[:, 0:1],
                                        in1=part_f[:, :], op0=ALU.mult, op1=ALU.add))
            v.tensor_scalar(begun[:, :], col_f[:, :], qc[:, 1:2], None, ALU.is_ge).then_inc(S("begun_made"), 1)
            v.tensor_copy(dst_f, dst_i)
            v.wait_ge(S("src_in"), 16)
            link(v.tensor_copy(src_f, src_i))
            link(v.tensor_scalar(i_f, src_f, 1.0 / KVOL, -(KVOL // 2) / KVOL, ALU.mult, ALU.add))
            link(v.tensor_single_scalar(i_f, i_f, WHOLE_NUMBERS, op=ALU.add))
            link(v.tensor_single_scalar(i_f, i_f, WHOLE_NUMBERS, op=ALU.subtract))
            v.scalar_tensor_tensor(out=k_f, in0=i_f, scalar=-float(KVOL), in1=src_f, op0=ALU.mult, op1=ALU.add)
            wait_next("begun_ps")
            link(v.tensor_scalar(cqb[:, :], ps[:, 0, 0:NT], -1.0, None, ALU.add))
            v.tensor_copy(ctab[:, :], cqb[:, :])
            link(v.tensor_tensor(bqb[:, :], col_f[:, :], cqb[:, :], ALU.subtract))
            v.tensor_scalar(btab[:, :], bqb[:, :], float(NB - 1), None, ALU.min)
            v.memset(bmin[:, :, 0:1], 0)
            v.tensor_scalar(bmin[:, 0, 1:NT + 1], bqb[0:1, :], float(NB - 1), None, ALU.min)
            link(v.tensor_scalar(bmin[:, 1, 1:NT + 1], bqb[0:1, :], -1.0, float(1 - NB), ALU.mult, ALU.max))
            link(v.tensor_scalar(bmin[:, 1, 1:NT + 1], bmin[:, 1, 1:NT + 1], float(NB - 1), None, ALU.add))
            link(v.tensor_copy(bpack[:, :, :], bmin[:, :, PACK - 1:PACK + NQ - GS]))
            for r in reversed(range(PACK - 1)):
                link(v.tensor_single_scalar(bpack[:, :, :], bpack[:, :, :], NB.bit_length() - 1,
                                            op=ALU.arith_shift_left))
                link(v.tensor_tensor(bpack[:, :, :], bpack[:, :, :], bmin[:, :, r:r + NQ - GS + 1], ALU.bitwise_or))
            link(v.tensor_scalar(bqb[:, :], bqb[:, :], float(P), None, ALU.mult))
            for k, (a, n) in enumerate(halves):
                last = v.tensor_scalar(qcol[0:n, k:k + 1], part_f[0:n, :], float(a + 1), None, ALU.add)
            link(last)
            for k, (a, n) in enumerate(halves):
                last = v.tensor_tensor(qcol[0:n, 2 + k:3 + k], qcol[0:n, k:k + 1], ps[0:n, 1, k:k + 1], ALU.subtract)
            link(last)
            v.tensor_scalar(selF[:, :], cqb[:, :], part_f[:, 0:1], None, ALU.is_equal).then_inc(S("sel_made"), 1)
            link(v.tensor_scalar(qcol[:, 0:1], qcol[:, 2:3], float(P), None, ALU.mult))
            link(v.tensor_scalar(qcol[0:NT - P, 1:2], qcol[0:NT - P, 3:4], float(P), None, ALU.mult))
            wait_next("ids_ps")
            for j in range(G):
                v.tensor_copy(split(srcI[:, 0:NCH * G], G)[:, :, j], ps[:, 0, j * P:(j + 1) * P])
                last = v.tensor_copy(split(dstK[:, :], G)[:, :, j], ps[:, G + j, 0:NT])
            link(last)
            link(v.tensor_tensor(split(dstL[:, :], G), split(dstK[:, :], G),
                                 bqb[:, :, None].to_broadcast([P, NT, G]), ALU.subtract))
            v.memset(srcI[:, NCH * G:(NCH + IXQ) * G], 0)
            v.tensor_copy(qtab[:, :], ps[0:1, 2, 0:NCH])
            link(v.tensor_scalar(mod_ni[:, 0:1], part_f[0:3 * NI, :], float(NI), -float(NI), ALU.is_ge, ALU.mult))
            link(v.tensor_scalar(mod_ni[:, 1:2], part_f[0:3 * NI, :], 2.0 * NI, -float(NI), ALU.is_ge, ALU.mult))
            link(v.tensor_tensor(mod_ni[:, 0:1], mod_ni[:, 0:1], mod_ni[:, 1:2], ALU.add))
            link(v.tensor_tensor(mod_ni[:, 0:1], mod_ni[:, 0:1], part_f[0:3 * NI, :], ALU.add))
            v.tensor_single_scalar(pen[:, :], dstL[:, :], 0.0, op=ALU.is_ge)
            link(v.tensor_single_scalar(prod[:, 0:0 + 512], dstL[:, 0:512], float(P), op=ALU.is_lt))
            link(v.tensor_tensor(pen[:, 0:512], pen[:, 0:512], prod[:, 0:512], ALU.mult))
            more = NT * G - 512
            link(v.tensor_single_scalar(prod[:, 0:more], dstL[:, 512:NT * G], float(P), op=ALU.is_lt))
            link(v.tensor_tensor(pen[:, 512:NT * G], pen[:, 512:NT * G], prod[:, 0:more], ALU.mult))
            v.tensor_scalar(pen[:, :], pen[:, :], -1.0, BIG, ALU.add, ALU.mult).then_inc(S("steps_made"), 1)

            wait_next("idrow_ps")
            for k, (a, n) in enumerate(halves):
                link(v.tensor_scalar(dst_f[0:n, :], ps[0:n, 3 * k, :], qcol[0:n, k:k + 1], -1.0,
                                     ALU.subtract, ALU.max))
                v.tensor_copy(idrow[k][0:n, 0:P].bitcast(F16), ps[0:n, 6 + k, 0:P])
                v.tensor_single_scalar(idrow[k][0:n, P:P + EC], dst_f[0:n, :], float(P), op=ALU.min)
                v.tensor_copy(idrow[k][0:n, P + EC:P + 2 * EC], ps[0:n, 3 * k + 1, :])
                link(v.tensor_copy(idrow[k][0:n, P + 2 * EC:P + 3 * EC], ps[0:n, 3 * k + 2, :]))
            v.sem_inc(S("idrow_made"), 1)

            link(v.scalar_tensor_tensor(out=node16[:, :, :], in0=col_f[:, 0:NB, None].to_broadcast([P, NB, P]),
                                        scalar=float(P), in1=part_f[:, :, None].to_broadcast([P, NB, P]),
                                        op0=ALU.mult, op1=ALU.add))

            wait_next("wt_ps")
            v.tensor_copy(wlr[0:C, :], ps[0:C, 0, 0:2 * C])
            v.tensor_copy(wns[0:C, :], ps[0:C, 0, 2 * C:4 * C])
            v.wait_ge(S("gmask"), 1)
            for j in range(G):
                last = v.tensor_scalar(web[:, j, :], ps[0:G * ED, 1, 0:C], gmask[:, j:j + 1], None, ALU.mult)
            last.then_inc(S("wt_made"), 1)

            def normalise(dst, src, parts, heads):
                w = heads * D0
                link(v.tensor_tensor(sq[0:parts, 0:w], src, src, ALU.mult))
                link(v.reduce_sum(nrm[0:parts, 0:heads], split(sq[0:parts, 0:w], D0), AX.X))
                v.tensor_single_scalar(nrm[0:parts, 0:heads], nrm[0:parts, 0:heads], 1e-24, op=ALU.max) \
                    .then_inc(S("square_sum"), 1)
                wait_next("root")
                link(v.reciprocal(nrm[0:parts, 0:heads], nrm[0:parts, 0:heads]))
                link(v.tensor_tensor(split(dst, D0), split(src, D0),
                                     nrm[0:parts, 0:heads, None].to_broadcast([parts, heads, D0]), ALU.mult))

            wait_next("proj_ps")
            hf = h[:, :, :].rearrange("p b c -> p (b c)")
            v.tensor_copy(kvn[:, :], ps[0:NI, 2, 0:2 * C])
            link(v.tensor_copy(hf, acc[:, 0:NB * C]))
            def thirds(dst3, src, tmp):
                link(v.tensor_copy(dst3(0), src))
                link(v.tensor_tensor(tmp, src, dst3(0), ALU.subtract))
                link(v.tensor_copy(dst3(1), tmp))
                link(v.tensor_tensor(tmp, tmp, dst3(1), ALU.subtract))
                link(v.tensor_copy(dst3(2), tmp))

            normalise(tab[:, 0:NB * C], hf, P, NB * H0)
            thirds(lambda k: tab3[:, k, 0:NB * C], tab[:, 0:NB * C], sq[:, 0:NB * C])
            normalise(kvn[:, 0:C], kvn[:, 0:C], NI, H0)
            thirds(lambda k: kvn3[:, k, :], kvn[:, :], sq[0:NI, 0:2 * C])
            v.sem_inc(S("kvn_made"), 1)
            normalise(pos[:, :], pos[:, :], KVOL, H0)
            thirds(lambda k: pos3[:, k, :], pos[:, :], sq[0:KVOL, 0:C])
            v.sem_inc(S("tables_made"), 1)
            v.sem_inc(S("sums_free"), 1)

            def onehot_T(layer, q, s, i, used, ids):
                for name in used:
                    done(v, name, q - SLOTS)
                v.wait_ge(S(f"{layer}_ids{s}"), i * 16 + 16)
                o = ohT[s % SLOTS]
                if layer != "l0":
                    v.tensor_scalar(o[:, 0:EC], ids, part_f[:, 0:1], None, ALU.is_equal) \
                        .then_inc(S(f"{layer}_ohT"), 1)
                    return
                v.tensor_scalar(o[:, 0:2 * EC], ids[:, 0:2 * EC], part_f[:, 0:1], None, ALU.is_equal)
                v.tensor_scalar(o[0:3 * NI, 2 * EC:3 * EC], ids[0:3 * NI, 2 * EC:3 * EC], mod_ni[:, 0:1], None,
                                ALU.is_equal).then_inc(S(f"{layer}_ohT"), 1)

            def onehot_S(layer, q, s, i):
                done(v, f"{layer}_near_ps", q - SLOTS)
                v.wait_ge(S(f"{layer}_ids{s}"), i * 16 + 16)
                ids = idb[s][:, 0:P].bitcast(F16)
                v.tensor_tensor(ohS[s % SLOTS][:, :, :], ids[:, None, :].to_broadcast([P, NB, P]),
                                node16[:, :, :], ALU.is_equal).then_inc(S(f"{layer}_ohS"), 1)

            def lowest(layer, q, s, width):
                def one():
                    done(v, f"{layer}_hi", q)
                    done(v, f"{layer}_lo", q - SLOTS)
                    v.tensor_tensor(rest[s % SLOTS][:, :, 0:width], pay[s % SLOTS][:, :, 0:width],
                                    pay3[s % GS][:, 0, :, 0:width], ALU.subtract).then_inc(S(f"{layer}_rest"), 1)

                def two():
                    done(v, f"{layer}_mid", q)
                    v.tensor_tensor(pay3[s % GS][:, 2, :, 0:width], rest[s % SLOTS][:, :, 0:width],
                                    pay3[s % GS][:, 1, :, 0:width], ALU.subtract).then_inc(S(f"{layer}_lo"), 1)
                return one, two

            def onehot_rest(layer, q, s):
                if POOL_TILES[layer] == G:
                    return
                done(v, f"{layer}_sum", q - GS)
                for j in range(POOL_TILES[layer], G):
                    last = v.tensor_scalar(ohb[s % GS][:, j, :], col_b[:, :], dstL[:, bass.ds(q * G + j, 1)], None,
                                           ALU.is_equal)
                last.then_inc(S(f"{layer}_ohv"), 1)

            def onehot(layer, q, s):
                done(v, f"{layer}_sum", q - SLOTS)
                v.tensor_tensor(oh[s % SLOTS][:, :, :], col_f[:, None, 0:P].to_broadcast([P, G, P]),
                                dstL[:, bass.ds(q * G, G)][:, :, None].to_broadcast([P, G, P]), ALU.is_equal) \
                    .then_inc(S(f"{layer}_oh"), 1)

            def step0(q, s, i):
                onehot_rest("l0", q, s)
                one, two = lowest("l0", q - 1, s - 1, C)
                done(v, "l0_ga", q)
                done(v, "l0_kv", q)
                v.tensor_tensor(split(prod[:, 0:G * C], C), split(ga[s % SLOTS][:, 0:G * C], C), gat[s][:, :, 0:C],
                                ALU.mult).then_inc(S("l0_prod"), 1)
                if not first(q):
                    one()
                done(v, "l0_prod", q)
                v.reduce_sum(attn[:, :], split(prod[:, 0:G * C], D0), AX.X).then_inc(S("l0_attn"), 1)
                onehot_T("l0", q + 2, (s + 2) % GS, i + (s + 2) // GS, ("l0_ga", "l0_src"), idb0[(s + 2) % GS])
                done(v, "l0_attn", q)
                v.tensor_tensor(pay[s % SLOTS][:, :, 0:C].rearrange("p j (h d) -> p j h d", d=D0),
                                gat[s][:, :, C:2 * C].rearrange("p j (h d) -> p j h d", d=D0),
                                split(attn[:, :], H0)[:, :, :, None].to_broadcast([P, G, H0, D0]), ALU.mult) \
                    .then_inc(S("l0_pay"), 1)
                if not first(q):
                    two()
            for q in range(2):
                onehot_T("l0", q, q, 0, ("l0_ga", "l0_src"), idb0[q])
            steps(v, step0)
            for part in lowest("l0", NQ - 1, GS - 1, C):
                part()

            def norm(dst, gamma=None):
                link(v.reduce_sum(st1[:, :], h[:, :, :], AX.X))
                link(v.tensor_single_scalar(st1[:, :], st1[:, :], 1.0 / C, op=ALU.mult))
                link(v.tensor_tensor(h[:, :, :], h[:, :, :], per_row(st1), ALU.subtract))
                link(v.tensor_tensor(split(sq[:, 0:NB * C], C), h[:, :, :], h[:, :, :], ALU.mult))
                link(v.reduce_sum(st2[:, :], split(sq[:, 0:NB * C], C), AX.X))
                v.tensor_scalar(st2[:, :], st2[:, :], 1.0 / C, 1e-5, ALU.mult, ALU.add).then_inc(S("square_sum"), 1)
                wait_next("root")
                link(v.reciprocal(st3[:, :], st2[:, :]))
                if gamma is None:
                    v.tensor_tensor(dst, h[:, :, :], per_row(st3), ALU.mult).then_inc(S("x_made"), 1)
                    return
                link(v.tensor_tensor(h[:, :, :], h[:, :, :], per_row(st3), ALU.mult))
                link(v.tensor_tensor(h[:, :, :], h[:, :, :], over(vecs, VGAMMA), ALU.mult))
                link(v.tensor_tensor(h[:, :, :], h[:, :, :], over(vecs, VBETA), ALU.add))
                link(v.tensor_single_scalar(h[:, :, :], h[:, :, :], 0.0, op=ALU.max))

            done(v, "l0_sum", NQ - 1)
            accb = split(acc, P)
            v.tensor_copy(cnt[:, :], accb[:, :, C])
            v.tensor_copy(h[:, :, :], accb[:, :, 0:C]).then_inc(S("agg_made"), 1)
            wait_next("agg_made")
            link(v.tensor_single_scalar(rdeg[:, :], cnt[:, :], 1.0, op=ALU.max))
            v.reciprocal(rdeg[:, :], rdeg[:, :])
            wait_next("proj_ps")
            link(v.tensor_tensor(h[:, :, :], split(acc[:, 0:NB * C], C), over(vecs, VBO), ALU.add))
            link(v.scalar_tensor_tensor(out=h[:, :, :], in0=x[:, :, :], scalar=2.0, in1=h[:, :, :],
                                        op0=ALU.mult, op1=ALU.add))
            norm(x[:, :, :])

            wait_next("proj_ps")
            v.tensor_copy(split(rows[:, 0:NB * C], C), accb[:, :, 0:C]).then_inc(S("xl_made"), 1)
            link(v.tensor_copy(split(tab[:, 0:NB * C], C), accb[:, :, C:P]))
            thirds(lambda k: tab3[:, k, 0:NB * C], tab[:, 0:NB * C], sq[:, 0:NB * C])
            thirds(lambda k: tab3[:, k, NB * C:2 * NB * C], rows[:, 0:NB * C], sq[:, 0:NB * C])
            v.sem_inc(S("tables_made"), 1)

            back = {}

            def logits(q):
                done(v, "l1_wgt", q)
                v.reduce_sum(lg[:, bass.ds(q * G * H1, G * H1)], split(wgt[:, :], D1), AX.X).then_inc(S("l1_lg"), 1)

            def step1(q, s, i):
                onehot_S("l1", q + 1, (s + 1) % GS, i + (s + 1) // GS)
                unpack(v, back, q, s, 0, 0, row=1)
                if not first(q):
                    logits(q - 1)
                c = q + back[s] + 1
                done(v, "l1_ga", q)
                v.wait_ge(S("l1_here"), c + 1)
                v.tensor_tensor(prod[:, 0:FAR * C], ga[s % SLOTS][:, 0:FAR * C],
                                ring[:, bass.ds(c % GS * (G * HID), FAR * C)], ALU.add)
                done(v, "l1_near", q)
                v.tensor_tensor(prod[:, FAR * C:G * C], ga[s % SLOTS][:, FAR * C:G * C], near[s][:, :], ALU.add) \
                    .then_inc(S("l1_z"), 1)
                onehot_T("l1", q + 1, (s + 1) % GS, i + (s + 1) // GS, ("l1_ga",), idb[(s + 1) % GS][:, P:P + EC])
                done(v, "l1_z", q)
                v.scalar_tensor_tensor(out=lky[:, :], in0=prod[:, 0:G * C], scalar=0.2, in1=prod[:, 0:G * C],
                                       op0=ALU.mult, op1=ALU.max).then_inc(S("l1_lky"), 1)
                done(v, "l1_lky", q)
                v.tensor_tensor(split(wgt[:, :], C), split(lky[:, :], C),
                                vecs[:, VATT:VATT + 1, :].to_broadcast([P, G, C]), ALU.mult) \
                    .then_inc(S("l1_wgt"), 1)
            onehot_T("l1", 0, 0, 0, ("l1_ga",), idb[0][:, P:P + EC])
            onehot_S("l1", 0, 0, 0)
            steps(v, step1)
            logits(NQ - 1)
            done(v, "l1_lg", NQ - 1)
            def by_group(t):
                return t.rearrange("p (g k) -> p g k", g=NG)[:, :, :, None].to_broadcast([P, NG, KG, H1])

            def by_tile(t):
                return t.rearrange("p (k g h) -> p g k h", g=NG, h=H1)
            v.tensor_copy(by_tile(brk[:, 0:TL]), by_group(dstK[:, 0:NQ * G])).then_inc(S("l1_keys"), 1)
            v.tensor_tensor(by_tile(run[:, :]), lg[:, :].rearrange("p (g k h) -> p g k h", g=NG, h=H1),
                            by_group(pen[:, 0:NQ * G]), ALU.add).then_inc(S("l1_logits"), 1)

            done(v, "bank_out", KG // 4 - 1)
            v.memset(brk[:, 0:1], 0.0)
            v.memset(brk[:, TL:TL + 1], 0.0)
            link(v.tensor_tensor(brk[:, 1:TL], keyT[:, 1:TL], keyT[:, 0:TL - 1], ALU.is_equal))
            link(v.tensor_scalar(brk[:, 1:TL], brk[:, 1:TL], -1.0, BIG, ALU.add, ALU.mult))
            done(v, "bank_out", 2 * KG // 4 - 1)

            def scan_right(src, initial, out=run):
                link(v.tensor_tensor_scan(out=out[:, :], data0=brk[:, 0:TL], data1=src, initial=initial,
                                          op0=ALU.add, op1=ALU.max))

            def scan_left(src, initial):
                link(v.tensor_tensor_scan(out=run[:, ::-1], data0=brk[:, 1:TL + 1][:, ::-1], data1=src[:, ::-1],
                                          initial=initial, op0=ALU.add, op1=ALU.max))
            scan_right(lgT[:, :], -BIG)
            v.tensor_copy(ends[:, 0:1], run[:, TL - 1:TL])
            v.tensor_copy(ends[:, 2:3], keyT[:, 0:1])
            link(v.tensor_copy(ends[:, 3:4], keyT[:, TL - 1:TL]))
            scan_left(lgT[:, :], -BIG)
            v.tensor_copy(ends[:, 1:2], run[:, 0:1]).then_inc(S("ends_made"), 1)
            wait_next("ends_ps")
            LAST, FIRST, KF, KL, WHOLE, SAME, S0, S1, T0, T1, CR, CL = range(12)
            for k in range(4):
                last = v.tensor_copy(crow[0:1, k, :].rearrange("p (h g) -> p h g", g=NG),
                                     ps[0:1, k, 0:P].rearrange("p (g h) -> p h g", h=H1))
            link(last)

            def row(k, a=0, b=NG):
                return crow[0:1, k, :].rearrange("p (h g) -> p h g", g=NG)[:, :, a:b]
            v.memset(crow[0:1, SAME:T1 + 1, :].rearrange("p a b -> p (a b)"), -BIG)
            link(v.tensor_tensor(row(WHOLE), row(KF), row(KL), ALU.is_equal))
            link(v.tensor_scalar(row(WHOLE), row(WHOLE), -1.0, BIG, ALU.add, ALU.mult))
            link(v.tensor_tensor(row(SAME, 0, NG - 1), row(KL, 0, NG - 1), row(KF, 1, NG), ALU.is_equal))
            link(v.tensor_scalar(row(SAME, 0, NG - 1), row(SAME, 0, NG - 1), -1.0, BIG, ALU.add, ALU.mult))
            v.tensor_tensor(row(S0, 1, NG), row(SAME, 0, NG - 1), row(WHOLE, 0, NG - 1), ALU.add)
            v.tensor_tensor(row(S1, 1, NG), row(SAME, 0, NG - 1), row(LAST, 0, NG - 1), ALU.add)
            v.tensor_tensor(row(T0, 0, NG - 1), row(SAME, 0, NG - 1), row(WHOLE, 1, NG), ALU.add)
            link(v.tensor_tensor(row(T1, 0, NG - 1), row(SAME, 0, NG - 1), row(FIRST, 1, NG), ALU.add))
            link(v.tensor_tensor_scan(out=crow[0:1, WHOLE, :], data0=crow[0:1, S0, :], data1=crow[0:1, S1, :],
                                      initial=-BIG, op0=ALU.add, op1=ALU.max))
            link(v.tensor_tensor_scan(out=crow[0:1, SAME, ::-1], data0=crow[0:1, T0, ::-1],
                                      data1=crow[0:1, T1, ::-1], initial=-BIG, op0=ALU.add, op1=ALU.max))
            for o, k in ((CR, WHOLE), (CL, SAME)):
                last = v.tensor_copy(crow[0:1, o, :].rearrange("p (g h) -> p h g", h=H1), row(k))
            last.then_inc(S("carry_made"), 1)
            wait_next("carry_ps")
            for k in range(2):
                last = v.tensor_copy(carry[:, k:k + 1], ps[:, 4 + k, 0:1])
            link(last)
            scan_right(lgT[:, :], carry[:, 0:1], out=keyT)
            scan_left(keyT[:, :], carry[:, 1:2])
            for k in range(0, KG, EXT):
                part = slice(k * P, (k + EXT) * P)
                v.tensor_tensor(lgT[:, part], lgT[:, part], run[:, part], ALU.subtract).then_inc(S("shift_made"), 1)

            v.sem_inc(S("sums_free"), 1)
            done(v, "ex_out", KG // 4 - 1)

            def step1b(q, s, i):
                one, two = lowest("l1b", q - 1, s - 1, C + H1)
                if not first(q):
                    one()
                ex = lg[:, bass.ds(q * G * H1, G * H1)]
                v.tensor_copy(pay[s % SLOTS][:, :, C:C + H1], split(ex, H1))
                v.wait_ge(S(f"l1b_rows{s}"), i * 16 + 16)
                v.wait_ge(S(f"l1b_near{s}"), i * 16 + 16)
                v.tensor_tensor(pay[s % SLOTS][:, :, 0:C].rearrange("p j (h d) -> p j h d", d=D1),
                                g64[s].rearrange("p (j h d) -> p j h d", j=G, d=D1),
                                split(ex, H1)[:, :, :, None].to_broadcast([P, G, H1, D1]), ALU.mult) \
                    .then_inc(S("l1b_pay"), 1)
                onehot_rest("l1b", q, s)
                if not first(q):
                    two()
            steps(v, step1b)
            for part in lowest("l1b", NQ - 1, GS - 1, C + H1):
                part()
            done(v, "l1b_sum", NQ - 1)
            den = sq[:, NB * C:NB * C + NB * H1]
            link(v.tensor_single_scalar(split(den, H1), accb[:, :, C:C + H1], 1e-16, op=ALU.add))
            link(v.reciprocal(den, den))
            link(v.tensor_copy(h[:, :, :], accb[:, :, 0:C]))
            hh = h[:, :, :].rearrange("p b c -> p (b c)")
            link(v.tensor_tensor(split(hh, D1), split(hh, D1), den[:, :, None].to_broadcast([P, NB * H1, D1]),
                                 ALU.mult))
            link(v.tensor_tensor(h[:, :, :], h[:, :, :], over(vecs, VBIAS), ALU.add))
            link(v.tensor_tensor(h[:, :, :], h[:, :, :], x[:, :, :], ALU.add))
            norm(None, gamma=True)
            link(v.tensor_tensor(h[:, :, :], h[:, :, :], x[:, :, :], ALU.add))
            norm(x[:, :, :])

            wait_next("proj_ps")
            v.tensor_copy(rows[:, 0:NB * HID], acc).then_inc(S("a_made"), 1)
            wait_next("proj_ps")
            link(v.tensor_copy(tab, top))
            thirds(lambda k: tab3[:, k, :], tab, sq)
            v.sem_inc(S("sums_free"), 1)
            for _ in range(2):
                wait_next("x_made")
            thirds(lambda k: xs3[:, k, :], x[:, :, :].rearrange("p b c -> p (b c)"), sq[:, 0:NB * C])
            v.sem_inc(S("tables_made"), 1)

            def step2(q, s, i):
                unpack(v, back, q, s, 0, 0, row=1)
                c = q + back[s] + 1
                done(v, "l2_ga", q)
                done(v, "l2_sum", q - SLOTS)
                v.wait_ge(S("l2_here"), c + 1)
                v.tensor_tensor(pay[s % SLOTS][:, 0:FAR, :], split(ga[s % SLOTS][:, 0:FAR * HID], HID),
                                split(ring[:, bass.ds(c % GS * (G * HID), FAR * HID)], HID), ALU.add) \
                    .then_inc(S("l2_z"), 1)
                onehot("l2", q, s)
                onehot_T("l2", q + 2, (s + 2) % GS, i + (s + 2) // GS, ("l2_ga",), idb[(s + 2) % GS][:, P:P + EC])
                onehot_S("l2", q + 2, (s + 2) % GS, i + (s + 2) // GS)
            for q in range(2):
                onehot_S("l2", q, q, 0)
                onehot_T("l2", q, q, 0, ("l2_ga",), idb[q][:, P:P + EC])
            steps(v, step2)
            done(v, "l2_sum", NQ - 1)
            v.wait_ge(S("a_out"), 16)
            v.tensor_copy(rows[:, 0:NB * HID], acc).then_inc(S("agg_made"), 1)
            link(v.tensor_tensor(h[:, :, :], over(vecs, VB2), per_row(cnt), ALU.mult))
            wait_next("proj_ps")
            link(v.tensor_tensor(h[:, :, :], h[:, :, :], split(acc[:, 0:NB * C], C), ALU.add))
            link(v.tensor_tensor(h[:, :, :], h[:, :, :], per_row(rdeg), ALU.mult))
            link(v.tensor_tensor(h[:, :, :], h[:, :, :], x[:, :, :], ALU.add))
            norm(x[:, :, :])
            v.sem_inc(S("sums_free"), 1)

            wait_next("x_made")
            thirds(lambda k: xs3[:, k, :], x[:, :, :].rearrange("p b c -> p (b c)"), sq[:, 0:NB * C])
            v.sem_inc(S("tables_made"), 1)
            onehot_S("l3", 0, 0, 0)

            def step3(q, s, i):
                onehot_S("l3", q + 1, (s + 1) % GS, i + (s + 1) // GS)
                onehot("l3", q, s)
            steps(v, step3)
            done(v, "l3_sum", NQ - 1)
            v.tensor_tensor(h[:, :, :], accb[:, :, 0:C], per_row(rdeg), ALU.mult).then_inc(S("agg_made"), 1)
            wait_next("proj_ps")
            v.wait_ge(S("x3_out"), 16)
            link(v.tensor_tensor(h[:, :, :], split(acc[:, 0:NB * C], C), x[:, :, :], ALU.add))
            norm(x[:, :, :])


_INS = ["x", "src", "dst", "edge_attr_16", "L0_gnn_Wq", "L0_gnn_bq", "L0_gnn_Wk", "L0_gnn_bk", "L0_gnn_Wv",
        "L0_gnn_bv", "L0_gnn_Wo", "L0_gnn_bo", "L0_gnn_pos_enc", "L1_gnn_W_l", "L1_gnn_b_l", "L1_gnn_W_r",
        "L1_gnn_b_r", "L1_gnn_W_e", "L1_gnn_att", "L1_gnn_bias", "L1_gnn_gamma", "L1_gnn_beta", "L2_gnn_W1",
        "L2_gnn_b1", "L2_gnn_W2", "L2_gnn_b2", "L3_gnn_w_neigh", "L3_gnn_w_self", "L3_gnn_b_self"]


def kernel(**inputs):
    import numpy as _np
    import concourse.bacc as _bacc
    from concourse import mybir as _mybir
    from concourse.bass_utils import run_bass_kernel_spmd as _run

    nc = _bacc.Bacc("TRN2", target_bir_lowering=False, num_devices=1)
    arrays, io = {}, {}
    for name in _INS:
        a = _np.ascontiguousarray(inputs[name])
        arrays[f"in_{name}_dram"] = a
        io[name] = nc.dram_tensor(f"in_{name}_dram", a.shape, _mybir.dt.from_np(a.dtype), kind="ExternalInput").ap()
    out = nc.dram_tensor("out_0_dram", (N, C), F32, kind="ExternalOutput").ap()
    build(nc, io, out)
    r = _run(nc, [arrays], core_ids=[0])
    return r.results[0]["out_0_dram"]
```
